# Optimizing a Trainium2 kernel written in Bass

```python
import numpy as np
import jax
import jax.numpy as jnp

def _softmax(x, axis=-1):
    return jax.nn.softmax(x, axis=axis)

def _gelu(x):
    return jax.nn.gelu(x, approximate=True)

def _silu(x):
    return jax.nn.silu(x)

def _sigmoid(x):
    return jax.nn.sigmoid(x)

def _layernorm(x, axis=-1, eps=1e-05):
    m = jnp.mean(x, axis=axis, keepdims=True)
    v = jnp.var(x, axis=axis, keepdims=True)
    return (x - m) / jnp.sqrt(v + eps)

def _scatter_add(tgt, idx, src, axis=0):
    return tgt.at[idx].add(src)

def _segment_sum(src, seg, n):
    return jax.ops.segment_sum(src, seg, n)
kernel_name = 'mk_decoder_postln_d1_seqx_r2_14f615'

def setup_inputs(seed: int=0):
    np.random.seed(seed)
    _w = jnp.asarray

    def _rec_inputs():
        import jax
        import jax.numpy as jnp
        _rk = jax.random.key(seed)
        x = -0.000125 + 0.9999 * jax.random.normal(jax.random.fold_in(_rk, 1), (16, 512, 512), jnp.float32)
        _lenS = 512 - jax.random.randint(jax.random.fold_in(_rk, 7), (16,), 0, max(1, 512 // 4) + 1, jnp.int32)
        _lenS2 = 512 - jax.random.randint(jax.random.fold_in(_rk, 8), (16,), 0, max(1, 512 // 4) + 1, jnp.int32)
        _ctx_1024P = jax.random.normal(jax.random.fold_in(_rk, 11), (16, 16, 512), jnp.float32)
        _ctx_1024c = jax.random.dirichlet(jax.random.fold_in(_rk, 511), 0.3 * jnp.ones((16,), jnp.float32), (16, 512))
        _ctx_1024t = jnp.einsum('bsk,bkd->bsd', _ctx_1024c, _ctx_1024P)
        _ctx_1024t = _ctx_1024t * jax.lax.rsqrt(jnp.mean(jnp.square(_ctx_1024t)) + 1e-12) * 0.953939
        ctx_1024 = -1.52775e-05 + 0.999936 * (_ctx_1024t + 0.3 * jax.random.normal(jax.random.fold_in(_rk, 611), (16, 512, 512), jnp.float32))
        return (x, ctx_1024)
    x, ctx_1024 = _rec_inputs()

    def _L0_attn_setup():
        import jax, jax.numpy as jnp
        import numpy as np
        N_EMBD = 512
        N_HEAD = 16
        HEAD_SIZE = N_EMBD // N_HEAD
        B, T = (8, 2048)
        EPS = 0.001
        key = jax.random.key(seed)
        k1, k2, k3 = jax.random.split(key, 3)
        x = jax.random.normal(k1, (B, T, N_EMBD), dtype=jnp.float32)
        Wqkv = jax.random.normal(k2, (3 * N_EMBD, N_EMBD), dtype=jnp.float32) * 0.02
        bqkv = jnp.zeros((3 * N_EMBD,), dtype=jnp.float32)
        Wproj = jax.random.normal(k3, (N_EMBD, N_EMBD), dtype=jnp.float32) * 0.02
        bproj = jnp.zeros((N_EMBD,), dtype=jnp.float32)
        scale = jnp.asarray(1.0 / np.sqrt(HEAD_SIZE), dtype=jnp.float32)
        return {'x': x, 'Wqkv': Wqkv, 'bqkv': bqkv, 'Wproj': Wproj, 'bproj': bproj, 'scale': scale}
    _L0_attn_all = _L0_attn_setup()
    _L0_attn_in = {k: v for k, v in _L0_attn_all.items() if k in ('Wqkv', 'bqkv', 'Wproj', 'bproj', 'scale')}
    del _L0_attn_all

    def _L0_xattn_setup():
        import jax, jax.numpy as jnp
        import numpy as np
        N_HEADS = 4
        IN_FEATURES = 512

        def _channel_attention(qm, km, vm, scale):
            b, n, c = qm.shape
            d = c // N_HEADS
            qh = qm.reshape(b, n, N_HEADS, d).transpose(0, 2, 3, 1)
            kh = km.reshape(b, n, N_HEADS, d).transpose(0, 2, 3, 1)
            vh = vm.reshape(b, n, N_HEADS, d).transpose(0, 2, 3, 1)
            scores = jnp.einsum('bhdn,bhen->bhde', qh, kh) * scale
            attn = jax.nn.softmax(scores, axis=-1)
            out = jnp.einsum('bhde,bhen->bhdn', attn, vh)
            return out.transpose(0, 3, 1, 2).reshape(b, n, c)
        key = jax.random.key(seed)
        ks = jax.random.split(key, 20)
        B, HW, C = (2, 8192, 512)
        inp = {'q': jax.random.normal(ks[0], (B, HW, C), dtype=jnp.float32), 'k': jax.random.normal(ks[1], (B, HW, C), dtype=jnp.float32), 'v': jax.random.normal(ks[2], (B, HW, C), dtype=jnp.float32)}
        names = ['wqg', 'bqg', 'wkg', 'bkg', 'wvg', 'bvg', 'wql', 'bql', 'wkl', 'bkl', 'wvl', 'bvl', 'wp', 'bp']
        for i, n in enumerate(names):
            inp[n] = jax.random.normal(ks[3 + i], (C,), dtype=jnp.float32)
        return inp
    _L0_xattn_all = _L0_xattn_setup()
    _L0_xattn_in = {k: v for k, v in _L0_xattn_all.items() if k in ('wqg', 'bqg', 'wkg', 'bkg', 'wvg', 'bvg', 'wql', 'bql', 'wkl', 'bkl', 'wvl', 'bvl', 'wp', 'bp')}
    del _L0_xattn_all

    def _L0_ffn_setup():
        import jax, jax.numpy as jnp
        import numpy as np
        D_MODEL = 512
        D_FF = 2048
        NUM_EXPERTS = 8
        B, N = (16, 512)
        key = jax.random.key(seed)
        ks = jax.random.split(key, 7)
        s_in = 1.0 / np.sqrt(D_MODEL)
        s_ff = 1.0 / np.sqrt(D_FF)
        return {'x': jax.random.normal(ks[0], (B, N, D_MODEL), dtype=jnp.float32), 'Wr': jax.random.uniform(ks[1], (D_MODEL, NUM_EXPERTS), jnp.float32, -s_in, s_in), 'br': jax.random.uniform(ks[2], (NUM_EXPERTS,), jnp.float32, -s_in, s_in), 'W1': jax.random.uniform(ks[3], (NUM_EXPERTS, D_MODEL, D_FF), jnp.float32, -s_in, s_in), 'b1': jax.random.uniform(ks[4], (NUM_EXPERTS, D_FF), jnp.float32, -s_in, s_in), 'W2': jax.random.uniform(ks[5], (NUM_EXPERTS, D_FF, D_MODEL), jnp.float32, -s_ff, s_ff), 'b2': jax.random.uniform(ks[6], (NUM_EXPERTS, D_MODEL), jnp.float32, -s_ff, s_ff)}
    _L0_ffn_all = _L0_ffn_setup()
    _L0_ffn_in = {k: v for k, v in _L0_ffn_all.items() if k in ('Wr', 'br', 'W1', 'b1', 'W2', 'b2')}
    del _L0_ffn_all
    return {'x': x, 'ctx_1024': ctx_1024, 'L0_attn_Wqkv': _L0_attn_in['Wqkv'], 'L0_attn_bqkv': _L0_attn_in['bqkv'], 'L0_attn_Wproj': _L0_attn_in['Wproj'], 'L0_attn_bproj': _L0_attn_in['bproj'], 'L0_attn_scale': _L0_attn_in['scale'], 'L0_xattn_wqg': _L0_xattn_in['wqg'], 'L0_xattn_bqg': _L0_xattn_in['bqg'], 'L0_xattn_wkg': _L0_xattn_in['wkg'], 'L0_xattn_bkg': _L0_xattn_in['bkg'], 'L0_xattn_wvg': _L0_xattn_in['wvg'], 'L0_xattn_bvg': _L0_xattn_in['bvg'], 'L0_xattn_wql': _L0_xattn_in['wql'], 'L0_xattn_bql': _L0_xattn_in['bql'], 'L0_xattn_wkl': _L0_xattn_in['wkl'], 'L0_xattn_bkl': _L0_xattn_in['bkl'], 'L0_xattn_wvl': _L0_xattn_in['wvl'], 'L0_xattn_bvl': _L0_xattn_in['bvl'], 'L0_xattn_wp': _L0_xattn_in['wp'], 'L0_xattn_bp': _L0_xattn_in['bp'], 'L0_ffn_Wr': _L0_ffn_in['Wr'], 'L0_ffn_br': _L0_ffn_in['br'], 'L0_ffn_W1': _L0_ffn_in['W1'], 'L0_ffn_b1': _L0_ffn_in['b1'], 'L0_ffn_W2': _L0_ffn_in['W2'], 'L0_ffn_b2': _L0_ffn_in['b2']}

def reference(x, ctx_1024, L0_attn_Wqkv, L0_attn_bqkv, L0_attn_Wproj, L0_attn_bproj, L0_attn_scale, L0_xattn_wqg, L0_xattn_bqg, L0_xattn_wkg, L0_xattn_bkg, L0_xattn_wvg, L0_xattn_bvg, L0_xattn_wql, L0_xattn_bql, L0_xattn_wkl, L0_xattn_bkl, L0_xattn_wvl, L0_xattn_bvl, L0_xattn_wp, L0_xattn_bp, L0_ffn_Wr, L0_ffn_br, L0_ffn_W1, L0_ffn_b1, L0_ffn_W2, L0_ffn_b2):
    import jax
    import jax.numpy as jnp

    def _L0_attn_ref(x, Wqkv, bqkv, Wproj, bproj, scale):
        import jax, jax.numpy as jnp
        import numpy as np
        N_EMBD = 512
        N_HEAD = 16
        HEAD_SIZE = N_EMBD // N_HEAD
        B, T = (8, 2048)
        EPS = 0.001
        Bsz, Tlen, C = x.shape
        H, D = (N_HEAD, HEAD_SIZE)
        qkv = jnp.einsum('btc,ec->bte', x, Wqkv) + bqkv
        q, k, v = jnp.split(qkv, 3, axis=-1)
        q = q.reshape(Bsz, Tlen, H, D) * scale
        k = k.reshape(Bsz, Tlen, H, D) * scale
        v = v.reshape(Bsz, Tlen, H, D)
        q = jax.nn.elu(q) + 1.0
        k = jax.nn.elu(k) + 1.0
        kv = k * v
        k_cumsum = jnp.cumsum(k, axis=1)
        kv_cumsum = jnp.cumsum(kv, axis=1)
        denom = jnp.einsum('bthd,bthd->bth', q, k_cumsum)
        denom = jnp.clip(denom, EPS, None)[..., None]
        y = q * kv_cumsum / denom
        y = y.reshape(Bsz, Tlen, C)
        return jnp.einsum('btc,ec->bte', y, Wproj) + bproj

    def _L0_xattn_ref(q, k, v, wqg, bqg, wkg, bkg, wvg, bvg, wql, bql, wkl, bkl, wvl, bvl, wp, bp):
        import jax, jax.numpy as jnp
        import numpy as np
        N_HEADS = 4
        IN_FEATURES = 512

        def _channel_attention(qm, km, vm, scale):
            b, n, c = qm.shape
            d = c // N_HEADS
            qh = qm.reshape(b, n, N_HEADS, d).transpose(0, 2, 3, 1)
            kh = km.reshape(b, n, N_HEADS, d).transpose(0, 2, 3, 1)
            vh = vm.reshape(b, n, N_HEADS, d).transpose(0, 2, 3, 1)
            scores = jnp.einsum('bhdn,bhen->bhde', qh, kh) * scale
            attn = jax.nn.softmax(scores, axis=-1)
            out = jnp.einsum('bhde,bhen->bhdn', attn, vh)
            return out.transpose(0, 3, 1, 2).reshape(b, n, c)
        scale = IN_FEATURES ** (-0.5)
        att_global = _channel_attention(q * wqg + bqg, k * wkg + bkg, v * wvg + bvg, scale)
        att_local = _channel_attention(q * wql + bql, k * wkl + bkl, v * wvl + bvl, scale)
        att = att_global + att_local
        return 2.0 * att * wp + bp

    def _L0_ffn_ref(x, Wr, br, W1, b1, W2, b2):
        import jax, jax.numpy as jnp
        import numpy as np
        D_MODEL = 512
        D_FF = 2048
        NUM_EXPERTS = 8
        B, N = (16, 512)
        scores = jnp.einsum('bh,he->be', x.mean(axis=1), Wr) + br
        top1 = jnp.argmax(scores, axis=-1)
        w1 = W1[top1]
        c1 = b1[top1]
        w2 = W2[top1]
        c2 = b2[top1]
        h = jax.nn.relu(jnp.einsum('bnh,bhf->bnf', x, w1) + c1[:, None, :])
        out = jnp.einsum('bnf,bfh->bnh', h, w2) + c2[:, None, :]
        return out
    x = _layernorm(x + _L0_attn_ref(x, L0_attn_Wqkv, L0_attn_bqkv, L0_attn_Wproj, L0_attn_bproj, L0_attn_scale), axis=-1)
    x = _layernorm(x + _L0_xattn_ref(x, ctx_1024, ctx_1024, L0_xattn_wqg, L0_xattn_bqg, L0_xattn_wkg, L0_xattn_bkg, L0_xattn_wvg, L0_xattn_bvg, L0_xattn_wql, L0_xattn_bql, L0_xattn_wkl, L0_xattn_bkl, L0_xattn_wvl, L0_xattn_bvl, L0_xattn_wp, L0_xattn_bp), axis=-1)
    x = _layernorm(x + _L0_ffn_ref(x, L0_ffn_Wr, L0_ffn_br, L0_ffn_W1, L0_ffn_b1, L0_ffn_W2, L0_ffn_b2), axis=-1)
    return x

_drawn_inputs = setup_inputs


def setup_inputs(seed=0):
    import zlib

    import numpy as np

    out = dict(_drawn_inputs(seed))
    spreads = {'L0_attn_bqkv': (0.0, 0.8), 'L0_attn_bproj': (0.0, 0.1)}
    factors = {'L0_attn_Wqkv': 8.0, 'L0_attn_Wproj': 8.0, 'L0_ffn_b1': 5.453, 'L0_ffn_b2': 4.437}
    for name, (base, spread) in spreads.items():
        noise = np.random.default_rng([zlib.crc32(name.encode()), seed]).standard_normal(out[name].shape)
        drawn = base * np.exp(spread * noise) if base else spread * noise
        out[name] = jnp.asarray(drawn.astype(out[name].dtype))
    for name, factor in factors.items():
        out[name] = (out[name] * factor).astype(out[name].dtype)
    return out
```

```python
import concourse.bass as bass
from concourse import mybir
from contextlib import ExitStack

F32 = mybir.dt.float32
F32R = mybir.dt.float32r
U32 = mybir.dt.uint32
ALU = mybir.AluOpType
ACT = mybir.ActivationFunctionType
AX = mybir.AxisListType

P = 128
NB = 16
T = 512
C = 512
CC = C // P
TT = T // P
HD = 32
NH = C // HD
XH = 4
DFF = 2048
FC = DFF // P
NE = 8
EPS_DEN = 0.001
EPS_LN = 1e-05
XSCALE = float(C) ** -0.5


def need(eng, sem, batch, per, upto):
    if isinstance(batch, int):
        if batch * per + upto <= 0:
            return
        eng.wait_ge(sem, min(batch * per + upto, NB * per))
    else:
        eng.wait_ge(sem, batch * per + upto)


def need_alone(eng, sem, batch, per, upto, const_sem, const):
    if not isinstance(batch, int):
        eng.wait_ge(const_sem, const)
    need(eng, sem, batch, per, upto)


def staged(eng, body):
    for i in range(3):
        body(i)
    with eng.Fori(3, NB - 1) as i:
        body(i)
    for i in range(NB - 1, NB + 2):
        body(i)


def inside(b):
    return not isinstance(b, int) or 0 <= b < NB


def setup_weights(nc, d, w):
    with ExitStack() as ctx:
        raw = ctx.enter_context(nc.sbuf_tensor("w_raw", [P, CC, 4 * C], F32))
        w_in = [ctx.enter_context(nc.semaphore(f"w_in{cc}")) for cc in range(CC)]
        w_hi_done = ctx.enter_context(nc.semaphore("w_hi_done"))
        w_lo_done = ctx.enter_context(nc.semaphore("w_lo_done"))
        with nc.Block() as block:

            @block.sync
            def _(sp):
                for cc in range(CC):
                    sp.dma_start(raw[:, cc, :], d["w_attn"][:, cc, :]).then_inc(w_in[cc], 16)

            @block.scalar
            def _(act):
                for cc in range(CC):
                    act.wait_ge(w_in[cc], 16)
                    act.activation(w["hi"][:, cc, :], raw[:, cc, :], ACT.Copy).then_inc(w_hi_done, 1)

            @block.vector
            def _(dve):
                for cc in range(CC):
                    dve.wait_ge(w_hi_done, cc + 1)
                    dve.tensor_tensor(w["lo"][:, cc, :], raw[:, cc, :], w["hi"][:, cc, :].bitcast(F32),
                                      ALU.subtract).then_inc(w_lo_done, 1)
                dve.wait_ge(w_lo_done, CC)


def mixers(nc, d, idx, x2_dram, x2_stored):
    with ExitStack() as ctx:
        def sb(name, shape, dt=F32):
            return ctx.enter_context(nc.sbuf_tensor(name, shape, dt))

        def sem(name):
            return ctx.enter_context(nc.semaphore(name))

        w = {"hi": sb("w_hi", [P, CC, 4 * C], F32R), "lo": sb("w_lo", [P, CC, 4 * C], F32R)}
        setup_weights(nc, d, w)

        rows = sb("rows", [P, 9, C])
        WKG, BKG, WKL, BKL, WVG, BVG, WVL, BVL, BPROJ = range(9)
        cols = sb("cols", [P, 6, XH])
        WQG, BQG, WQL, BQL, WP, BP = range(6)
        b_qkv = sb("b_qkv", [P, 3 * CC])
        sb_qkv = sb("sb_qkv", [P, 3 * CC])
        scale = sb("scale", [P, 1])
        wr = sb("wr", [P, CC, NE])
        br = sb("br", [1, NE])
        ident = sb("ident", [P, P])
        ones = sb("ones", [P, P])
        head_sum = sb("head_sum", [P, CC, NH])
        head_all = sb("head_all", [NH, CC, P])
        half = sb("half", [P, TT])
        ln_eps, minus = sb("ln_eps", [P, TT]), sb("minus", [P, TT])
        nbq = sb("nbq", [P, 2, XH])
        wp2 = sb("wp2", [P, XH])

        xT_raw = sb("xT_raw", [P, CC, T])
        xT_hi = sb("xT_hi", [P, CC, T], F32R)
        xT_lo = sb("xT_lo", [P, CC, T], F32R)
        e_k, r_k = sb("e_k", [P, T]), sb("r_k", [P, T])
        e_q, r_q = sb("e_q", [P, T]), sb("r_q", [P, T])
        k_sum, kv_sum, q = sb("k_sum", [P, T]), sb("kv_sum", [P, T]), sb("q", [P, T])
        qk = sb("qk", [P, CC, T])
        y = sb("y", [P, CC, T])
        y_hi, y_lo = sb("y_hi", [P, CC, T], F32R), sb("y_lo", [P, CC, T], F32R)
        den, rden = sb("den", [NH, T]), sb("rden", [NH, T])
        x_tok = sb("x_tok", [P, TT, C])
        x1 = sb("x1", [P, TT, C])
        ctx_tok, ctx_T = sb("ctx_tok", [P, TT, C]), sb("ctx_T", [P, CC, T])
        x2 = sb("x2", [P, TT, C])
        junk = sb("junk", [P, T])
        c_col = sb("c_col", [P, XH])
        diag = sb("diag", [P, XH, P])
        s_x = sb("s_x", [P, XH])
        s_q = sb("s_q", [P, 2, XH])
        s_a = sb("s_a", [P, 2, XH, P])
        neg_max = sb("neg_max", [P, 2, XH])
        neg_scaled = sb("neg_scaled", [P, 2, XH])
        e_sum = sb("e_sum", [P, 2, XH])
        e_rec = sb("e_rec", [P, 2, XH])
        e_rec2 = sb("e_rec2", [P, 2, XH])
        a_v = sb("a_v", [P, 2, XH, P])
        junk_v = sb("junk_v", [P, P])
        k_const = sb("k_const", [P, 2, XH])
        k_all, k_all2 = sb("k_all", [P, XH]), sb("k_all2", [P, XH])
        aT = sb("aT", [P, XH, P])
        const_b = sb("const_b", [P, C])
        m_col = sb("m_col", [P, CC])
        logits = sb("logits", [1, NE])
        top = sb("top", [1, NE])
        found = sb("found", [1, NE], U32)
        stats = sb("stats", [P, 2, TT, 6])
        mv = sb("mv", [P, 2, TT, 2])
        var_e, rstd, m_r, shift = (sb(n, [P, 2, TT]) for n in ("var_e", "rstd", "m_r", "shift"))

        bank = [ctx.enter_context(nc.psum_tensor(f"bank{i}", [P, 512], F32)) for i in range(8)]
        K_BANK, V_BANK, Q_BANK, DEN_BANK, G_BANK, C_BANK = bank[0], bank[1], bank[2], bank[3], bank[6], bank[7]
        WIDE = [bank[4], bank[5]]
        den_ps = DEN_BANK[0:NH, :]
        route_ps = DEN_BANK[0:1, 0:NE]
        mean_ps, sx_ps = WIDE[0][:, 0:CC], WIDE[1][:, 0:XH]
        g_ps = G_BANK[:, :].rearrange("p (h e) -> p h e", h=XH)
        c_ps = C_BANK[:, :].rearrange("p (h e) -> p h e", h=XH)

        consts_in = sem("consts_in")
        made = sem("made")
        preset = sem("preset")
        xT_in, xtok_in, ctx_in, ctxT_in = sem("xT_in"), sem("xtok_in"), sem("ctx_in"), sem("ctxT_in")
        xhi_done, xlo_done = sem("xhi_done"), sem("xlo_done")
        k_mm, v_mm, q_mm = sem("k_mm"), sem("v_mm"), sem("q_mm")
        ek_done, eq_done = sem("ek_done"), sem("eq_done")
        k_done, kv_done, kc_done = sem("k_done"), sem("kv_done"), sem("kc_done")
        kvc_done, q_done, qk_done, num_done = sem("kvc_done"), sem("q_done"), sem("qk_done"), sem("num_done")
        den_mm, den_max, rden_done, rb_mm = sem("den_mm"), sem("den_max"), sem("rden_done"), sem("rb_mm")
        y_done, yhi_done, ylo_done = sem("y_done"), sem("yhi_done"), sem("ylo_done")
        proj_mm, xb_done, res1_done = sem("proj_mm"), sem("xb_done"), sem("res1_done")
        st_done = [sem("st1_done"), sem("st2_done")]
        mv_done = [sem("mv1_done"), sem("mv2_done")]
        ve_done = [sem("ve1_done"), sem("ve2_done")]
        rstd_done = [sem("rstd1_done"), sem("rstd2_done")]
        mr_done = [sem("mr1_done"), sem("mr2_done")]
        shift_done = [sem("shift1_done"), sem("shift2_done")]
        x1_done, x2_done = sem("x1_done"), sem("x2_done")
        g_mm, sx_mm, c_mm = sem("g_mm"), sem("sx_mm"), sem("c_mm")
        csum_done, diag_done, sx_done, sq_done = sem("csum_done"), sem("diag_done"), sem("sx_done"), sem("sq_done")
        sc_done = sem("sc_done")
        max_done, nmax_done = sem("max_done"), sem("nmax_done")
        exp_done = sem("exp_done")
        rec_done, rec2_done = sem("rec_done"), sem("rec2_done")
        av_done = sem("av_done")
        asum_done, kall_done, kall2_done, diag2_done = (sem(n) for n in ("asum_done", "kall_done", "kall2_done", "diag2_done"))
        aT_mm, kb_mm, aT_done, kb_done, x1c_done = (sem(n) for n in ("aT_mm", "kb_mm", "aT_done", "kb_done", "x1c_done"))
        out_mm, res2_done = sem("out_mm"), sem("res2_done")
        mean_mm, mcol_done, route_mm, logit_done, top_done, idx_done = (
            sem(n) for n in ("mean_mm", "mcol_done", "route_mm", "logit_done", "top_done", "idx_done"))
        found_done = sem("found_done")

        block = ctx.enter_context(nc.Block())
        N_CONST = 6

        @block.sync
        def _(sp):
            sp.dma_start(xT_raw[:, :, :], d["xT"][0]).then_inc(xT_in, 16)
            for r in range(9):
                sp.dma_start(rows[:, r, :], d["rows"][r:r + 1, :].broadcast_to([P, C])).then_inc(consts_in, 16)
            sp.dma_start(cols[:, :, :], d["cols"]).then_inc(consts_in, 16)
            sp.dma_start(b_qkv[:, :], d["b_qkv"]).then_inc(consts_in, 16)
            sp.dma_start(scale[:, :], d["scale"].broadcast_to([P, 1])).then_inc(consts_in, 16)
            sp.dma_start(wr[:, :, :], d["wr"]).then_inc(consts_in, 16)
            sp.dma_start(br[:, :], d["br"]).then_inc(consts_in, 16)

            def step(i):
                a, b, c = i, i - 1, i - 2
                if inside(i + 1):
                    need(sp, xhi_done, a, 1, 1)
                    need(sp, xlo_done, a, 1, 1)
                    sp.dma_start(xT_raw[:, :, :], dyn(d["xT"], i + 1)).then_inc(xT_in, 16)
                if inside(b):
                    need(sp, out_mm, c, TT, TT)
                    need(sp, csum_done, c, XH, XH)
                    sp.dma_start(ctx_T[:, :, :], dyn(d["ctxT"], b)).then_inc(ctxT_in, 16)
                if inside(a):
                    need(sp, x1_done, b, TT, TT)
                    sp.dma_start(x_tok[:, :, :], dyn(d["x_tok"], a)).then_inc(xtok_in, 16)
                if inside(c):
                    need(sp, x2_done, c, TT, TT)
                    sp.dma_start(dyn(x2_dram, c), x2[:, :, :]).then_inc(x2_stored, 16)
                if inside(a):
                    need(sp, g_mm, b, 1, 1)
                    sp.dma_start(ctx_tok[:, :, :], dyn(d["ctx_tok"], a)).then_inc(ctx_in, 16)

            staged(sp, step)
            sp.wait_ge(x2_stored, 16 * NB)

        @block.gpsimd
        def _(pool):
            pool.memset(ident[:, :], 0.0).then_inc(made, 1)
            pool.memset(ones[:, :], 1.0).then_inc(made, 1)
            pool.memset(head_sum[:, :, :], 1.0).then_inc(made, 1)
            pool.memset(head_all[:, :, :], 1.0).then_inc(made, 1)
            pool.memset(half[:, :], -0.5).then_inc(made, 1)
            pool.memset(ln_eps[:, :], EPS_LN).then_inc(made, 1)
            pool.memset(minus[:, :], -1.0).then_inc(made, 1)
            pool.wait_ge(made, 7)
            pool.affine_select(out=ident[:, :], in_=ident[:, :], compare_op=ALU.not_equal, fill=1.0, base=0,
                               pattern=[[-1, P]], channel_multiplier=1).then_inc(made, 1)
            pool.affine_select(out=head_sum[:, :, :], in_=head_sum[:, :, :], compare_op=ALU.is_ge, fill=0.0, base=0,
                               pattern=[[P, CC], [-HD, NH]], channel_multiplier=1).then_inc(made, 1)
            pool.affine_select(out=head_all[:, :, :], in_=head_all[:, :, :], compare_op=ALU.is_ge, fill=0.0, base=0,
                               pattern=[[P, CC], [1, P]], channel_multiplier=-HD).then_inc(made, 1)
            pool.wait_ge(made, 10)
            pool.affine_select(out=head_sum[:, :, :], in_=head_sum[:, :, :], compare_op=ALU.is_ge, fill=0.0, base=HD - 1,
                               pattern=[[-P, CC], [HD, NH]], channel_multiplier=-1).then_inc(made, 1)
            pool.affine_select(out=head_all[:, :, :], in_=head_all[:, :, :], compare_op=ALU.is_ge, fill=0.0, base=HD - 1,
                               pattern=[[-P, CC], [-1, P]], channel_multiplier=HD).then_inc(made, 1)
            pool.wait_ge(made, 12)
            pool.wait_ge(consts_in, 16 * (N_CONST + 8))

            def rstd_of(n, b):
                need(pool, mv_done[n], b, TT, TT)
                need(pool, x1_done if n == 0 else x2_done, b - 1, TT, TT)
                pool.tensor_tensor(var_e[:, n, :], mv[:, n, :, 1], ln_eps[:, :], ALU.add).then_inc(ve_done[n], 1)
                need(pool, ve_done[n], b, 1, 1)
                pool.tensor_tensor(rstd[:, n, :], var_e[:, n, :], half[:, :], ALU.pow).then_inc(rstd_done[n], 1)
                need(pool, rstd_done[n], b, 1, 1)
                pool.tensor_tensor(m_r[:, n, :], mv[:, n, :, 0], rstd[:, n, :], ALU.mult).then_inc(mr_done[n], 1)
                need(pool, mr_done[n], b, 1, 1)
                pool.tensor_tensor(shift[:, n, :], m_r[:, n, :], minus[:, :], ALU.mult).then_inc(shift_done[n], 1)

            def step(i):
                b, c = i - 1, i - 2
                if inside(b):
                    need(pool, xtok_in, b, 16, 16)
                    pool.tensor_tensor(x_tok[:, :, :], x_tok[:, :, :],
                                       rows[:, BPROJ:BPROJ + 1, :].broadcast_to([P, TT, C]), ALU.add).then_inc(xb_done, 1)
                if inside(c):
                    need(pool, kall2_done, c, 1, 1)
                    need(pool, c_mm, c, 1, 1)
                    pool.tensor_tensor(diag[:, :, :], ident[:, :].unsqueeze(1).broadcast_to([P, XH, P]),
                                       k_all2[:, :].unsqueeze(2).broadcast_to([P, XH, P]), ALU.mult).then_inc(diag2_done, 1)
                    need(pool, kb_done, c, 1, 1)
                    need(pool, sx_mm, c, 1, 1)
                    pool.tensor_tensor(x1[:, :, :], x1[:, :, :],
                                       const_b[:, :].unsqueeze(1).broadcast_to([P, TT, C]), ALU.add).then_inc(x1c_done, 1)
                if inside(b):
                    rstd_of(0, b)
                if inside(c):
                    rstd_of(1, c)
                if inside(b):
                    need(pool, csum_done, b, XH, XH)
                    need(pool, kb_mm, c, 1, 1)
                    pool.tensor_tensor(diag[:, :, :], ident[:, :].unsqueeze(1).broadcast_to([P, XH, P]),
                                       c_col[:, :].unsqueeze(2).broadcast_to([P, XH, P]), ALU.mult).then_inc(diag_done, 1)

            staged(pool, step)

        @block.scalar
        def _(act):
            act.wait_ge(preset, 4)

            def features(a, cc):
                for n, (mm, e, r, done, used, ps) in enumerate((
                        (k_mm, e_k, r_k, ek_done, k_done, K_BANK), (q_mm, e_q, r_q, eq_done, q_done, Q_BANK))):
                    col = (1 - n) * CC + cc
                    need(act, mm, a, CC, cc + 1)
                    need(act, used, a, CC, cc)
                    act.activation(e[:, :], ps[:, :], ACT.Exp, bias=sb_qkv[:, col:col + 1],
                                   scale=scale[:, 0:1]).then_inc(done, 1)
                    act.activation(r[:, :], ps[:, :], ACT.Relu, bias=sb_qkv[:, col:col + 1],
                                   scale=scale[:, 0:1]).then_inc(done, 1)

            def split_x(b):
                need(act, xT_in, b, 16, 16)
                need(act, q_mm, b - 1, CC, CC)
                act.activation(xT_hi[:, :, :], xT_raw[:, :, :], ACT.Copy).then_inc(xhi_done, 1)

            def normalise(n, b):
                need(act, shift_done[n], b, 1, 1)
                if n == 0:
                    need(act, res2_done, b - 1, TT, TT)
                src, dst, done = ((x_tok, x1, x1_done), (x2, x2, x2_done))[n]
                for t in range(TT):
                    act.activation(dst[:, t, :], src[:, t, :], ACT.Identity, bias=shift[:, n, t:t + 1],
                                   scale=rstd[:, n, t:t + 1]).then_inc(done, 1)

            split_x(0)

            def step(i):
                a, b, c = i, i - 1, i - 2
                if inside(a):
                    features(a, 0)
                if inside(b):
                    need(act, proj_mm, c, TT, TT)
                    for cc in range(CC):
                        need(act, y_done, b, CC, cc + 1)
                        act.activation(y_hi[:, cc, :], y[:, cc, :], ACT.Copy).then_inc(yhi_done, 1)
                if inside(a):
                    features(a, 1)
                if inside(c):
                    for v in range(2):
                        need(act, nmax_done, c, 2, v + 1)
                        need(act, av_done, c - 1, 4 * XH, 4 * XH)
                        for h in range(XH):
                            act.activation(s_a[:, v, h, :], s_a[:, v, h, :], ACT.Exp, bias=neg_scaled[:, v, h:h + 1],
                                           scale=XSCALE, accum_out=e_sum[:, v, h:h + 1]).then_inc(exp_done, 1)
                if inside(a):
                    features(a, 2)
                if inside(c):
                    need(act, aT_mm, c, 1, 1)
                    need(act, out_mm, c - 1, TT, TT)
                    act.activation(aT[:, :, :], g_ps, ACT.Copy).then_inc(aT_done, 1)
                    need(act, kb_mm, c, 1, 1)
                    need(act, x1c_done, c - 1, 1, 1)
                    act.activation(const_b[:, :], C_BANK[:, :], ACT.Copy).then_inc(kb_done, 1)
                if inside(b):
                    normalise(0, b)
                if inside(a):
                    features(a, 3)
                if inside(c):
                    normalise(1, c)
                if inside(b):
                    need(act, ctxT_in, b, 16, 16)
                    need(act, diag_done, c, 1, 1)
                    for h in range(XH):
                        need(act, csum_done, b, XH, h)
                        act.activation(junk[:, :], ctx_T[:, h, :], ACT.Copy,
                                       accum_out=c_col[:, h:h + 1]).then_inc(csum_done, 1)
                if inside(c):
                    need(act, mean_mm, c, 1, 1)
                    need(act, route_mm, c - 1, 1, 1)
                    act.activation(m_col[:, :], mean_ps, ACT.Copy, scale=1.0 / T).then_inc(mcol_done, 1)
                if inside(i + 1):
                    split_x(i + 1)

            staged(act, step)

        @block.vector
        def _(dve):
            dve.wait_ge(consts_in, 16 * (N_CONST + 8))
            dve.tensor_scalar(sb_qkv[:, :], b_qkv[:, :], scale[:, 0:1], None, ALU.mult).then_inc(preset, 1)
            dve.tensor_scalar(nbq[:, 0, :], cols[:, BQG, :], float(T), None, ALU.mult).then_inc(preset, 1)
            dve.tensor_scalar(nbq[:, 1, :], cols[:, BQL, :], float(T), None, ALU.mult).then_inc(preset, 1)
            dve.tensor_scalar(wp2[:, :], cols[:, WP, :], 2.0, None, ALU.mult).then_inc(preset, 1)
            dve.wait_ge(preset, 4)

            def keys_values(a, cc):
                need(dve, ek_done, a, 2 * CC, 2 * cc + 2)
                need(dve, qk_done, a, CC, cc)
                dve.scalar_tensor_tensor(k_sum[:, :], e_k[:, :], 1.0, r_k[:, :], ALU.min, ALU.add).then_inc(k_done, 1)
                need(dve, v_mm, a, CC, cc + 1)
                need(dve, k_done, a, CC, cc + 1)
                need(dve, num_done, a, CC, cc)
                dve.scalar_tensor_tensor(kv_sum[:, :], V_BANK[:, :], b_qkv[:, 2 * CC + cc:2 * CC + cc + 1],
                                         k_sum[:, :], ALU.add, ALU.mult).then_inc(kv_done, 1)
                need(dve, kv_done, a, CC, cc + 1)
                dve.tensor_tensor_scan(k_sum[:, :], k_sum[:, :], k_sum[:, :], 0.0, ALU.add, ALU.bypass).then_inc(kc_done, 1)
                dve.tensor_tensor_scan(kv_sum[:, :], kv_sum[:, :], kv_sum[:, :], 0.0, ALU.add, ALU.bypass).then_inc(kvc_done, 1)
                need(dve, eq_done, a, 2 * CC, 2 * cc + 2)
                dve.scalar_tensor_tensor(q[:, :], e_q[:, :], 1.0, r_q[:, :], ALU.min, ALU.add).then_inc(q_done, 1)
                need(dve, q_done, a, CC, cc + 1)
                need(dve, kc_done, a, CC, cc + 1)
                need(dve, den_mm, a - 1, 1, 1)
                dve.tensor_tensor(qk[:, cc, :], q[:, :], k_sum[:, :], ALU.mult).then_inc(qk_done, 1)

            def numerator(a, cc):
                need(dve, q_done, a, CC, cc + 1)
                need(dve, kvc_done, a, CC, cc + 1)
                need(dve, ylo_done, a - 1, CC, CC)
                dve.tensor_tensor(y[:, cc, :], q[:, :], kv_sum[:, :], ALU.mult).then_inc(num_done, 1)

            def residual(n, b, t):
                mm, res, done, src, dst = ((proj_mm, x_tok, res1_done, x_tok, x_tok),
                                           (out_mm, x1, res2_done, x1, x2))[n]
                need(dve, mm, b, TT, t + 1)
                if n == 0:
                    need(dve, xb_done, b, 1, 1)
                else:
                    need(dve, x1c_done, b, 1, 1)
                    need(dve, mean_mm, b - 1, 1, 1)
                    need(dve, x2_stored, b - 1, 16, 16)
                ps = WIDE[t % 2]
                dve.tensor_tensor(dst[:, t, :], ps[:, :], src[:, t, :], ALU.add).then_inc(done, 1)

            def statistics(n, b):
                done = (res1_done, res2_done)[n]
                x = (x_tok, x2)[n]
                for t in range(TT):
                    need(dve, done, b, TT, t + 1)
                    need(dve, mv_done[n], b - 1, TT, TT)
                    dve.bn_stats(stats[:, n, t, :], x[:, t, :]).then_inc(st_done[n], 1)
                for t in range(TT):
                    need_alone(dve, st_done[n], b, TT, t + 1, preset, 4)
                    if t == 0:
                        need(dve, shift_done[n], b - 1, 1, 1)
                    dve.bn_aggr(mv[:, n, t, :], stats[:, n, t, :]).then_inc(mv_done[n], 1)

            def token_sums(c):
                need(dve, sx_mm, c, 1, 1)
                dve.tensor_copy(s_x[:, :], sx_ps).then_inc(sx_done, 1)
                need(dve, sx_done, c, 1, 1)
                dve.tensor_tensor(s_q[:, 0, :], s_x[:, :], cols[:, WQG, :], ALU.mult).then_inc(sq_done, 1)
                dve.tensor_tensor(s_q[:, 1, :], s_x[:, :], cols[:, WQL, :], ALU.mult).then_inc(sq_done, 1)
                need(dve, sq_done, c, 3, 2)
                dve.tensor_tensor(s_q[:, :, :], s_q[:, :, :], nbq[:, :, :], ALU.add).then_inc(sq_done, 1)

            def scores(c):
                need(dve, g_mm, c, 1, 1)
                need(dve, c_mm, c, 1, 1)
                need(dve, av_done, c - 1, 4 * XH, 4 * XH)
                wq, bq = (WQG, WQL), (BQG, BQL)
                for v in range(2):
                    dve.tensor_tensor(s_a[:, v, :, :], g_ps, cols[:, wq[v], :].unsqueeze(2).broadcast_to([P, XH, P]),
                                      ALU.mult).then_inc(sc_done, 1)
                    dve.tensor_tensor(a_v[:, v, :, :], c_ps, cols[:, bq[v], :].unsqueeze(2).broadcast_to([P, XH, P]),
                                      ALU.mult).then_inc(sc_done, 1)
                wk, bk = (WKG, WKL), (BKG, BKL)

                def row(n):
                    return rows[:, n, :].rearrange("p (h e) -> p h e", h=XH)

                need(dve, sc_done, c, 12, 4)
                for v in range(2):
                    dve.tensor_tensor(s_a[:, v, :, :], s_a[:, v, :, :], a_v[:, v, :, :], ALU.add).then_inc(sc_done, 1)
                need(dve, sc_done, c, 12, 6)
                need(dve, sq_done, c, 3, 3)
                for v in range(2):
                    dve.tensor_tensor(s_a[:, v, :, :], s_a[:, v, :, :], row(wk[v]), ALU.mult).then_inc(sc_done, 1)
                    dve.tensor_tensor(a_v[:, v, :, :], row(bk[v]), s_q[:, v, :].unsqueeze(2).broadcast_to([P, XH, P]),
                                      ALU.mult).then_inc(sc_done, 1)
                need(dve, sc_done, c, 12, 10)
                for v in range(2):
                    dve.tensor_tensor(s_a[:, v, :, :], s_a[:, v, :, :], a_v[:, v, :, :], ALU.add).then_inc(sc_done, 1)
                for v in range(2):
                    need(dve, sc_done, c, 12, 11 + v)
                    dve.reduce_max(neg_max[:, v, :], s_a[:, v, :, :], AX.X).then_inc(max_done, 1)
                for v in range(2):
                    need(dve, max_done, c, 2, v + 1)
                    dve.tensor_scalar(neg_scaled[:, v, :], neg_max[:, v, :], -XSCALE, None, ALU.mult).then_inc(nmax_done, 1)

            def weigh(c):
                need(dve, exp_done, c, 2 * XH, 2 * XH)
                dve.reciprocal(e_rec[:, :, :], e_sum[:, :, :]).then_inc(rec_done, 1)
                need(dve, rec_done, c, 1, 1)
                dve.tensor_tensor(e_rec2[:, :, :], e_rec[:, :, :], wp2[:, :].unsqueeze(1).broadcast_to([P, 2, XH]),
                                  ALU.mult).then_inc(rec2_done, 1)
                need(dve, rec2_done, c, 1, 1)
                need(dve, kall_done, c - 1, 1, 1)
                n = 0
                for v, (wv, bv) in enumerate(((WVG, BVG), (WVL, BVL))):
                    for h in range(XH):
                        hs = slice(h * P, h * P + P)
                        need(dve, av_done, c, 4 * XH, n)
                        dve.scalar_tensor_tensor(junk_v[:, :], s_a[:, v, h, :], e_rec2[:, v, h:h + 1], rows[:, bv, hs],
                                                 ALU.mult, ALU.mult, accum_out=k_const[:, v, h:h + 1]).then_inc(av_done, 1)
                        dve.scalar_tensor_tensor(a_v[:, v, h, :], s_a[:, v, h, :], e_rec2[:, v, h:h + 1], rows[:, wv, hs],
                                                 ALU.mult, ALU.mult).then_inc(av_done, 1)
                        n += 2
                need(dve, av_done, c, 4 * XH, 4 * XH)
                dve.tensor_tensor(k_all[:, :], k_const[:, 0, :], k_const[:, 1, :], ALU.add).then_inc(kall_done, 1)
                dve.tensor_tensor(a_v[:, 0, :, :], a_v[:, 0, :, :], a_v[:, 1, :, :], ALU.add).then_inc(asum_done, 1)
                need(dve, kall_done, c, 1, 1)
                need(dve, diag2_done, c - 1, 1, 1)
                dve.tensor_tensor(k_all2[:, :], k_all[:, :], cols[:, BP, :], ALU.add).then_inc(kall2_done, 1)

            def choose(c):
                need(dve, route_mm, c, 1, 1)
                dve.tensor_tensor(logits[:, :], route_ps, br[:, :], ALU.add).then_inc(logit_done, 1)
                need_alone(dve, logit_done, c, 1, 1, preset, 4)
                dve.max(top[:, :], logits[:, :]).then_inc(top_done, 1)
                need_alone(dve, top_done, c, 1, 1, preset, 4)
                dve.max_index(found[:, :], top[:, :], logits[:, :]).then_inc(found_done, 1)
                need(dve, found_done, c, 1, 1)
                dve.tensor_copy(idx[0:1, c:c + 1] if isinstance(c, int) else idx[0:1, bass.ds(c, 1)],
                                found[:, 0:1]).then_inc(idx_done, 1)

            def split_x(b):
                need(dve, xhi_done, b, 1, 1)
                need(dve, q_mm, b - 1, CC, CC)
                dve.tensor_tensor(xT_lo[:, :, :], xT_raw[:, :, :], xT_hi[:, :, :].bitcast(F32), ALU.subtract).then_inc(xlo_done, 1)

            split_x(0)

            def step(i):
                a, b, c = i, i - 1, i - 2
                if inside(c):
                    token_sums(c)
                if inside(b):
                    need(dve, den_mm, b, 1, 1)
                    dve.tensor_scalar(den[:, :], den_ps, EPS_DEN, None, ALU.max).then_inc(den_max, 1)
                    need(dve, den_max, b, 1, 1)
                    need(dve, rb_mm, b - 1, CC, CC)
                    dve.reciprocal(rden[:, :], den[:, :]).then_inc(rden_done, 1)
                if inside(a):
                    keys_values(a, 0)
                if inside(b):
                    for cc in range(CC):
                        need(dve, rb_mm, b, CC, cc + 1)
                        need(dve, num_done, b, CC, cc + 1)
                        dve.tensor_tensor(y[:, cc, :], y[:, cc, :], WIDE[cc % 2][:, :], ALU.mult).then_inc(y_done, 1)
                    for cc in range(CC):
                        need(dve, yhi_done, b, CC, cc + 1)
                        need(dve, proj_mm, b - 1, TT, TT)
                        dve.tensor_tensor(y_lo[:, cc, :], y[:, cc, :], y_hi[:, cc, :].bitcast(F32), ALU.subtract).then_inc(ylo_done, 1)
                if inside(a):
                    numerator(a, 0)
                if inside(c):
                    scores(c)
                if inside(a):
                    keys_values(a, 1)
                    numerator(a, 1)
                if inside(c):
                    weigh(c)
                if inside(a):
                    keys_values(a, 2)
                    numerator(a, 2)
                if inside(b):
                    for t in range(TT):
                        residual(0, b, t)
                    statistics(0, b)
                if inside(c):
                    for t in range(TT):
                        residual(1, c, t)
                    statistics(1, c)
                if inside(a):
                    keys_values(a, 3)
                    numerator(a, 3)
                if inside(i + 1):
                    split_x(i + 1)
                if inside(c):
                    choose(c)

            staged(dve, step)

        @block.tensor
        def _(pe):
            pe.wait_ge(made, 12)
            pe.wait_ge(consts_in, 16 * (N_CONST + 8))

            def product(out, pairs, done):
                n = 0
                for (ah, al), (bh, bl) in pairs:
                    for lhsT, rhs in ((ah, bh), (ah, bl), (al, bh)):
                        last = pe.matmul(out, lhsT, rhs, start=(n == 0), stop=(n == 3 * len(pairs) - 1))
                        n += 1
                last.then_inc(done, 1)

            def qkv(a, cc):
                if cc == 0:
                    need(pe, xhi_done, a, 1, 1)
                    need(pe, xlo_done, a, 1, 1)
                for part, ps, done, free, per in ((1, K_BANK, k_mm, ek_done, 2), (2, V_BANK, v_mm, kv_done, 1),
                                                  (0, Q_BANK, q_mm, eq_done, 2)):
                    need(pe, free, a, per * CC, per * cc)
                    es = slice(part * C + cc * P, part * C + cc * P + P)
                    product(ps[:, :], [((w["hi"][:, j, es], w["lo"][:, j, es]), (xT_hi[:, j, :], xT_lo[:, j, :]))
                                       for j in range(CC)], done)

            def step(i):
                a, b, c = i, i - 1, i - 2
                if inside(b):
                    need(pe, qk_done, b, CC, CC)
                    need(pe, idx_done, b - 2, 1, 1)
                    for cc in range(CC):
                        last = pe.matmul(den_ps, head_sum[:, cc, :], qk[:, cc, :], start=(cc == 0), stop=(cc == CC - 1))
                    last.then_inc(den_mm, 1)
                if inside(a):
                    qkv(a, 0)
                if inside(b):
                    need(pe, rden_done, b, 1, 1)
                    for cc in range(CC):
                        if cc == 0:
                            need(pe, mcol_done, b - 2, 1, 1)
                        elif cc == 1:
                            need(pe, sx_done, b - 1, 1, 1)
                        else:
                            need(pe, y_done, b, CC, cc - 1)
                        pe.matmul(WIDE[cc % 2][:, :], head_all[:, cc, :], rden[:, :], start=True, stop=True).then_inc(rb_mm, 1)
                if inside(a):
                    qkv(a, 1)
                    qkv(a, 2)
                if inside(c):
                    need(pe, asum_done, c, 1, 1)
                    for h in range(XH):
                        last = pe.transpose(G_BANK[:, h * P:h * P + P], a_v[:, 0, h, :], ident[:, :])
                    last.then_inc(aT_mm, 1)
                    need(pe, diag2_done, c, 1, 1)
                    pe.matmul(c_ps, ones[:, :], diag[:, :, :], start=True, stop=True).then_inc(kb_mm, 1)
                if inside(b):
                    need(pe, yhi_done, b, CC, CC)
                    need(pe, ylo_done, b, CC, CC)
                    for t in range(TT):
                        if t >= 2:
                            need(pe, res1_done, b, TT, t - 1)
                        else:
                            need(pe, y_done, b, CC, CC)
                        ts = slice(t * P, t * P + P)
                        product(WIDE[t % 2][:, :], [((y_hi[:, j, ts], y_lo[:, j, ts]), (w["hi"][:, j, 3 * C:], w["lo"][:, j, 3 * C:]))
                                                    for j in range(CC)], proj_mm)
                if inside(c):
                    need(pe, aT_done, c, 1, 1)
                    need(pe, ctxT_in, c, 16, 16)
                    for t in range(TT):
                        if t >= 2:
                            need(pe, res2_done, c, TT, t - 1)
                        else:
                            need(pe, res1_done, b, TT, TT)
                        for h in range(XH):
                            last = pe.matmul(WIDE[t % 2][:, h * P:h * P + P], ctx_T[:, h, t * P:t * P + P], aT[:, h, :],
                                             start=True, stop=True)
                        last.then_inc(out_mm, 1)
                if inside(a):
                    qkv(a, 3)
                if inside(c):
                    need(pe, x2_done, c, TT, TT)
                    need(pe, res2_done, c, TT, TT)
                    for j in range(CC):
                        for t in range(TT):
                            last = pe.matmul(mean_ps[:, j:j + 1], x2[:, t, j * P:j * P + P], ones[:, 0:1],
                                             start=(t == 0), stop=(t == TT - 1))
                    last.then_inc(mean_mm, 1)
                if inside(b):
                    need(pe, x1_done, b, TT, TT)
                    need(pe, ctx_in, b, 16, 16)
                    need(pe, aT_done, c, 1, 1)
                    need(pe, res2_done, c, TT, TT)
                    for h in range(XH):
                        hs = slice(h * P, h * P + P)
                        for t in range(TT):
                            last = pe.matmul(g_ps[:, h, :], x1[:, t, hs], ctx_tok[:, t, hs], start=(t == 0), stop=(t == TT - 1))
                    last.then_inc(g_mm, 1)
                    need(pe, res1_done, b, TT, TT)
                    for h in range(XH):
                        for t in range(TT):
                            last = pe.matmul(sx_ps[:, h:h + 1], x1[:, t, h * P:h * P + P], ones[:, 0:1],
                                             start=(t == 0), stop=(t == TT - 1))
                    last.then_inc(sx_mm, 1)
                    need(pe, diag_done, b, 1, 1)
                    need(pe, kb_done, c, 1, 1)
                    pe.matmul(c_ps, ones[:, :], diag[:, :, :], start=True, stop=True).then_inc(c_mm, 1)
                if inside(c):
                    need(pe, mcol_done, c, 1, 1)
                    need(pe, den_max, b, 1, 1)
                    for j in range(CC):
                        last = pe.matmul(route_ps, m_col[:, j:j + 1], wr[:, j, :], start=(j == 0), stop=(j == CC - 1))
                    last.then_inc(route_mm, 1)

            staged(pe, step)


def dyn(ap, b):
    return ap[b] if isinstance(b, int) else ap[bass.ds(b, 1)].rearrange("a p t n -> p (a t) n")


def experts(nc, d, idx, x2_dram, out):
    with ExitStack() as ctx:
        def sb(name, shape, dt=F32):
            return ctx.enter_context(nc.sbuf_tensor(name, shape, dt))

        def sem(name):
            return ctx.enter_context(nc.semaphore(name))

        NR = 4
        AHEAD = 2
        LAG = 2
        raw = sb("raw", [P, NR, 2 * C])
        w_hi, w_lo = sb("we_hi", [P, NR, 2 * C], F32R), sb("we_lo", [P, NR, 2 * C], F32R)
        x_res = [sb(f"x_res{i}", [P, TT, C]) for i in range(2)]
        xT_hi = [sb(f"x2T_hi{i}", [P, CC, T], F32R) for i in range(2)]
        xT_lo = [sb(f"x2T_lo{i}", [P, CC, T], F32R) for i in range(2)]
        hid = sb("hid", [P, 2, T])
        h_hi, h_lo = sb("h_hi", [P, NR, T], F32R), sb("h_lo", [P, NR, T], F32R)
        b1 = sb("b1", [P, 2, FC])
        b2 = sb("b2", [P, 2, C])
        ident = sb("ident_e", [P, P])
        half, ln_eps, minus = (sb(n, [P, TT]) for n in ("half_e", "ln_eps_e", "minus_e"))
        stats, mv = sb("stats_e", [P, TT, 6]), sb("mv_e", [P, TT, 2])
        var_e, rstd, m_r, shift = (sb(n, [P, TT]) for n in ("var_f", "rstd_f", "m_r_f", "shift_f"))
        acc = [ctx.enter_context(nc.psum_tensor(f"acc{t}", [P, C], F32)) for t in range(TT)]
        h_ps = [ctx.enter_context(nc.psum_tensor(f"h_ps{i}", [P, T], F32)) for i in range(2)]
        t_ps = [ctx.enter_context(nc.psum_tensor(f"t_ps{i}", [P, T], F32)) for i in range(2)]

        made = sem("made_e")
        w_in = [sem(f"we_in{s}") for s in range(NR)]
        b_in = [sem("b_in0"), sem("b_in1")]
        x_in = [sem("x2_in0"), sem("x2_in1")]
        whi_done, wlo_done = sem("whi_done"), sem("wlo_done")
        up_mm, down_mm = sem("up_mm"), sem("down_mm")
        h_done, hhi_done, hlo_done = sem("h_done"), sem("hhi_done"), sem("hlo_done")
        tr_mm, xhi_done, xlo_done = sem("tr_mm"), sem("x2hi_done"), sem("x2lo_done")
        xb_done, acc_mm = sem("x2b_done"), sem("acc_mm")
        res_done, st_done, mv_done = sem("res_done"), sem("st_done"), sem("mv_done")
        ve_done, rstd_done, mr_done, shift_done = (sem(n) for n in ("ve_done", "rstd_done", "mr_done", "shift_done"))
        norm_done = sem("norm_done")
        stored = sem("stored")
        block = ctx.enter_context(nc.Block())
        TR_AT = (6, 8, 10, 12)

        def paired(eng, body):
            for b in range(2):
                body(b, b % 2)
            with eng.Fori(1, NB // 2 - 1) as pair:
                for parity in range(2):
                    body(pair * 2 + parity, parity)
            for b in range(NB - 2, NB):
                body(b, b % 2)

        def b_wait(eng, b, parity):
            eng.wait_ge(b_in[parity], (b - parity) * 16 + 32)

        def w_wait(eng, b, f):
            if isinstance(b, int) and f >= FC:
                b, f = b + 1, f - FC
            eng.wait_ge(w_in[f % NR], b * (16 * FC // NR) + 16 * (f // NR + 1))

        def after_last(b, f):
            return isinstance(b, int) and b * FC + f >= NB * FC

        @block.sync
        def _(sp):
            sp.dma_start(x_res[0][:, :, :], x2_dram[0]).then_inc(x_in[0], 16)

            def step(b, parity):
                e = sp.value_load(idx[0:1, bass.ds(b, 1)], min_val=0, max_val=NE - 1)
                need(sp, h_done, b - 2, FC, FC)
                sp.dma_start(b1[:, parity, :], d["b1"][bass.ds(e, 1)].rearrange("a p f -> p (a f)")).then_inc(b_in[parity], 16)
                need(sp, xb_done, b - 2, 1, 1)
                sp.dma_start(b2[:, parity, :], d["b2"][bass.ds(e, 1), :].broadcast_to([P, C])).then_inc(b_in[parity], 16)
                for f in range(FC):
                    need(sp, wlo_done, b, FC, f - NR + 1)
                    sp.dma_start(raw[:, f % NR, :],
                                 d["w12"][bass.ds(e, 1), f].rearrange("a p n -> p (a n)")).then_inc(w_in[f % NR], 16)
                    if f == 3:
                        if inside(b - 1) and not (isinstance(b, int) and b == 0):
                            need(sp, norm_done, b - 1, TT, TT)
                            sp.dma_start(dyn(out, b - 1), x_res[1 - parity][:, :, :]).then_inc(stored, 16)
                        if inside(b + 1):
                            need(sp, stored, b - 1, 16, 16)
                            sp.dma_start(x_res[1 - parity][:, :, :], dyn(x2_dram, b + 1)).then_inc(x_in[1 - parity], 16)

            paired(sp, step)
            sp.wait_ge(norm_done, NB * TT)
            sp.dma_start(out[NB - 1], x_res[1][:, :, :]).then_inc(stored, 16)
            sp.wait_ge(stored, 16 * NB)

        @block.gpsimd
        def _(pool):
            pool.memset(ident[:, :], 0.0).then_inc(made, 1)
            pool.memset(half[:, :], -0.5).then_inc(made, 1)
            pool.memset(ln_eps[:, :], EPS_LN).then_inc(made, 1)
            pool.memset(minus[:, :], -1.0).then_inc(made, 1)
            pool.wait_ge(made, 4)
            pool.affine_select(out=ident[:, :], in_=ident[:, :], compare_op=ALU.not_equal, fill=1.0, base=0,
                               pattern=[[-1, P]], channel_multiplier=1).then_inc(made, 1)

            def step(b, parity):
                need(pool, tr_mm, b, CC, CC)
                b_wait(pool, b, parity)
                pool.tensor_tensor(x_res[parity][:, :, :], x_res[parity][:, :, :],
                                   b2[:, parity:parity + 1, :].broadcast_to([P, TT, C]), ALU.add).then_inc(xb_done, 1)
                need(pool, mv_done, b, TT, TT)
                need(pool, norm_done, b - 1, TT, TT)
                pool.tensor_tensor(var_e[:, :], mv[:, :, 1], ln_eps[:, :], ALU.add).then_inc(ve_done, 1)
                need(pool, ve_done, b, 1, 1)
                pool.tensor_tensor(rstd[:, :], var_e[:, :], half[:, :], ALU.pow).then_inc(rstd_done, 1)
                need(pool, rstd_done, b, 1, 1)
                pool.tensor_tensor(m_r[:, :], mv[:, :, 0], rstd[:, :], ALU.mult).then_inc(mr_done, 1)
                need(pool, mr_done, b, 1, 1)
                pool.tensor_tensor(shift[:, :], m_r[:, :], minus[:, :], ALU.mult).then_inc(shift_done, 1)

            paired(pool, step)

        @block.scalar
        def _(act):
            def split_w(b, f):
                if after_last(b, f):
                    return
                w_wait(act, b, f)
                need(act, down_mm, b, FC, f - NR + 1)
                need(act, up_mm, b, FC, f - NR + 1)
                s = f % NR
                act.activation(w_hi[:, s, :], raw[:, s, :], ACT.Copy).then_inc(whi_done, 1)

            def split_x(b, parity, j):
                need(act, tr_mm, b, CC, j + 1)
                need(act, up_mm, b - 2, FC, FC)
                act.activation(xT_hi[parity][:, j, :], t_ps[j % 2][:, :], ACT.Copy).then_inc(xhi_done, 1)

            for j in range(CC):
                split_x(0, 0, j)
            for f in range(AHEAD):
                split_w(0, f)

            def step(b, parity):
                for f in range(FC):
                    need(act, up_mm, b, FC, f + 1)
                    if f == 0:
                        b_wait(act, b, parity)
                    need(act, hlo_done, b, FC, f - 1)
                    act.activation(hid[:, f % 2, :], h_ps[f % 2][:, :], ACT.Relu, bias=b1[:, parity, f:f + 1]).then_inc(h_done, 1)
                    split_w(b, f + AHEAD)
                    if f in TR_AT and inside(b + 1):
                        split_x(b + 1, 1 - parity, TR_AT.index(f))
                    if f == 1:
                        finish(b - 1, 1 - parity)

            def finish(b, parity):
                if not inside(b):
                    return
                need(act, shift_done, b, 1, 1)
                for t in range(TT):
                    act.activation(x_res[parity][:, t, :], x_res[parity][:, t, :], ACT.Identity,
                                   bias=shift[:, t:t + 1], scale=rstd[:, t:t + 1]).then_inc(norm_done, 1)

            paired(act, step)
            finish(NB - 1, 1)

        @block.vector
        def _(dve):
            def split_w(b, f):
                if after_last(b, f):
                    return
                need(dve, whi_done, b, FC, f + 1)
                need(dve, down_mm, b, FC, f - NR + 1)
                s = f % NR
                dve.tensor_tensor(w_lo[:, s, :], raw[:, s, :], w_hi[:, s, :].bitcast(F32), ALU.subtract).then_inc(wlo_done, 1)

            def split_x(b, parity, j):
                need(dve, xhi_done, b, CC, j + 1)
                need(dve, up_mm, b - 2, FC, FC)
                dve.tensor_tensor(xT_lo[parity][:, j, :], t_ps[j % 2][:, :], xT_hi[parity][:, j, :].bitcast(F32),
                                  ALU.subtract).then_inc(xlo_done, 1)

            for j in range(CC):
                split_x(0, 0, j)
            for f in range(AHEAD):
                split_w(0, f)

            def step(b, parity):
                for f in range(FC):
                    need(dve, h_done, b, FC, f + 1)
                    need(dve, down_mm, b, FC, f - NR + 1)
                    s = f % NR
                    dve.tensor_copy(h_hi[:, s, :], hid[:, f % 2, :]).then_inc(hhi_done, 1)
                    need(dve, hhi_done, b, FC, f + 1)
                    dve.tensor_tensor(h_lo[:, s, :], hid[:, f % 2, :], h_hi[:, s, :].bitcast(F32), ALU.subtract).then_inc(hlo_done, 1)
                    split_w(b, f + AHEAD)
                    if f in TR_AT and inside(b + 1):
                        split_x(b + 1, 1 - parity, TR_AT.index(f))
                for t in range(TT):
                    if t < TT - 1:
                        need(dve, acc_mm, b, TT - 1, t + 1)
                    else:
                        need(dve, down_mm, b, FC, FC)
                    need(dve, xb_done, b, 1, 1)
                    x = x_res[parity][:, t, :]
                    dve.tensor_tensor(x, acc[t][:, :], x, ALU.add).then_inc(res_done, 1)
                need(dve, mv_done, b - 1, TT, TT)
                for t in range(TT):
                    need(dve, res_done, b, TT, t + 1)
                    dve.bn_stats(stats[:, t, :], x_res[parity][:, t, :]).then_inc(st_done, 1)
                for t in range(TT):
                    need_alone(dve, st_done, b, TT, t + 1, made, 5)
                    if t == 0:
                        need(dve, shift_done, b - 1, 1, 1)
                    dve.bn_aggr(mv[:, t, :], stats[:, t, :]).then_inc(mv_done, 1)

            paired(dve, step)

        @block.tensor
        def _(pe):
            pe.wait_ge(made, 5)

            def transpose_x(b, parity, j):
                pe.wait_ge(x_in[parity], (b - parity) * 8 + 16)
                need(pe, xlo_done, b, CC, j - 1)
                for t in range(TT):
                    last = pe.transpose(t_ps[j % 2][:, t * P:t * P + P], x_res[parity][:, t, j * P:j * P + P], ident[:, :])
                last.then_inc(tr_mm, 1)

            for j in range(CC):
                transpose_x(0, 0, j)

            def up(b, parity, f):
                if f == 0:
                    need(pe, xlo_done, b, CC, CC)
                need(pe, whi_done, b, FC, f + 1)
                need(pe, wlo_done, b, FC, f + 1)
                need(pe, h_done, b, FC, f - 1)
                s, n = f % NR, 0
                for j in range(CC):
                    js = slice(j * P, j * P + P)
                    for wx, xx in ((w_hi, xT_hi), (w_hi, xT_lo), (w_lo, xT_hi)):
                        last = pe.matmul(h_ps[f % 2][:, :], wx[:, s, js], xx[parity][:, j, :], start=(n == 0), stop=(n == 3 * CC - 1))
                        n += 1
                last.then_inc(up_mm, 1)

            def down(b, f):
                need(pe, hhi_done, b, FC, f + 1)
                need(pe, hlo_done, b, FC, f + 1)
                s = f % NR
                for t in range(TT):
                    ts = slice(t * P, t * P + P)
                    if f == 0:
                        need(pe, res_done, b - 1, TT, t + 1)
                    for n, (hx, wx) in enumerate(((h_hi, w_hi), (h_hi, w_lo), (h_lo, w_hi))):
                        last = pe.matmul(acc[t][:, :], hx[:, s, ts], wx[:, s, C:], start=(f == 0 and n == 0),
                                         stop=(f == FC - 1 and n == 2))
                    if f == FC - 1 and t < TT - 1:
                        last.then_inc(acc_mm, 1)
                last.then_inc(down_mm, 1)

            def step(b, parity):
                for f in range(FC):
                    up(b, parity, f)
                    if f >= LAG:
                        down(b, f - LAG)
                    if f in TR_AT and inside(b + 1):
                        transpose_x(b + 1, 1 - parity, TR_AT.index(f))
                for f in range(FC - LAG, FC):
                    down(b, f)

            paired(pe, step)


def build(nc, d, out):
    x2_dram = nc.dram_tensor("x2_scratch", [NB, P, TT, C], F32, kind="Internal").ap()
    with ExitStack() as ctx:
        idx = ctx.enter_context(nc.sbuf_tensor("idx", [1, NB], U32))
        x2_stored = ctx.enter_context(nc.semaphore("x2_stored"))
        mixers(nc, d, idx, x2_dram, x2_stored)
        experts(nc, d, idx, x2_dram, out)


def kernel(**inputs):
    import numpy as np
    import concourse.bacc as bacc
    from concourse.bass_utils import run_bass_kernel_spmd

    g = {k: np.asarray(v) for k, v in inputs.items()}

    def tokens(x):
        return x.reshape(NB, TT, P, C).transpose(0, 2, 1, 3)

    def channels(x):
        return x.transpose(0, 2, 1).reshape(NB, CC, P, T).transpose(0, 2, 1, 3)

    def column(v):
        return v.reshape(-1, P).T

    def weights(w):
        return w.T.reshape(CC, P, -1).transpose(1, 0, 2)

    x_names = {n: g[f"L0_xattn_{n}"] for n in
               ("wqg", "bqg", "wkg", "bkg", "wvg", "bvg", "wql", "bql", "wkl", "bkl", "wvl", "bvl", "wp", "bp")}
    w1 = g["L0_ffn_W1"].reshape(NE, CC, P, FC, P).transpose(0, 3, 2, 1, 4).reshape(NE, FC, P, C)
    w2 = g["L0_ffn_W2"].reshape(NE, FC, P, C)
    laid = {
        "xT": channels(g["x"]),
        "x_tok": tokens(g["x"]),
        "ctx_tok": tokens(g["ctx_1024"]),
        "ctxT": channels(g["ctx_1024"]),
        "w_attn": np.concatenate([weights(g["L0_attn_Wqkv"]), weights(g["L0_attn_Wproj"])], axis=2),
        "b_qkv": column(g["L0_attn_bqkv"]),
        "scale": g["L0_attn_scale"].reshape(1, 1),
        "rows": np.stack([x_names[n] for n in ("wkg", "bkg", "wkl", "bkl", "wvg", "bvg", "wvl", "bvl")]
                         + [g["L0_attn_bproj"]]),
        "cols": np.stack([column(x_names[n]) for n in ("wqg", "bqg", "wql", "bql", "wp", "bp")], axis=1),
        "wr": g["L0_ffn_Wr"].reshape(CC, P, NE).transpose(1, 0, 2),
        "br": g["L0_ffn_br"].reshape(1, NE),
        "w12": np.concatenate([w1, w2], axis=3),
        "b1": g["L0_ffn_b1"].reshape(NE, FC, P).transpose(0, 2, 1),
        "b2": g["L0_ffn_b2"],
    }
    nc = bacc.Bacc("TRN2", target_bir_lowering=False, num_devices=1, dynamic_dma_scratch_size=2048)
    arrays, d = {}, {}
    for name, a in laid.items():
        a = np.ascontiguousarray(a)
        arrays[f"in_{name}"] = a
        d[name] = nc.dram_tensor(f"in_{name}", a.shape, mybir.dt.from_np(a.dtype), kind="ExternalInput").ap()
    out = nc.dram_tensor("out_dram", (NB, P, TT, C), F32, kind="ExternalOutput").ap()
    build(nc, d, out)
    r = run_bass_kernel_spmd(nc, [arrays], core_ids=[0])
    got = r.results[0]["out_dram"]
    return got.transpose(0, 2, 1, 3).reshape(NB, T, C)
```

```python
import concourse.bass as bass
from concourse import mybir
from contextlib import ExitStack

F32 = mybir.dt.float32
F32R = mybir.dt.float32r
U32 = mybir.dt.uint32
ALU = mybir.AluOpType
ACT = mybir.ActivationFunctionType
AX = mybir.AxisListType

P = 128
NB = 16
T = 512
C = 512
CC = C // P
TT = T // P
HD = 32
NH = C // HD
XH = 4
DFF = 2048
FC = DFF // P
NE = 8
SEG = P // TT
EPS_DEN = 0.001
EPS_LN = 1e-05
XSCALE = float(C) ** -0.5


def upto(batch, per, n):
    if not isinstance(batch, int):
        return batch * per + n
    return min(batch * per + n, NB * per) if batch * per + n > 0 else None


def staged(eng, body):
    for i in range(3):
        body(i)
    with eng.Fori(3, NB - 1) as i:
        body(i)
    for i in range(NB - 1, NB + 2):
        body(i)


def inside(b):
    return not isinstance(b, int) or 0 <= b < NB


def mixers(nc, d, idx, x2_dram, x2_stored):
    with ExitStack() as ctx:
        def sb(name, shape, dt=F32):
            return ctx.enter_context(nc.sbuf_tensor(name, shape, dt))

        def sem(name):
            return ctx.enter_context(nc.semaphore(name))

        w = {"hi": sb("w_hi", [P, CC, 4 * C], F32R), "lo": sb("w_lo", [P, CC, 4 * C], F32R)}

        rows = sb("rows", [P, 9, C])
        WKG, BKG, WKL, BKL, WVG, BVG, WVL, BVL, BPROJ = range(9)
        cols = sb("cols", [P, 6, XH])
        WQG, BQG, WQL, BQL, WP, BP = range(6)
        b_qkv = sb("b_qkv", [P, 3 * CC])
        sb_qkv = sb("sb_qkv", [P, 3 * CC])
        scale = sb("scale", [P, 1])
        wr = sb("wr", [P, CC, NE])
        br = sb("br", [1, NE])
        ident = sb("ident", [P, P])
        ones = sb("ones", [P, P])
        head_sum = sb("head_sum", [P, CC, SEG])
        head_all = sb("head_all", [P, CC, P])
        half = sb("half", [P, TT])
        ln_eps, minus = sb("ln_eps", [P, TT]), sb("minus", [P, TT])
        nbq = sb("nbq", [P, 2, XH])
        wp2 = sb("wp2", [P, XH])

        xT_raw = sb("xT_raw", [P, CC, T])
        xT_hi = sb("xT_hi", [P, CC, T], F32R)
        xT_lo = sb("xT_lo", [P, CC, T], F32R)
        e_k, r_k = sb("e_k", [P, T]), sb("r_k", [P, T])
        e_q, r_q = sb("e_q", [P, T]), sb("r_q", [P, T])
        k_sum, kv_sum, q = sb("k_sum", [P, T]), sb("kv_sum", [P, T]), sb("q", [P, T])
        qk = sb("qk", [P, CC, T])
        y = sb("y", [P, CC, T])
        y_hi, y_lo = sb("y_hi", [P, CC, T], F32R), sb("y_lo", [P, CC, T], F32R)
        den, rden = sb("den", [P, P]), sb("rden", [P, P])
        rden_all = sb("rden_all", [P, T])
        x_tok = sb("x_tok", [P, TT, C])
        x1 = sb("x1", [P, TT, C])
        ctx_tok, ctx_T = sb("ctx_tok", [P, TT, C]), sb("ctx_T", [P, CC, T])
        x2 = sb("x2", [P, TT, C])
        c_col = sb("c_col", [P, XH])
        diag = sb("diag", [P, XH, P])
        s_x = sb("s_x", [P, XH])
        s_q = sb("s_q", [P, 2, XH])
        s_a = sb("s_a", [P, 2, XH, P])
        neg_max = sb("neg_max", [P, 2, XH])
        neg_scaled = sb("neg_scaled", [P, 2, XH])
        e_sum = sb("e_sum", [P, 2, XH])
        e_rec = sb("e_rec", [P, 2, XH])
        e_rec2 = sb("e_rec2", [P, 2, XH])
        a_v = sb("a_v", [P, 2, XH, P])
        junk_v = sb("junk_v", [P, P])
        k_const = sb("k_const", [P, 2, XH])
        k_all, k_all2 = sb("k_all", [P, XH]), sb("k_all2", [P, XH])
        aT = sb("aT", [P, XH, P])
        const_b = sb("const_b", [P, C])
        x_sum = sb("x_sum", [P, 2, C])
        m_col = sb("m_col", [P, CC])
        logits = sb("logits", [1, NE])
        top = sb("top", [1, NE])
        found = sb("found", [1, NE], U32)
        stats = sb("stats", [P, 2, TT, 6])
        mv = sb("mv", [P, 2, TT, 2])
        var_e, rstd, m_r, shift = (sb(n, [P, 2, TT]) for n in ("var_e", "rstd", "m_r", "shift"))

        bank = [ctx.enter_context(nc.psum_tensor(f"bank{i}", [P, 512], F32)) for i in range(8)]
        K_BANK, V_BANK, Q_BANK, DEN_BANK, G_BANK, C_BANK = bank[0], bank[1], bank[2], bank[3], bank[6], bank[7]
        WIDE = [bank[4], bank[5]]
        den_ps = DEN_BANK[:, 0:P]
        route_ps = DEN_BANK[0:1, 0:NE]
        sx_ps, mean_ps = (WIDE[n][:, :].rearrange("p (h e) -> p h e", h=XH) for n in range(2))
        g_ps = G_BANK[:, :].rearrange("p (h e) -> p h e", h=XH)
        c_ps = C_BANK[:, :].rearrange("p (h e) -> p h e", h=XH)

        w_in = [sem(f"w_in{cc}") for cc in range(CC)]
        w_hi_done, w_lo_done = sem("w_hi_done"), sem("w_lo_done")
        w_raw = [buf[:, :, :].rearrange("p t n -> p (t n)") for buf in (y, qk, x1, x2)]
        consts_in = sem("consts_in")
        made = sem("made")
        preset = sem("preset")
        xT_in, xtok_in, ctx_in, ctxT_in = sem("xT_in"), sem("xtok_in"), sem("ctx_in"), sem("ctxT_in")
        xhi_done, xlo_done = sem("xhi_done"), sem("xlo_done")
        k_mm, v_mm, q_mm = sem("k_mm"), sem("v_mm"), sem("q_mm")
        ek_done, eq_done = sem("ek_done"), sem("eq_done")
        k_done, kv_done, kc_done = sem("k_done"), sem("kv_done"), sem("kc_done")
        kvc_done, q_done, qk_done, num_done = sem("kvc_done"), sem("q_done"), sem("qk_done"), sem("num_done")
        den_mm, den_max, rden_done, rb_mm = sem("den_mm"), sem("den_max"), sem("rden_done"), sem("rb_mm")
        y_done, yhi_done, ylo_done = sem("y_done"), sem("yhi_done"), sem("ylo_done")
        proj_mm, xb_done, res1_done = sem("proj_mm"), sem("xb_done"), sem("res1_done")
        st_done = [sem("st1_done"), sem("st2_done")]
        mv_done = [sem("mv1_done"), sem("mv2_done")]
        ve_done = [sem("ve1_done"), sem("ve2_done")]
        rstd_done = [sem("rstd1_done"), sem("rstd2_done")]
        mr_done = [sem("mr1_done"), sem("mr2_done")]
        shift_done = [sem("shift1_done"), sem("shift2_done")]
        x1_done, x2_done = sem("x1_done"), sem("x2_done")
        g_mm, sx_mm, c_mm = sem("g_mm"), sem("sx_mm"), sem("c_mm")
        csum_done, diag_done, sx_done, sq_done = sem("csum_done"), sem("diag_done"), sem("sx_done"), sem("sq_done")
        sc_done = sem("sc_done")
        max_done, nmax_done = sem("max_done"), sem("nmax_done")
        exp_done = sem("exp_done")
        rec_done, rec2_done = sem("rec_done"), sem("rec2_done")
        av_done = sem("av_done")
        asum_done, kall_done, kall2_done, diag2_done = (sem(n) for n in ("asum_done", "kall_done", "kall2_done", "diag2_done"))
        aT_mm, kb_mm, aT_done, kb_done, x1c_done = (sem(n) for n in ("aT_mm", "kb_mm", "aT_done", "kb_done", "x1c_done"))
        out_mm, res2_done = sem("out_mm"), sem("res2_done")
        mean_mm, mcol_done, route_mm, logit_done, top_done, idx_done = (
            sem(n) for n in ("mean_mm", "mcol_done", "route_mm", "logit_done", "top_done", "idx_done"))
        found_done = sem("found_done")
        xsum_done, x2sum_done = sem("xsum_done"), sem("x2sum_done")
        rall_done = sem("rall_done")

        block = ctx.enter_context(nc.Block())
        N_CONST = 6
        MADE = 11 + 2 * TT

        @block.sync
        def _(sp):
            sp.dma_start(xT_raw[:, :, :], d["xT"][0]).then_inc(xT_in, 16)
            for cc in range(CC):
                sp.dma_start(w_raw[cc], d["w_attn"][:, cc, :]).then_inc(w_in[cc], 16)
            for r in range(9):
                sp.dma_start(rows[:, r, :], d["rows"][r:r + 1, :].broadcast_to([P, C])).then_inc(consts_in, 16)
            sp.dma_start(cols[:, :, :], d["cols"]).then_inc(consts_in, 16)
            sp.dma_start(b_qkv[:, :], d["b_qkv"]).then_inc(consts_in, 16)
            sp.dma_start(scale[:, :], d["scale"].broadcast_to([P, 1])).then_inc(consts_in, 16)
            sp.dma_start(wr[:, :, :], d["wr"]).then_inc(consts_in, 16)
            sp.dma_start(br[:, :], d["br"]).then_inc(consts_in, 16)

            def step(i):
                a, b, c = i, i - 1, i - 2
                if inside(i + 1):
                    if (due := upto(a, 1, 1)) is not None:
                        sp.wait_ge(xhi_done, due)
                    if (due := upto(a, 1, 1)) is not None:
                        sp.wait_ge(xlo_done, due)
                    sp.dma_start(xT_raw[:, :, :], dyn(d["xT"], i + 1)).then_inc(xT_in, 16)
                if inside(b):
                    if (due := upto(c, TT, TT)) is not None:
                        sp.wait_ge(out_mm, due)
                    if (due := upto(c, XH, XH)) is not None:
                        sp.wait_ge(csum_done, due)
                    sp.dma_start(ctx_T[:, :, :], dyn(d["ctxT"], b)).then_inc(ctxT_in, 16)
                if inside(c):
                    if (due := upto(c, TT, TT)) is not None:
                        sp.wait_ge(x2_done, due)
                    sp.dma_start(dyn(x2_dram, c), x2[:, :, :]).then_inc(x2_stored, 16)
                if inside(a):
                    if (due := upto(b, TT, TT)) is not None:
                        sp.wait_ge(x1_done, due)
                    sp.dma_start(x_tok[:, :, :], dyn(d["x_tok"], a)).then_inc(xtok_in, 16)
                if inside(a):
                    if (due := upto(b, 1, 1)) is not None:
                        sp.wait_ge(g_mm, due)
                    sp.dma_start(ctx_tok[:, :, :], dyn(d["ctx_tok"], a)).then_inc(ctx_in, 16)

            staged(sp, step)
            sp.wait_ge(x2_stored, 16 * NB)

        @block.gpsimd
        def _(pool):
            for m, value in ((ident, 0.0), (ones, 1.0), (half, -0.5), (ln_eps, EPS_LN), (minus, -1.0), (rden_all, 0.0)):
                pool.memset(m[:, :], value).then_inc(made, 1)
            pool.memset(head_sum[:, :, :], 1.0).then_inc(made, 1)
            pool.memset(head_all[:, :, :], 1.0).then_inc(made, 1)
            masks = [(ident[:, :], ALU.not_equal, 1.0, 0, [[-1, P]], 1),
                     (head_sum[:, :, :], ALU.is_ge, 0.0, 0, [[P, CC], [-HD, SEG]], 1),
                     (head_sum[:, :, :], ALU.is_ge, 0.0, HD - 1, [[-P, CC], [HD, SEG]], -1)]
            for s in range(TT):
                part = head_all[s * SEG:s * SEG + SEG, :, :]
                masks += [(part, ALU.is_ge, 0.0, 0, [[P, CC], [1, P]], -HD),
                          (part, ALU.is_ge, 0.0, HD - 1, [[-P, CC], [-1, P]], HD)]
            for n, (m, op, fill, base, pattern, step_p) in enumerate(masks):
                pool.wait_ge(made, 8 + n)
                pool.affine_select(out=m, in_=m, compare_op=op, fill=fill, base=base, pattern=pattern,
                                   channel_multiplier=step_p).then_inc(made, 1)
            pool.wait_ge(made, MADE)
            pool.wait_ge(consts_in, 16 * (N_CONST + 8))

            def rstd_of(n, b):
                if (due := upto(b, TT, TT)) is not None:
                    pool.wait_ge(mv_done[n], due)
                if (due := upto(b - 1, TT, TT)) is not None:
                    pool.wait_ge(x1_done if n == 0 else x2_done, due)
                pool.tensor_tensor(var_e[:, n, :], mv[:, n, :, 1], ln_eps[:, :], ALU.add).then_inc(ve_done[n], 1)
                if (due := upto(b, 1, 1)) is not None:
                    pool.wait_ge(ve_done[n], due)
                pool.tensor_tensor(rstd[:, n, :], var_e[:, n, :], half[:, :], ALU.pow).then_inc(rstd_done[n], 1)
                if (due := upto(b, 1, 1)) is not None:
                    pool.wait_ge(rstd_done[n], due)
                pool.tensor_tensor(m_r[:, n, :], mv[:, n, :, 0], rstd[:, n, :], ALU.mult).then_inc(mr_done[n], 1)
                if (due := upto(b, 1, 1)) is not None:
                    pool.wait_ge(mr_done[n], due)
                pool.tensor_tensor(shift[:, n, :], m_r[:, n, :], minus[:, :], ALU.mult).then_inc(shift_done[n], 1)

            def tile_sum(n, b, x, x_done, used, done):
                if (due := upto(b, TT, TT)) is not None:
                    pool.wait_ge(x_done, due)
                if (due := upto(b - 1, 1, 1)) is not None:
                    pool.wait_ge(used, due)
                pool.tensor_tensor(x_sum[:, n, :], x[:, 0, :], x[:, 1, :], ALU.add).then_inc(done, 1)
                for t in range(2, TT):
                    if (due := upto(b, TT - 1, t - 1)) is not None:
                        pool.wait_ge(done, due)
                    pool.tensor_tensor(x_sum[:, n, :], x_sum[:, n, :], x[:, t, :], ALU.add).then_inc(done, 1)

            def step(i):
                b, c = i - 1, i - 2
                if inside(b):
                    if (due := upto(b, 16, 16)) is not None:
                        pool.wait_ge(xtok_in, due)
                    pool.tensor_tensor(x_tok[:, :, :], x_tok[:, :, :],
                                       rows[:, BPROJ:BPROJ + 1, :].broadcast_to([P, TT, C]), ALU.add).then_inc(xb_done, 1)
                if inside(c):
                    if (due := upto(c, 1, 1)) is not None:
                        pool.wait_ge(kall2_done, due)
                    if (due := upto(c, 1, 1)) is not None:
                        pool.wait_ge(c_mm, due)
                    pool.tensor_tensor(diag[:, :, :], ident[:, :].unsqueeze(1).broadcast_to([P, XH, P]),
                                       k_all2[:, :].unsqueeze(2).broadcast_to([P, XH, P]), ALU.mult).then_inc(diag2_done, 1)
                    if (due := upto(c, 1, 1)) is not None:
                        pool.wait_ge(kb_done, due)
                    if (due := upto(c, 1, 1)) is not None:
                        pool.wait_ge(g_mm, due)
                    if (due := upto(c, TT - 1, TT - 1)) is not None:
                        pool.wait_ge(xsum_done, due)
                    pool.tensor_tensor(x1[:, :, :], x1[:, :, :],
                                       const_b[:, :].unsqueeze(1).broadcast_to([P, TT, C]), ALU.add).then_inc(x1c_done, 1)
                if inside(c):
                    rstd_of(1, c)
                if inside(b):
                    if (due := upto(b, XH, XH)) is not None:
                        pool.wait_ge(csum_done, due)
                    if (due := upto(c, 1, 1)) is not None:
                        pool.wait_ge(kb_mm, due)
                    pool.tensor_tensor(diag[:, :, :], ident[:, :].unsqueeze(1).broadcast_to([P, XH, P]),
                                       c_col[:, :].unsqueeze(2).broadcast_to([P, XH, P]), ALU.mult).then_inc(diag_done, 1)
                    rstd_of(0, b)
                if inside(c):
                    tile_sum(1, c, x2, x2_done, mean_mm, x2sum_done)
                if inside(b):
                    tile_sum(0, b, x1, x1_done, sx_mm, xsum_done)

            staged(pool, step)

        @block.scalar
        def _(act):
            for cc in range(CC):
                act.wait_ge(w_in[cc], 16)
                act.activation(w["hi"][:, cc, :], w_raw[cc], ACT.Copy).then_inc(w_hi_done, 1)
            act.wait_ge(preset, 4)

            def features(a, cc, kinds=(0, 1)):
                for n, (mm, e, r, done, used, ps) in enumerate((
                        (k_mm, e_k, r_k, ek_done, k_done, K_BANK), (q_mm, e_q, r_q, eq_done, q_done, Q_BANK))):
                    if n not in kinds:
                        continue
                    col = (1 - n) * CC + cc
                    if (due := upto(a, CC, cc + 1)) is not None:
                        act.wait_ge(mm, due)
                    if (due := upto(a, CC, cc)) is not None:
                        act.wait_ge(used, due)
                    act.activation(e[:, :], ps[:, :], ACT.Exp, bias=sb_qkv[:, col:col + 1],
                                   scale=scale[:, 0:1]).then_inc(done, 1)
                    act.activation(r[:, :], ps[:, :], ACT.Relu, bias=sb_qkv[:, col:col + 1],
                                   scale=scale[:, 0:1]).then_inc(done, 1)

            def split_x(b):
                if (due := upto(b, 16, 16)) is not None:
                    act.wait_ge(xT_in, due)
                if (due := upto(b - 1, CC, CC)) is not None:
                    act.wait_ge(q_mm, due)
                act.activation(xT_hi[:, :, :], xT_raw[:, :, :], ACT.Copy).then_inc(xhi_done, 1)

            def normalise(n, b):
                if (due := upto(b, 1, 1)) is not None:
                    act.wait_ge(shift_done[n], due)
                if n == 0:
                    if (due := upto(b - 1, TT, TT)) is not None:
                        act.wait_ge(res2_done, due)
                src, dst, done = ((x_tok, x1, x1_done), (x2, x2, x2_done))[n]
                for t in range(TT):
                    act.activation(dst[:, t, :], src[:, t, :], ACT.Identity, bias=shift[:, n, t:t + 1],
                                   scale=rstd[:, n, t:t + 1]).then_inc(done, 1)

            split_x(0)

            def exps(c, v):
                if (due := upto(c, 2, v + 1)) is not None:
                    act.wait_ge(nmax_done, due)
                if (due := upto(c - 1, 4 * XH, 4 * XH)) is not None:
                    act.wait_ge(av_done, due)
                for h in range(XH):
                    act.activation(s_a[:, v, h, :], s_a[:, v, h, :], ACT.Exp, bias=neg_scaled[:, v, h:h + 1],
                                   scale=XSCALE, accum_out=e_sum[:, v, h:h + 1]).then_inc(exp_done, 1)

            def step(i):
                a, b, c = i, i - 1, i - 2
                if inside(b):
                    if (due := upto(b, 1, 1)) is not None:
                        act.wait_ge(rden_done, due)
                    if (due := upto(b - 1, CC, CC)) is not None:
                        act.wait_ge(rb_mm, due)
                    if isinstance(b, int):
                        act.wait_ge(made, MADE)
                    for s in range(TT):
                        rows_s = slice(s * SEG, s * SEG + SEG)
                        act.activation(rden_all[rows_s, s * P:s * P + P], rden[rows_s, :], ACT.Copy).then_inc(rall_done, 1)
                if inside(a):
                    features(a, 0, (0,))
                if inside(b):
                    if (due := upto(c, TT, TT)) is not None:
                        act.wait_ge(proj_mm, due)
                    for cc in range(CC):
                        if (due := upto(b, CC, cc + 1)) is not None:
                            act.wait_ge(y_done, due)
                        act.activation(y_hi[:, cc, :], y[:, cc, :], ACT.Copy).then_inc(yhi_done, 1)
                if inside(c):
                    exps(c, 0)
                if inside(a):
                    features(a, 0, (1,))
                if inside(c):
                    exps(c, 1)
                if inside(a):
                    features(a, 1)
                    features(a, 2)
                if inside(c):
                    if (due := upto(c, 1, 1)) is not None:
                        act.wait_ge(aT_mm, due)
                    if (due := upto(c - 1, TT, TT)) is not None:
                        act.wait_ge(out_mm, due)
                    act.activation(aT[:, :, :], g_ps, ACT.Copy).then_inc(aT_done, 1)
                    if (due := upto(c, 1, 1)) is not None:
                        act.wait_ge(kb_mm, due)
                    if (due := upto(b - 1, XH, XH)) is not None:
                        act.wait_ge(csum_done, due)
                    act.activation(const_b[:, :], C_BANK[:, :], ACT.Copy).then_inc(kb_done, 1)
                if inside(b):
                    if (due := upto(b, 16, 16)) is not None:
                        act.wait_ge(ctxT_in, due)
                    if (due := upto(c, 1, 1)) is not None:
                        act.wait_ge(diag_done, due)
                    if (due := upto(c, 1, 1)) is not None:
                        act.wait_ge(x1c_done, due)
                    for h in range(XH):
                        if (due := upto(b, XH, h)) is not None:
                            act.wait_ge(csum_done, due)
                        act.activation(const_b[:, :], ctx_T[:, h, :], ACT.Copy,
                                       accum_out=c_col[:, h:h + 1]).then_inc(csum_done, 1)
                if inside(c):
                    normalise(1, c)
                if inside(a):
                    features(a, 3, (0,))
                if inside(b):
                    normalise(0, b)
                if inside(a):
                    features(a, 3, (1,))
                if inside(i + 1):
                    split_x(i + 1)
                if inside(c):
                    if (due := upto(c, 1, 1)) is not None:
                        act.wait_ge(mean_mm, due)
                    if (due := upto(c - 1, 1, 1)) is not None:
                        act.wait_ge(route_mm, due)
                    act.activation(m_col[:, :], mean_ps[:, :, 0], ACT.Copy, scale=1.0 / T).then_inc(mcol_done, 1)

            staged(act, step)

        @block.vector
        def _(dve):
            dve.wait_ge(consts_in, 16 * (N_CONST + 8))
            dve.tensor_scalar(sb_qkv[:, :], b_qkv[:, :], scale[:, 0:1], None, ALU.mult).then_inc(preset, 1)
            dve.tensor_scalar(nbq[:, 0, :], cols[:, BQG, :], float(T), None, ALU.mult).then_inc(preset, 1)
            dve.tensor_scalar(nbq[:, 1, :], cols[:, BQL, :], float(T), None, ALU.mult).then_inc(preset, 1)
            dve.tensor_scalar(wp2[:, :], cols[:, WP, :], 2.0, None, ALU.mult).then_inc(preset, 1)
            dve.wait_ge(preset, 4)
            for cc in range(CC):
                dve.wait_ge(w_hi_done, cc + 1)
                dve.tensor_tensor(w["lo"][:, cc, :], w_raw[cc], w["hi"][:, cc, :].bitcast(F32),
                                  ALU.subtract).then_inc(w_lo_done, 1)
            dve.wait_ge(w_lo_done, CC)

            def keys(a, cc):
                if (due := upto(a, 2 * CC, 2 * cc + 2)) is not None:
                    dve.wait_ge(ek_done, due)
                if (due := upto(a, CC, cc)) is not None:
                    dve.wait_ge(qk_done, due)
                dve.scalar_tensor_tensor(k_sum[:, :], e_k[:, :], 1.0, r_k[:, :], ALU.min, ALU.add).then_inc(k_done, 1)

            def values(a, cc):
                if (due := upto(a, CC, cc + 1)) is not None:
                    dve.wait_ge(v_mm, due)
                if (due := upto(a, CC, cc + 1)) is not None:
                    dve.wait_ge(k_done, due)
                if (due := upto(a, CC, cc)) is not None:
                    dve.wait_ge(num_done, due)
                dve.scalar_tensor_tensor(kv_sum[:, :], V_BANK[:, :], b_qkv[:, 2 * CC + cc:2 * CC + cc + 1],
                                         k_sum[:, :], ALU.add, ALU.mult).then_inc(kv_done, 1)
                if (due := upto(a, CC, cc + 1)) is not None:
                    dve.wait_ge(kv_done, due)
                dve.tensor_tensor_scan(k_sum[:, :], k_sum[:, :], k_sum[:, :], 0.0, ALU.add, ALU.bypass).then_inc(kc_done, 1)
                dve.tensor_tensor_scan(kv_sum[:, :], kv_sum[:, :], kv_sum[:, :], 0.0, ALU.add, ALU.bypass).then_inc(kvc_done, 1)

            def queries(a, cc):
                if (due := upto(a, 2 * CC, 2 * cc + 2)) is not None:
                    dve.wait_ge(eq_done, due)
                dve.scalar_tensor_tensor(q[:, :], e_q[:, :], 1.0, r_q[:, :], ALU.min, ALU.add).then_inc(q_done, 1)
                if (due := upto(a, CC, cc + 1)) is not None:
                    dve.wait_ge(q_done, due)
                if (due := upto(a, CC, cc + 1)) is not None:
                    dve.wait_ge(kc_done, due)
                if (due := upto(a - 1, 1, 1)) is not None:
                    dve.wait_ge(den_mm, due)
                dve.tensor_tensor(qk[:, cc, :], q[:, :], k_sum[:, :], ALU.mult).then_inc(qk_done, 1)

            def numerator(a, cc):
                if (due := upto(a, CC, cc + 1)) is not None:
                    dve.wait_ge(q_done, due)
                if (due := upto(a, CC, cc + 1)) is not None:
                    dve.wait_ge(kvc_done, due)
                if (due := upto(a - 1, CC, CC)) is not None:
                    dve.wait_ge(ylo_done, due)
                dve.tensor_tensor(y[:, cc, :], q[:, :], kv_sum[:, :], ALU.mult).then_inc(num_done, 1)

            def residual(n, b, t):
                mm, res, done, src, dst = ((proj_mm, x_tok, res1_done, x_tok, x_tok),
                                           (out_mm, x1, res2_done, x1, x2))[n]
                if (due := upto(b, TT, t + 1)) is not None:
                    dve.wait_ge(mm, due)
                if n == 0:
                    if (due := upto(b, 1, 1)) is not None:
                        dve.wait_ge(xb_done, due)
                else:
                    if (due := upto(b, 1, 1)) is not None:
                        dve.wait_ge(x1c_done, due)
                    if (due := upto(b - 1, TT - 1, TT - 1)) is not None:
                        dve.wait_ge(x2sum_done, due)
                    if (due := upto(b - 1, 16, 16)) is not None:
                        dve.wait_ge(x2_stored, due)
                ps = WIDE[t % 2]
                dve.tensor_tensor(dst[:, t, :], ps[:, :], src[:, t, :], ALU.add).then_inc(done, 1)

            def statistics(n, b, tiles):
                done = (res1_done, res2_done)[n]
                x = (x_tok, x2)[n]
                for t in tiles:
                    if (due := upto(b, TT, t + 1)) is not None:
                        dve.wait_ge(done, due)
                    if (due := upto(b - 1, TT, TT)) is not None:
                        dve.wait_ge(mv_done[n], due)
                    dve.bn_stats(stats[:, n, t, :], x[:, t, :]).then_inc(st_done[n], 1)

            def moments(n, b):
                for t in range(TT):
                    dve.wait_ge(preset, 4)
                    if (due := upto(b, TT, t + 1)) is not None:
                        dve.wait_ge(st_done[n], due)
                    if t == 0:
                        if (due := upto(b - 1, 1, 1)) is not None:
                            dve.wait_ge(shift_done[n], due)
                    dve.bn_aggr(mv[:, n, t, :], stats[:, n, t, :]).then_inc(mv_done[n], 1)

            def token_sums(c):
                if (due := upto(c, 1, 1)) is not None:
                    dve.wait_ge(sx_mm, due)
                dve.tensor_copy(s_x[:, :], sx_ps[:, :, 0]).then_inc(sx_done, 1)
                if (due := upto(c, 1, 1)) is not None:
                    dve.wait_ge(sx_done, due)
                dve.tensor_tensor(s_q[:, 0, :], s_x[:, :], cols[:, WQG, :], ALU.mult).then_inc(sq_done, 1)
                dve.tensor_tensor(s_q[:, 1, :], s_x[:, :], cols[:, WQL, :], ALU.mult).then_inc(sq_done, 1)
                if (due := upto(c, 3, 2)) is not None:
                    dve.wait_ge(sq_done, due)
                dve.tensor_tensor(s_q[:, :, :], s_q[:, :, :], nbq[:, :, :], ALU.add).then_inc(sq_done, 1)

            def scores(c, part):
                wq, bq = (WQG, WQL), (BQG, BQL)
                wk, bk = (WKG, WKL), (BKG, BKL)

                def row(n):
                    return rows[:, n, :].rearrange("p (h e) -> p h e", h=XH)

                if part == 0:
                    scores_inner(c, wq, bq)
                elif part == 1:
                    scores_outer(c, wk, bk, row)
                else:
                    scores_max(c)

            def scores_inner(c, wq, bq):
                if (due := upto(c, 1, 1)) is not None:
                    dve.wait_ge(g_mm, due)
                if (due := upto(c, 1, 1)) is not None:
                    dve.wait_ge(c_mm, due)
                if (due := upto(c - 1, 4 * XH, 4 * XH)) is not None:
                    dve.wait_ge(av_done, due)
                for v in range(2):
                    dve.tensor_tensor(s_a[:, v, :, :], g_ps, cols[:, wq[v], :].unsqueeze(2).broadcast_to([P, XH, P]),
                                      ALU.mult).then_inc(sc_done, 1)
                    dve.tensor_tensor(a_v[:, v, :, :], c_ps, cols[:, bq[v], :].unsqueeze(2).broadcast_to([P, XH, P]),
                                      ALU.mult).then_inc(sc_done, 1)
                if (due := upto(c, 12, 4)) is not None:
                    dve.wait_ge(sc_done, due)
                for v in range(2):
                    dve.tensor_tensor(s_a[:, v, :, :], s_a[:, v, :, :], a_v[:, v, :, :], ALU.add).then_inc(sc_done, 1)

            def scores_outer(c, wk, bk, row):
                if (due := upto(c, 12, 6)) is not None:
                    dve.wait_ge(sc_done, due)
                if (due := upto(c, 3, 3)) is not None:
                    dve.wait_ge(sq_done, due)
                for v in range(2):
                    dve.tensor_tensor(s_a[:, v, :, :], s_a[:, v, :, :], row(wk[v]), ALU.mult).then_inc(sc_done, 1)
                    dve.tensor_tensor(a_v[:, v, :, :], row(bk[v]), s_q[:, v, :].unsqueeze(2).broadcast_to([P, XH, P]),
                                      ALU.mult).then_inc(sc_done, 1)

            def scores_max(c):
                if (due := upto(c, 12, 10)) is not None:
                    dve.wait_ge(sc_done, due)
                for v in range(2):
                    dve.tensor_tensor(s_a[:, v, :, :], s_a[:, v, :, :], a_v[:, v, :, :], ALU.add).then_inc(sc_done, 1)
                for v in range(2):
                    if (due := upto(c, 12, 11 + v)) is not None:
                        dve.wait_ge(sc_done, due)
                    dve.reduce_max(neg_max[:, v, :], s_a[:, v, :, :], AX.X).then_inc(max_done, 1)
                for v in range(2):
                    if (due := upto(c, 2, v + 1)) is not None:
                        dve.wait_ge(max_done, due)
                    dve.tensor_scalar(neg_scaled[:, v, :], neg_max[:, v, :], -XSCALE, None, ALU.mult).then_inc(nmax_done, 1)

            def weigh(c, v):
                pairs = ((WVG, BVG), (WVL, BVL))
                if (due := upto(c, 2 * XH, (v + 1) * XH)) is not None:
                    dve.wait_ge(exp_done, due)
                dve.reciprocal(e_rec[:, v, :], e_sum[:, v, :]).then_inc(rec_done, 1)
                if (due := upto(c, 2, v + 1)) is not None:
                    dve.wait_ge(rec_done, due)
                dve.tensor_tensor(e_rec2[:, v, :], e_rec[:, v, :], wp2[:, :], ALU.mult).then_inc(rec2_done, 1)
                if (due := upto(c, 2, v + 1)) is not None:
                    dve.wait_ge(rec2_done, due)
                if (due := upto(c - 1, 1, 1)) is not None:
                    dve.wait_ge(kall_done, due)
                wv, bv = pairs[v]
                for h in range(XH):
                    n = 2 * (v * XH + h)
                    hs = slice(h * P, h * P + P)
                    if (due := upto(c, 4 * XH, n)) is not None:
                        dve.wait_ge(av_done, due)
                    dve.scalar_tensor_tensor(junk_v[:, :], s_a[:, v, h, :], e_rec2[:, v, h:h + 1], rows[:, bv, hs],
                                             ALU.mult, ALU.mult, accum_out=k_const[:, v, h:h + 1]).then_inc(av_done, 1)
                    dve.scalar_tensor_tensor(a_v[:, v, h, :], s_a[:, v, h, :], e_rec2[:, v, h:h + 1], rows[:, wv, hs],
                                             ALU.mult, ALU.mult).then_inc(av_done, 1)
                if v == 0:
                    return
                if (due := upto(c, 4 * XH, 4 * XH)) is not None:
                    dve.wait_ge(av_done, due)
                dve.tensor_tensor(k_all[:, :], k_const[:, 0, :], k_const[:, 1, :], ALU.add).then_inc(kall_done, 1)
                dve.tensor_tensor(a_v[:, 0, :, :], a_v[:, 0, :, :], a_v[:, 1, :, :], ALU.add).then_inc(asum_done, 1)
                if (due := upto(c, 1, 1)) is not None:
                    dve.wait_ge(kall_done, due)
                if (due := upto(c - 1, 1, 1)) is not None:
                    dve.wait_ge(diag2_done, due)
                dve.tensor_tensor(k_all2[:, :], k_all[:, :], cols[:, BP, :], ALU.add).then_inc(kall2_done, 1)

            def choose(c):
                if (due := upto(c, 1, 1)) is not None:
                    dve.wait_ge(route_mm, due)
                dve.tensor_tensor(logits[:, :], route_ps, br[:, :], ALU.add).then_inc(logit_done, 1)
                dve.wait_ge(preset, 4)
                if (due := upto(c, 1, 1)) is not None:
                    dve.wait_ge(logit_done, due)
                dve.max(top[:, :], logits[:, :]).then_inc(top_done, 1)
                dve.wait_ge(preset, 4)
                if (due := upto(c, 1, 1)) is not None:
                    dve.wait_ge(top_done, due)
                dve.max_index(found[:, :], top[:, :], logits[:, :]).then_inc(found_done, 1)
                if (due := upto(c, 1, 1)) is not None:
                    dve.wait_ge(found_done, due)
                dve.tensor_copy(idx[0:1, c:c + 1] if isinstance(c, int) else idx[0:1, bass.ds(c, 1)],
                                found[:, 0:1]).then_inc(idx_done, 1)

            def split_x(b):
                if (due := upto(b, 1, 1)) is not None:
                    dve.wait_ge(xhi_done, due)
                if (due := upto(b - 1, CC, CC)) is not None:
                    dve.wait_ge(q_mm, due)
                dve.tensor_tensor(xT_lo[:, :, :], xT_raw[:, :, :], xT_hi[:, :, :].bitcast(F32), ALU.subtract).then_inc(xlo_done, 1)

            split_x(0)

            def times_reciprocal(b, cc):
                if (due := upto(b, CC, cc + 1)) is not None:
                    dve.wait_ge(rb_mm, due)
                if (due := upto(b, CC, cc + 1)) is not None:
                    dve.wait_ge(num_done, due)
                dve.tensor_tensor(y[:, cc, :], y[:, cc, :], WIDE[cc % 2][:, :], ALU.mult).then_inc(y_done, 1)

            def step(i):
                a, b, c = i, i - 1, i - 2
                if inside(c):
                    token_sums(c)
                    scores(c, 0)
                if inside(b):
                    if (due := upto(b, 1, 1)) is not None:
                        dve.wait_ge(den_mm, due)
                    if (due := upto(b - 1, TT, TT)) is not None:
                        dve.wait_ge(rall_done, due)
                    dve.tensor_scalar(den[:, :], den_ps, EPS_DEN, None, ALU.max).then_inc(den_max, 1)
                    if (due := upto(b, 1, 1)) is not None:
                        dve.wait_ge(den_max, due)
                    dve.reciprocal(rden[:, :], den[:, :]).then_inc(rden_done, 1)
                if inside(c):
                    scores(c, 1)
                if inside(b):
                    times_reciprocal(b, 0)
                    times_reciprocal(b, 1)
                if inside(a):
                    keys(a, 0)
                if inside(b):
                    times_reciprocal(b, 2)
                    times_reciprocal(b, 3)
                if inside(c):
                    scores(c, 2)
                if inside(a):
                    values(a, 0)
                if inside(b):
                    for cc in range(CC):
                        if (due := upto(b, CC, cc + 1)) is not None:
                            dve.wait_ge(yhi_done, due)
                        if (due := upto(b - 1, TT, TT)) is not None:
                            dve.wait_ge(proj_mm, due)
                        dve.tensor_tensor(y_lo[:, cc, :], y[:, cc, :], y_hi[:, cc, :].bitcast(F32), ALU.subtract).then_inc(ylo_done, 1)
                if inside(a):
                    queries(a, 0)
                    numerator(a, 0)
                    keys(a, 1)
                    values(a, 1)
                if inside(c):
                    weigh(c, 0)
                if inside(a):
                    queries(a, 1)
                    numerator(a, 1)
                if inside(c):
                    weigh(c, 1)
                if inside(a):
                    keys(a, 2)
                    values(a, 2)
                    queries(a, 2)
                    numerator(a, 2)
                if inside(b):
                    residual(0, b, 0)
                    residual(0, b, 1)
                    statistics(0, b, (0, 1))
                if inside(c):
                    for t in range(TT):
                        residual(1, c, t)
                    statistics(1, c, range(TT))
                    moments(1, c)
                if inside(b):
                    residual(0, b, 2)
                    residual(0, b, 3)
                    statistics(0, b, (2, 3))
                    moments(0, b)
                if inside(a):
                    keys(a, 3)
                    values(a, 3)
                    queries(a, 3)
                    numerator(a, 3)
                if inside(i + 1):
                    split_x(i + 1)
                if inside(c):
                    choose(c)

            staged(dve, step)

        @block.tensor
        def _(pe):
            pe.wait_ge(made, MADE)
            pe.wait_ge(w_lo_done, CC)
            pe.wait_ge(consts_in, 16 * (N_CONST + 8))

            def product(out, pairs, done):
                n = 0
                for (ah, al), (bh, bl) in pairs:
                    for lhsT, rhs in ((ah, bh), (ah, bl), (al, bh)):
                        last = pe.matmul(out, lhsT, rhs, start=(n == 0), stop=(n == 3 * len(pairs) - 1))
                        n += 1
                last.then_inc(done, 1)

            PARTS = {"k": (1, K_BANK, k_mm, ek_done, 2), "v": (2, V_BANK, v_mm, kv_done, 1), "q": (0, Q_BANK, q_mm, eq_done, 2)}

            def qkv(a, cc, which):
                part, ps, done, free, per = PARTS[which]
                if cc == 0:
                    if (due := upto(a, 1, 1)) is not None:
                        pe.wait_ge(xhi_done, due)
                    if (due := upto(a, 1, 1)) is not None:
                        pe.wait_ge(xlo_done, due)
                if (due := upto(a, per * CC, per * cc)) is not None:
                    pe.wait_ge(free, due)
                es = slice(part * C + cc * P, part * C + cc * P + P)
                product(ps[:, :], [((w["hi"][:, j, es], w["lo"][:, j, es]), (xT_hi[:, j, :], xT_lo[:, j, :]))
                                   for j in range(CC)], done)

            def project(b, t):
                ts = slice(t * P, t * P + P)
                product(WIDE[t % 2][:, :], [((y_hi[:, j, ts], y_lo[:, j, ts]), (w["hi"][:, j, 3 * C:], w["lo"][:, j, 3 * C:]))
                                            for j in range(CC)], proj_mm)

            def step(i):
                a, b, c = i, i - 1, i - 2
                if inside(b):
                    if (due := upto(b, CC, CC)) is not None:
                        pe.wait_ge(qk_done, due)
                    if (due := upto(b - 2, 1, 1)) is not None:
                        pe.wait_ge(logit_done, due)
                    for s in range(TT):
                        for cc in range(CC):
                            last = pe.matmul(DEN_BANK[s * SEG:s * SEG + SEG, 0:P], head_sum[:, cc, :], qk[:, cc, s * P:s * P + P],
                                             start=(cc == 0), stop=(cc == CC - 1))
                    last.then_inc(den_mm, 1)
                if inside(a):
                    qkv(a, 0, "k")
                if inside(b):
                    if (due := upto(b, TT, TT)) is not None:
                        pe.wait_ge(rall_done, due)
                    for cc in range(CC):
                        if cc == 0:
                            if (due := upto(b - 1, 1, 1)) is not None:
                                pe.wait_ge(sx_done, due)
                        elif cc == 1:
                            if (due := upto(b - 2, 1, 1)) is not None:
                                pe.wait_ge(mcol_done, due)
                        else:
                            if (due := upto(b, CC, cc - 1)) is not None:
                                pe.wait_ge(y_done, due)
                        pe.matmul(WIDE[cc % 2][:, :], head_all[:, cc, :], rden_all[:, :], start=True, stop=True).then_inc(rb_mm, 1)
                if inside(a):
                    qkv(a, 0, "v")
                    qkv(a, 0, "q")
                    for cc in (1, 2):
                        for which in "kvq":
                            qkv(a, cc, which)
                if inside(c):
                    if (due := upto(c, 1, 1)) is not None:
                        pe.wait_ge(asum_done, due)
                    for h in range(XH):
                        last = pe.transpose(G_BANK[:, h * P:h * P + P], a_v[:, 0, h, :], ident[:, :])
                    last.then_inc(aT_mm, 1)
                    if (due := upto(c, 1, 1)) is not None:
                        pe.wait_ge(diag2_done, due)
                    pe.matmul(c_ps, ones[:, :], diag[:, :, :], start=True, stop=True).then_inc(kb_mm, 1)
                if inside(b):
                    if (due := upto(b, CC, CC)) is not None:
                        pe.wait_ge(yhi_done, due)
                    if (due := upto(b, CC, CC)) is not None:
                        pe.wait_ge(ylo_done, due)
                    if (due := upto(b, CC, CC)) is not None:
                        pe.wait_ge(y_done, due)
                    project(b, 0)
                    project(b, 1)
                if inside(c):
                    if (due := upto(c, 1, 1)) is not None:
                        pe.wait_ge(aT_done, due)
                    if (due := upto(c, 16, 16)) is not None:
                        pe.wait_ge(ctxT_in, due)
                    for t in range(TT):
                        if t < 2:
                            if (due := upto(b, TT, t + 1)) is not None:
                                pe.wait_ge(res1_done, due)
                        else:
                            if (due := upto(c, TT, t - 1)) is not None:
                                pe.wait_ge(res2_done, due)
                        for h in range(XH):
                            last = pe.matmul(WIDE[t % 2][:, h * P:h * P + P], ctx_T[:, h, t * P:t * P + P], aT[:, h, :],
                                             start=True, stop=True)
                        last.then_inc(out_mm, 1)
                if inside(b):
                    for t in (2, 3):
                        if (due := upto(b, TT, t - 1)) is not None:
                            pe.wait_ge(res1_done, due)
                        if (due := upto(c, TT, t + 1)) is not None:
                            pe.wait_ge(res2_done, due)
                        project(b, t)
                if inside(a):
                    for which in "kvq":
                        qkv(a, 3, which)
                if inside(b):
                    if (due := upto(b, TT, TT)) is not None:
                        pe.wait_ge(x1_done, due)
                    if (due := upto(b, 16, 16)) is not None:
                        pe.wait_ge(ctx_in, due)
                    if (due := upto(c, 1, 1)) is not None:
                        pe.wait_ge(aT_done, due)
                    for h in range(XH):
                        hs = slice(h * P, h * P + P)
                        for t in range(TT):
                            last = pe.matmul(g_ps[:, h, :], x1[:, t, hs], ctx_tok[:, t, hs], start=(t == 0), stop=(t == TT - 1))
                    last.then_inc(g_mm, 1)
                    if (due := upto(b, 1, 1)) is not None:
                        pe.wait_ge(diag_done, due)
                    if (due := upto(c, 1, 1)) is not None:
                        pe.wait_ge(kb_done, due)
                    pe.matmul(c_ps, ones[:, :], diag[:, :, :], start=True, stop=True).then_inc(c_mm, 1)
                if inside(c):
                    if (due := upto(c, TT - 1, TT - 1)) is not None:
                        pe.wait_ge(x2sum_done, due)
                    if (due := upto(b, TT, TT)) is not None:
                        pe.wait_ge(res1_done, due)
                    if (due := upto(c, TT, TT)) is not None:
                        pe.wait_ge(res2_done, due)
                    for j in range(CC):
                        last = pe.matmul(mean_ps[:, j, :], x_sum[:, 1, j * P:j * P + P], ones[:, :], start=True, stop=True)
                    last.then_inc(mean_mm, 1)
                if inside(b):
                    if (due := upto(b, TT - 1, TT - 1)) is not None:
                        pe.wait_ge(xsum_done, due)
                    if (due := upto(b, TT, TT)) is not None:
                        pe.wait_ge(res1_done, due)
                    for h in range(XH):
                        last = pe.matmul(sx_ps[:, h, :], x_sum[:, 0, h * P:h * P + P], ones[:, :], start=True, stop=True)
                    last.then_inc(sx_mm, 1)
                if inside(c):
                    if (due := upto(c, 1, 1)) is not None:
                        pe.wait_ge(mcol_done, due)
                    if (due := upto(b, 1, 1)) is not None:
                        pe.wait_ge(den_max, due)
                    for j in range(CC):
                        last = pe.matmul(route_ps, m_col[:, j:j + 1], wr[:, j, :], start=(j == 0), stop=(j == CC - 1))
                    last.then_inc(route_mm, 1)

            staged(pe, step)


def dyn(ap, b):
    return ap[b] if isinstance(b, int) else ap[bass.ds(b, 1)].rearrange("a p t n -> p (a t) n")


def experts(nc, d, idx, x2_dram, out):
    with ExitStack() as ctx:
        def sb(name, shape, dt=F32):
            return ctx.enter_context(nc.sbuf_tensor(name, shape, dt))

        def sem(name):
            return ctx.enter_context(nc.semaphore(name))

        NR = 4
        NW = 8
        AHEAD = 4
        LAG = 2
        raw = sb("raw", [P, NR, 2 * C])
        w_hi, w_lo = sb("we_hi", [P, NW, 2 * C], F32R), sb("we_lo", [P, NW, 2 * C], F32R)
        x_res = [sb(f"x_res{i}", [P, TT, C]) for i in range(2)]
        xT_hi = [sb(f"x2T_hi{i}", [P, CC, T], F32R) for i in range(2)]
        xT_lo = [sb(f"x2T_lo{i}", [P, CC, T], F32R) for i in range(2)]
        hid = sb("hid", [P, 2, T])
        h_hi, h_lo = sb("h_hi", [P, NR, T], F32R), sb("h_lo", [P, NR, T], F32R)
        b1 = sb("b1", [P, 2, FC])
        b2 = sb("b2", [P, 2, C])
        ident = sb("ident_e", [P, P])
        half, ln_eps, minus = (sb(n, [P, TT]) for n in ("half_e", "ln_eps_e", "minus_e"))
        stats, mv = sb("stats_e", [P, TT, 6]), sb("mv_e", [P, TT, 2])
        var_e, rstd, m_r, shift = (sb(n, [P, TT]) for n in ("var_f", "rstd_f", "m_r_f", "shift_f"))
        acc = [ctx.enter_context(nc.psum_tensor(f"acc{t}", [P, C], F32)) for t in range(TT)]
        h_ps = [ctx.enter_context(nc.psum_tensor(f"h_ps{i}", [P, T], F32)) for i in range(2)]
        t_ps = [ctx.enter_context(nc.psum_tensor(f"t_ps{i}", [P, T], F32)) for i in range(2)]

        made = sem("made_e")
        w_in = [sem(f"we_in{s}") for s in range(NR)]
        b_in = [sem("b_in0"), sem("b_in1")]
        x_in = [sem("x2_in0"), sem("x2_in1")]
        whi_done, wlo_done = sem("whi_done"), sem("wlo_done")
        up_mm, down_mm = sem("up_mm"), sem("down_mm")
        h_done, hhi_done, hlo_done = sem("h_done"), sem("hhi_done"), sem("hlo_done")
        tr_mm, xhi_done, xlo_done = sem("tr_mm"), sem("x2hi_done"), sem("x2lo_done")
        xb_done, acc_mm = sem("x2b_done"), sem("acc_mm")
        res_done, st_done, mv_done = sem("res_done"), sem("st_done"), sem("mv_done")
        ve_done, rstd_done, mr_done, shift_done = (sem(n) for n in ("ve_done", "rstd_done", "mr_done", "shift_done"))
        norm_done = sem("norm_done")
        stored = sem("stored")
        block = ctx.enter_context(nc.Block())
        TR_AT = (10, 11, 12, 13)

        def paired(eng, body):
            for b in range(2):
                body(b, b % 2)
            with eng.Fori(1, NB // 2 - 1) as pair:
                for parity in range(2):
                    body(pair * 2 + parity, parity)
            for b in range(NB - 2, NB):
                body(b, b % 2)

        def b_wait(eng, b, parity):
            eng.wait_ge(b_in[parity], (b - parity) * 16 + 32)

        def w_wait(eng, b, f):
            if isinstance(b, int) and f >= FC:
                b, f = b + 1, f - FC
            eng.wait_ge(w_in[f % NR], b * (16 * FC // NR) + 16 * (f // NR + 1))

        def after_last(b, f):
            return isinstance(b, int) and b * FC + f >= NB * FC

        @block.sync
        def _(sp):
            sp.dma_start(x_res[0][:, :, :], x2_dram[0]).then_inc(x_in[0], 16)

            def step(b, parity):
                e = sp.value_load(idx[0:1, bass.ds(b, 1)], min_val=0, max_val=NE - 1)
                if (due := upto(b - 2, FC, FC)) is not None:
                    sp.wait_ge(h_done, due)
                sp.dma_start(b1[:, parity, :], d["b1"][bass.ds(e, 1)].rearrange("a p f -> p (a f)")).then_inc(b_in[parity], 16)
                if (due := upto(b - 2, 1, 1)) is not None:
                    sp.wait_ge(xb_done, due)
                sp.dma_start(b2[:, parity, :], d["b2"][bass.ds(e, 1), :].broadcast_to([P, C])).then_inc(b_in[parity], 16)
                for f in range(FC):
                    if (due := upto(b, FC, f - NR + 1)) is not None:
                        sp.wait_ge(wlo_done, due)
                    sp.dma_start(raw[:, f % NR, :],
                                 d["w12"][bass.ds(e, 1), f].rearrange("a p n -> p (a n)")).then_inc(w_in[f % NR], 16)
                    if f == 9:
                        if inside(b - 1):
                            if (due := upto(b - 1, TT, TT)) is not None:
                                sp.wait_ge(norm_done, due)
                            sp.dma_start(dyn(out, b - 1), x_res[1 - parity][:, :, :]).then_inc(stored, 16)
                    if f == 10:
                        if inside(b + 1):
                            if (due := upto(b - 1, 16, 16)) is not None:
                                sp.wait_ge(stored, due)
                            sp.dma_start(x_res[1 - parity][:, :, :], dyn(x2_dram, b + 1)).then_inc(x_in[1 - parity], 16)

            paired(sp, step)
            sp.wait_ge(norm_done, NB * TT)
            sp.dma_start(out[NB - 1], x_res[1][:, :, :]).then_inc(stored, 16)
            sp.wait_ge(stored, 16 * NB)

        @block.gpsimd
        def _(pool):
            pool.memset(ident[:, :], 0.0).then_inc(made, 1)
            pool.memset(half[:, :], -0.5).then_inc(made, 1)
            pool.memset(ln_eps[:, :], EPS_LN).then_inc(made, 1)
            pool.memset(minus[:, :], -1.0).then_inc(made, 1)
            pool.wait_ge(made, 4)
            pool.affine_select(out=ident[:, :], in_=ident[:, :], compare_op=ALU.not_equal, fill=1.0, base=0,
                               pattern=[[-1, P]], channel_multiplier=1).then_inc(made, 1)

            def step(b, parity):
                if (due := upto(b, CC, CC)) is not None:
                    pool.wait_ge(tr_mm, due)
                b_wait(pool, b, parity)
                pool.tensor_tensor(x_res[parity][:, :, :], x_res[parity][:, :, :],
                                   b2[:, parity:parity + 1, :].broadcast_to([P, TT, C]), ALU.add).then_inc(xb_done, 1)
                if (due := upto(b, TT, TT)) is not None:
                    pool.wait_ge(mv_done, due)
                if (due := upto(b - 1, TT, TT)) is not None:
                    pool.wait_ge(norm_done, due)
                pool.tensor_tensor(var_e[:, :], mv[:, :, 1], ln_eps[:, :], ALU.add).then_inc(ve_done, 1)
                if (due := upto(b, 1, 1)) is not None:
                    pool.wait_ge(ve_done, due)
                pool.tensor_tensor(rstd[:, :], var_e[:, :], half[:, :], ALU.pow).then_inc(rstd_done, 1)
                if (due := upto(b, 1, 1)) is not None:
                    pool.wait_ge(rstd_done, due)
                pool.tensor_tensor(m_r[:, :], mv[:, :, 0], rstd[:, :], ALU.mult).then_inc(mr_done, 1)
                if (due := upto(b, 1, 1)) is not None:
                    pool.wait_ge(mr_done, due)
                pool.tensor_tensor(shift[:, :], m_r[:, :], minus[:, :], ALU.mult).then_inc(shift_done, 1)

            paired(pool, step)

        @block.scalar
        def _(act):
            def split_w(b, f):
                if after_last(b, f):
                    return
                w_wait(act, b, f)
                if (due := upto(b, FC, f - NW + 1)) is not None:
                    act.wait_ge(down_mm, due)
                act.activation(w_hi[:, f % NW, :], raw[:, f % NR, :], ACT.Copy).then_inc(whi_done, 1)

            def split_x(b, parity, j):
                if (due := upto(b, CC, j + 1)) is not None:
                    act.wait_ge(tr_mm, due)
                if (due := upto(b - 2, FC, FC)) is not None:
                    act.wait_ge(up_mm, due)
                act.activation(xT_hi[parity][:, j, :], t_ps[j % 2][:, :], ACT.Copy).then_inc(xhi_done, 1)

            for j in range(CC):
                split_x(0, 0, j)
            for f in range(AHEAD):
                split_w(0, f)

            def step(b, parity):
                for f in range(FC):
                    if (due := upto(b, FC, f + 1)) is not None:
                        act.wait_ge(up_mm, due)
                    if f == 0:
                        b_wait(act, b, parity)
                    if (due := upto(b, FC, f - 1)) is not None:
                        act.wait_ge(hlo_done, due)
                    act.activation(hid[:, f % 2, :], h_ps[f % 2][:, :], ACT.Relu, bias=b1[:, parity, f:f + 1]).then_inc(h_done, 1)
                    split_w(b, f + AHEAD)
                    if f in TR_AT and inside(b + 1):
                        split_x(b + 1, 1 - parity, TR_AT.index(f))
                    if f == 5:
                        finish(b - 1, 1 - parity)

            def finish(b, parity):
                if not inside(b):
                    return
                if (due := upto(b, 1, 1)) is not None:
                    act.wait_ge(shift_done, due)
                for t in range(TT):
                    act.activation(x_res[parity][:, t, :], x_res[parity][:, t, :], ACT.Identity,
                                   bias=shift[:, t:t + 1], scale=rstd[:, t:t + 1]).then_inc(norm_done, 1)

            paired(act, step)
            finish(NB - 1, 1)

        @block.vector
        def _(dve):
            def split_w(b, f):
                if after_last(b, f):
                    return
                if (due := upto(b, FC, f + 1)) is not None:
                    dve.wait_ge(whi_done, due)
                if (due := upto(b, FC, f - NW + 1)) is not None:
                    dve.wait_ge(down_mm, due)
                dve.tensor_tensor(w_lo[:, f % NW, :], raw[:, f % NR, :], w_hi[:, f % NW, :].bitcast(F32), ALU.subtract).then_inc(wlo_done, 1)

            def split_x(b, parity, j):
                if (due := upto(b, CC, j + 1)) is not None:
                    dve.wait_ge(xhi_done, due)
                if (due := upto(b - 2, FC, FC)) is not None:
                    dve.wait_ge(up_mm, due)
                dve.tensor_tensor(xT_lo[parity][:, j, :], t_ps[j % 2][:, :], xT_hi[parity][:, j, :].bitcast(F32),
                                  ALU.subtract).then_inc(xlo_done, 1)

            for j in range(CC):
                split_x(0, 0, j)
            for f in range(AHEAD):
                split_w(0, f)

            def step(b, parity):
                for f in range(FC):
                    if (due := upto(b, FC, f + 1)) is not None:
                        dve.wait_ge(h_done, due)
                    if (due := upto(b, FC, f - NR + 1)) is not None:
                        dve.wait_ge(down_mm, due)
                    s = f % NR
                    dve.tensor_copy(h_hi[:, s, :], hid[:, f % 2, :]).then_inc(hhi_done, 1)
                    if (due := upto(b, FC, f + 1)) is not None:
                        dve.wait_ge(hhi_done, due)
                    dve.tensor_tensor(h_lo[:, s, :], hid[:, f % 2, :], h_hi[:, s, :].bitcast(F32), ALU.subtract).then_inc(hlo_done, 1)
                    if f in (2, 3):
                        statistics(b - 1, 1 - parity, (0, 1) if f == 2 else (2, 3))
                    split_w(b, f + AHEAD)
                    if f in TR_AT and inside(b + 1):
                        split_x(b + 1, 1 - parity, TR_AT.index(f))
                for t in range(TT):
                    if t < TT - 1:
                        if (due := upto(b, TT - 1, t + 1)) is not None:
                            dve.wait_ge(acc_mm, due)
                    else:
                        if (due := upto(b, FC, FC)) is not None:
                            dve.wait_ge(down_mm, due)
                    if (due := upto(b, 1, 1)) is not None:
                        dve.wait_ge(xb_done, due)
                    x = x_res[parity][:, t, :]
                    dve.tensor_tensor(x, acc[t][:, :], x, ALU.add).then_inc(res_done, 1)

            def statistics(b, parity, tiles):
                if not inside(b):
                    return
                for t in tiles:
                    if (due := upto(b, TT, t + 1)) is not None:
                        dve.wait_ge(res_done, due)
                    if (due := upto(b - 1, TT, TT)) is not None:
                        dve.wait_ge(mv_done, due)
                    dve.bn_stats(stats[:, t, :], x_res[parity][:, t, :]).then_inc(st_done, 1)
                if TT - 1 not in tiles:
                    return
                for t in range(TT):
                    dve.wait_ge(made, 5)
                    if (due := upto(b, TT, t + 1)) is not None:
                        dve.wait_ge(st_done, due)
                    if t == 0:
                        if (due := upto(b - 1, 1, 1)) is not None:
                            dve.wait_ge(shift_done, due)
                    dve.bn_aggr(mv[:, t, :], stats[:, t, :]).then_inc(mv_done, 1)

            paired(dve, step)
            statistics(NB - 1, 1, range(TT))

        @block.tensor
        def _(pe):
            pe.wait_ge(made, 5)

            def transpose_x(b, parity, j):
                pe.wait_ge(x_in[parity], (b - parity) * 8 + 16)
                if (due := upto(b, CC, j - 1)) is not None:
                    pe.wait_ge(xlo_done, due)
                for t in range(TT):
                    last = pe.transpose(t_ps[j % 2][:, t * P:t * P + P], x_res[parity][:, t, j * P:j * P + P], ident[:, :])
                last.then_inc(tr_mm, 1)

            for j in range(CC):
                transpose_x(0, 0, j)

            def up(b, parity, f):
                if f == 0:
                    if (due := upto(b, CC, CC)) is not None:
                        pe.wait_ge(xlo_done, due)
                if (due := upto(b, FC, f + 1)) is not None:
                    pe.wait_ge(whi_done, due)
                if (due := upto(b, FC, f + 1)) is not None:
                    pe.wait_ge(wlo_done, due)
                if (due := upto(b, FC, f - 1)) is not None:
                    pe.wait_ge(h_done, due)
                s, n = f % NW, 0
                for j in range(CC):
                    js = slice(j * P, j * P + P)
                    for wx, xx in ((w_hi, xT_hi), (w_hi, xT_lo), (w_lo, xT_hi)):
                        last = pe.matmul(h_ps[f % 2][:, :], wx[:, s, js], xx[parity][:, j, :], start=(n == 0), stop=(n == 3 * CC - 1))
                        n += 1
                last.then_inc(up_mm, 1)

            def down(b, f):
                if (due := upto(b, FC, f + 1)) is not None:
                    pe.wait_ge(hhi_done, due)
                if (due := upto(b, FC, f + 1)) is not None:
                    pe.wait_ge(hlo_done, due)
                s, sw = f % NR, f % NW
                for t in range(TT):
                    ts = slice(t * P, t * P + P)
                    if f == 0:
                        if (due := upto(b - 1, TT, t + 1)) is not None:
                            pe.wait_ge(res_done, due)
                    for n, (hx, wx) in enumerate(((h_hi, w_hi), (h_hi, w_lo), (h_lo, w_hi))):
                        last = pe.matmul(acc[t][:, :], hx[:, s, ts], wx[:, sw, C:], start=(f == 0 and n == 0),
                                         stop=(f == FC - 1 and n == 2))
                    if f == FC - 1 and t < TT - 1:
                        last.then_inc(acc_mm, 1)
                last.then_inc(down_mm, 1)

            def step(b, parity):
                for f in range(FC):
                    up(b, parity, f)
                    if f >= LAG:
                        down(b, f - LAG)
                    if f in TR_AT and inside(b + 1):
                        transpose_x(b + 1, 1 - parity, TR_AT.index(f))
                for f in range(FC - LAG, FC):
                    down(b, f)

            paired(pe, step)


def build(nc, d, out):
    x2_dram = nc.dram_tensor("x2_scratch", [NB, P, TT, C], F32, kind="Internal").ap()
    with ExitStack() as ctx:
        idx = ctx.enter_context(nc.sbuf_tensor("idx", [1, NB], U32))
        x2_stored = ctx.enter_context(nc.semaphore("x2_stored"))
        mixers(nc, d, idx, x2_dram, x2_stored)
        experts(nc, d, idx, x2_dram, out)


def kernel(**inputs):
    import numpy as np
    import concourse.bacc as bacc
    from concourse.bass_utils import run_bass_kernel_spmd

    g = {k: np.asarray(v) for k, v in inputs.items()}

    def tokens(x):
        return x.reshape(NB, TT, P, C).transpose(0, 2, 1, 3)

    def channels(x):
        return x.transpose(0, 2, 1).reshape(NB, CC, P, T).transpose(0, 2, 1, 3)

    def column(v):
        return v.reshape(-1, P).T

    def weights(w):
        return w.T.reshape(CC, P, -1).transpose(1, 0, 2)

    x_names = {n: g[f"L0_xattn_{n}"] for n in
               ("wqg", "bqg", "wkg", "bkg", "wvg", "bvg", "wql", "bql", "wkl", "bkl", "wvl", "bvl", "wp", "bp")}
    w1 = g["L0_ffn_W1"].reshape(NE, CC, P, FC, P).transpose(0, 3, 2, 1, 4).reshape(NE, FC, P, C)
    w2 = g["L0_ffn_W2"].reshape(NE, FC, P, C)
    laid = {
        "xT": channels(g["x"]),
        "x_tok": tokens(g["x"]),
        "ctx_tok": tokens(g["ctx_1024"]),
        "ctxT": channels(g["ctx_1024"]),
        "w_attn": np.concatenate([weights(g["L0_attn_Wqkv"]), weights(g["L0_attn_Wproj"])], axis=2),
        "b_qkv": column(g["L0_attn_bqkv"]),
        "scale": g["L0_attn_scale"].reshape(1, 1),
        "rows": np.stack([x_names[n] for n in ("wkg", "bkg", "wkl", "bkl", "wvg", "bvg", "wvl", "bvl")]
                         + [g["L0_attn_bproj"]]),
        "cols": np.stack([column(x_names[n]) for n in ("wqg", "bqg", "wql", "bql", "wp", "bp")], axis=1),
        "wr": g["L0_ffn_Wr"].reshape(CC, P, NE).transpose(1, 0, 2),
        "br": g["L0_ffn_br"].reshape(1, NE),
        "w12": np.concatenate([w1, w2], axis=3),
        "b1": g["L0_ffn_b1"].reshape(NE, FC, P).transpose(0, 2, 1),
        "b2": g["L0_ffn_b2"],
    }
    nc = bacc.Bacc("TRN2", target_bir_lowering=False, num_devices=1, dynamic_dma_scratch_size=2048)
    arrays, d = {}, {}
    for name, a in laid.items():
        a = np.ascontiguousarray(a)
        arrays[f"in_{name}"] = a
        d[name] = nc.dram_tensor(f"in_{name}", a.shape, mybir.dt.from_np(a.dtype), kind="ExternalInput").ap()
    out = nc.dram_tensor("out_dram", (NB, P, TT, C), F32, kind="ExternalOutput").ap()
    build(nc, d, out)
    r = run_bass_kernel_spmd(nc, [arrays], core_ids=[0])
    got = r.results[0]["out_dram"]
    return got.transpose(0, 2, 1, 3).reshape(NB, T, C)
```

```python
import concourse.bass as bass
from concourse import mybir
from contextlib import ExitStack

F32 = mybir.dt.float32
F32R = mybir.dt.float32r
U32 = mybir.dt.uint32
ALU = mybir.AluOpType
ACT = mybir.ActivationFunctionType
AX = mybir.AxisListType

P = 128
NB = 16
T = 512
C = 512
CC = C // P
TT = T // P
HD = 32
NH = C // HD
XH = 4
DFF = 2048
FC = DFF // P
NE = 8
SEG = P // TT
SUM = 32
EPS_DEN = 0.001
EPS_LN = 1e-05
XSCALE = float(C) ** -0.5


def upto(batch, per, n):
    if not isinstance(batch, int):
        return batch * per + n
    return min(batch * per + n, NB * per) if batch * per + n > 0 else None


def staged(eng, body):
    for i in range(3):
        body(i)
    with eng.Fori(3, NB - 1) as i:
        body(i)
    for i in range(NB - 1, NB + 3):
        body(i)


def inside(b):
    return not isinstance(b, int) or 0 <= b < NB


def mixers(nc, d, idx, x2_dram, x2_stored):
    with ExitStack() as ctx:
        def sb(name, shape, dt=F32):
            return ctx.enter_context(nc.sbuf_tensor(name, shape, dt))

        def sem(name):
            return ctx.enter_context(nc.semaphore(name))

        w = {"hi": sb("w_hi", [P, 4, CC, C], F32R), "lo": sb("w_lo", [P, 4, CC, C], F32R)}
        WK, WV, WQ, WPROJ = range(4)

        rows = sb("rows", [P, 9, C])
        WKG, BKG, WKL, BKL, WVG, BVG, WVL, BVL, BPROJ = range(9)
        cols = sb("cols", [P, 6, XH])
        WQG, BQG, WQL, BQL, WP, BP = range(6)
        b_qkv = sb("b_qkv", [P, 3 * CC])
        sb_qkv = sb("sb_qkv", [P, 3 * CC])
        scale = sb("scale", [P, 1])
        wr = sb("wr", [P, CC, NE])
        br = sb("br", [1, NE])
        ident = sb("ident", [P, P])
        ones = sb("ones", [P, P])
        head_sum = sb("head_sum", [P, CC, SEG])
        head_all = sb("head_all", [P, CC, P], F32R)
        low_rows = sb("low_rows", [P, 1])
        half = sb("half", [P, TT])
        ln_eps, minus = sb("ln_eps", [P, TT]), sb("minus", [P, TT])
        nbq = sb("nbq", [P, 2, XH])
        wp2 = sb("wp2", [P, XH])

        xT_raw = sb("xT_raw", [P, CC, T])
        xT_hi = sb("xT_hi", [P, CC, T], F32R)
        xT_lo = sb("xT_lo", [P, CC, T], F32R)
        e_k, r_k = sb("e_k", [P, T]), sb("r_k", [P, T])
        e_q, r_q = sb("e_q", [P, T]), sb("r_q", [P, T])
        k_sum, kv_sum, q = sb("k_sum", [P, T]), sb("kv_sum", [P, T]), sb("q", [P, T])
        qk = sb("qk", [P, CC, T])
        y = sb("y", [P, CC, T])
        y_hi, y_lo = sb("y_hi", [P, CC, T], F32R), sb("y_lo", [P, CC, T], F32R)
        den, rden = sb("den", [P, P], F32R), sb("rden", [P, P])
        rden_all = sb("rden_all", [P, T], F32R)
        x_tok = sb("x_tok", [P, TT, C])
        x1 = sb("x1", [P, TT, C])
        ctx_tok, ctx_T = sb("ctx_tok", [P, TT, C]), sb("ctx_T", [P, CC, T])
        x2 = sb("x2", [P, TT, C])
        c_col = sb("c_col", [P, XH])
        diag = sb("diag", [P, XH, P])
        s_x = sb("s_x", [P, XH])
        s_q = sb("s_q", [P, 2, XH])
        s_a = sb("s_a", [P, 2, XH, P])
        neg_max = sb("neg_max", [P, 2, XH])
        neg_scaled = sb("neg_scaled", [P, 2, XH])
        e_sum = sb("e_sum", [P, 2, XH])
        e_rec = sb("e_rec", [P, 2, XH])
        e_rec2 = sb("e_rec2", [P, 2, XH])
        a_v = sb("a_v", [P, 2, XH, P])
        junk_v = sb("junk_v", [P, 2, P])
        k_const = sb("k_const", [P, 2, XH])
        k_all, k_all2 = sb("k_all", [P, XH]), sb("k_all2", [P, XH])
        aT = sb("aT", [P, XH, P])
        const_b = sb("const_b", [P, C])
        x_sum = sb("x_sum", [P, 2, C])
        m_col = sb("m_col", [P, CC])
        logits = sb("logits", [1, NE])
        top = sb("top", [1, NE])
        found = sb("found", [1, NE], U32)
        stats = sb("stats", [P, 2, TT, 6])
        mv = sb("mv", [P, 2, TT, 2])
        var_e, rstd, m_r, shift = (sb(n, [P, 2, TT]) for n in ("var_e", "rstd", "m_r", "shift"))

        bank = [ctx.enter_context(nc.psum_tensor(f"bank{i}", [P, 512], F32)) for i in range(8)]
        K_BANK, V_BANK, Q_BANK, DEN_BANK, G_BANK, C_BANK = bank[0], bank[1], bank[2], bank[3], bank[6], bank[7]
        WIDE = [bank[4], bank[5]]
        den_ps = DEN_BANK[:, 0:P]
        route_ps = DEN_BANK[0:1, 0:NE]
        sx_ps, mean_ps = (DEN_BANK[:, n:n + XH * SUM].rearrange("p (h e) -> p h e", h=XH) for n in (P, P + XH * SUM))
        g_ps = G_BANK[:, :].rearrange("p (h e) -> p h e", h=XH)
        c_ps = C_BANK[:, :].rearrange("p (h e) -> p h e", h=XH)

        w_in = [sem(f"w_in{n}") for n in range(4)]
        w_hi_done, w_lo_done = sem("w_hi_done"), sem("w_lo_done")
        w_raw = [buf[:, :, :].rearrange("p t n -> p (t n)") for buf in (y, qk, x1, x2)]
        small_in, consts_in = sem("small_in"), sem("consts_in")
        masks_done = sem("masks_done")
        made = sem("made")
        preset = sem("preset")
        xT_in, xtok_in, ctx_in, ctxT_in = sem("xT_in"), sem("xtok_in"), sem("ctx_in"), sem("ctxT_in")
        xhi_done, xlo_done = sem("xhi_done"), sem("xlo_done")
        k_mm, v_mm, q_mm = sem("k_mm"), sem("v_mm"), sem("q_mm")
        ek_done, eq_done = sem("ek_done"), sem("eq_done")
        k_done, kv_done, kc_done = sem("k_done"), sem("kv_done"), sem("kc_done")
        kvc_done, q_done, qk_done, num_done = sem("kvc_done"), sem("q_done"), sem("qk_done"), sem("num_done")
        den_mm, den_max, rden_done, rb_mm = sem("den_mm"), sem("den_max"), sem("rden_done"), sem("rb_mm")
        y_done, yhi_done, ylo_done = sem("y_done"), sem("yhi_done"), sem("ylo_done")
        proj_mm, xb_done, res1_done = sem("proj_mm"), sem("xb_done"), sem("res1_done")
        st_done = [sem("st1_done"), sem("st2_done")]
        mv_done = [sem("mv1_done"), sem("mv2_done")]
        ve_done = [sem("ve1_done"), sem("ve2_done")]
        rstd_done = [sem("rstd1_done"), sem("rstd2_done")]
        mr_done = [sem("mr1_done"), sem("mr2_done")]
        shift_done = [sem("shift1_done"), sem("shift2_done")]
        x1_done, x2_done = sem("x1_done"), sem("x2_done")
        g_mm, sx_mm, c_mm = sem("g_mm"), sem("sx_mm"), sem("c_mm")
        csum_done, diag_done, sx_done, sq_done = sem("csum_done"), sem("diag_done"), sem("sx_done"), sem("sq_done")
        sc_done = sem("sc_done")
        max_done, nmax_done = sem("max_done"), sem("nmax_done")
        exp_done = sem("exp_done")
        rec_done, rec2_done = sem("rec_done"), sem("rec2_done")
        av_done = sem("av_done")
        asum_done, kall_done, kall2_done, diag2_done = (sem(n) for n in ("asum_done", "kall_done", "kall2_done", "diag2_done"))
        aT_mm, kb_mm, aT_done, kb_done, x1c_done = (sem(n) for n in ("aT_mm", "kb_mm", "aT_done", "kb_done", "x1c_done"))
        out_mm, res2_done = sem("out_mm"), sem("res2_done")
        mean_mm, mcol_done, route_mm, logit_done, top_done, idx_done = (
            sem(n) for n in ("mean_mm", "mcol_done", "route_mm", "logit_done", "top_done", "idx_done"))
        found_done = sem("found_done")
        xsum_done, x2sum_done = sem("xsum_done"), sem("x2sum_done")
        rall_done = sem("rall_done")

        block = ctx.enter_context(nc.Block())
        MADE = 12 + 5 * TT
        head_mask = s_a[:, 0, :, :]
        zeros = s_a[:, 1, :, :].rearrange("p h e -> p (h e)")

        @block.sync
        def _(sp):
            sp.dma_start(xT_raw[:, :, :], d["xT"][0]).then_inc(xT_in, 16)
            sp.dma_start(w_raw[WK], d["w_attn"][WK]).then_inc(w_in[WK], 16)
            sp.dma_start(w_raw[WV], d["w_attn"][WV]).then_inc(w_in[WV], 16)
            sp.dma_start(cols[:, :, :], d["cols"]).then_inc(small_in, 16)
            sp.dma_start(b_qkv[:, :], d["b_qkv"]).then_inc(small_in, 16)
            sp.dma_start(scale[:, :], d["scale"].broadcast_to([P, 1])).then_inc(small_in, 16)
            sp.dma_start(w_raw[WQ], d["w_attn"][WQ]).then_inc(w_in[WQ], 16)
            sp.dma_start(w_raw[WPROJ], d["w_attn"][WPROJ]).then_inc(w_in[WPROJ], 16)
            sp.dma_start(rows[:, :, :], d["rows"].broadcast_to([P, 9, C])).then_inc(consts_in, 16)
            sp.dma_start(wr[:, :, :], d["wr"]).then_inc(consts_in, 16)
            sp.dma_start(br[:, :], d["br"]).then_inc(consts_in, 16)

            def step(i):
                a, b, c, e = i, i - 1, i - 2, i - 3
                if inside(i + 1):
                    if (due := upto(a, 2, 2)) is not None:
                        sp.wait_ge(xhi_done, due)
                    if (due := upto(a, 2, 2)) is not None:
                        sp.wait_ge(xlo_done, due)
                    sp.dma_start(xT_raw[:, :, :], dyn(d["xT"], i + 1)).then_inc(xT_in, 16)
                if inside(b):
                    if (due := upto(c, TT, TT)) is not None:
                        sp.wait_ge(out_mm, due)
                    if (due := upto(c, XH, XH)) is not None:
                        sp.wait_ge(csum_done, due)
                    sp.dma_start(ctx_T[:, :, :], dyn(d["ctxT"], b)).then_inc(ctxT_in, 16)
                if inside(c):
                    if (due := upto(c, TT, TT)) is not None:
                        sp.wait_ge(x2_done, due)
                    sp.dma_start(dyn(x2_dram, c), x2[:, :, :]).then_inc(x2_stored, 16)
                if inside(a):
                    if (due := upto(b, TT, TT)) is not None:
                        sp.wait_ge(x1_done, due)
                    sp.dma_start(x_tok[:, :, :], dyn(d["x_tok"], a)).then_inc(xtok_in, 16)
                if inside(a):
                    if (due := upto(b, 1, 1)) is not None:
                        sp.wait_ge(g_mm, due)
                    sp.dma_start(ctx_tok[:, :, :], dyn(d["ctx_tok"], a)).then_inc(ctx_in, 16)

            staged(sp, step)
            sp.wait_ge(x2_stored, 16 * NB)

        @block.gpsimd
        def _(pool):
            for m, value in ((ident, 0.0), (ones, 1.0), (half, -0.5), (ln_eps, EPS_LN), (minus, -1.0), (low_rows, 0.0)):
                pool.memset(m[:, :], value).then_inc(made, 1)
            pool.memset(head_sum[:, :, :], 1.0).then_inc(made, 1)
            pool.memset(head_mask, 1.0).then_inc(made, 1)
            pool.memset(zeros, 0.0).then_inc(made, 1)
            twice = head_sum[:, :, :].rearrange("p t (r h) -> p t r h", r=2)
            masks = [(ident[:, :], ALU.not_equal, 1.0, 0, [[-1, P]], 1),
                     (twice, ALU.is_ge, 0.0, 0, [[P, CC], [0, 2], [-HD, NH]], 1),
                     (twice, ALU.is_ge, 0.0, HD - 1, [[-P, CC], [0, 2], [HD, NH]], -1)]
            for s in range(TT):
                rows_s = slice(s * SEG, s * SEG + SEG)
                part = head_mask[rows_s]
                masks += [(part, ALU.is_ge, 0.0, -C + HD - 1, [[-P, CC], [-1, P]], HD),
                          (part, ALU.is_ge, 1.0, -1, [[-P, CC], [-1, P]], HD),
                          (part, ALU.is_ge, 0.0, HD - 1, [[-P, CC], [-1, P]], HD),
                          (part, ALU.is_ge, 0.0, C, [[P, CC], [1, P]], -HD),
                          (low_rows[rows_s, :], ALU.is_ge, -1.0, NH - 1, [[0, 1]], -1)]
            for n, (m, op, fill, base, pattern, step_p) in enumerate(masks):
                pool.wait_ge(made, 9 + n)
                pool.affine_select(out=m, in_=m, compare_op=op, fill=fill, base=base, pattern=pattern,
                                   channel_multiplier=step_p).then_inc(made, 1)
            pool.wait_ge(made, MADE)
            pool.wait_ge(consts_in, 16 * 3)

            def rstd_of(n, b):
                if (due := upto(b, TT, TT)) is not None:
                    pool.wait_ge(mv_done[n], due)
                if (due := upto(b - 1, TT, TT)) is not None:
                    pool.wait_ge(x1_done if n == 0 else x2_done, due)
                pool.tensor_tensor(var_e[:, n, :], mv[:, n, :, 1], ln_eps[:, :], ALU.add).then_inc(ve_done[n], 1)
                if (due := upto(b, 1, 1)) is not None:
                    pool.wait_ge(ve_done[n], due)
                pool.tensor_tensor(rstd[:, n, :], var_e[:, n, :], half[:, :], ALU.pow).then_inc(rstd_done[n], 1)
                if (due := upto(b, 1, 1)) is not None:
                    pool.wait_ge(rstd_done[n], due)
                pool.tensor_tensor(m_r[:, n, :], mv[:, n, :, 0], rstd[:, n, :], ALU.mult).then_inc(mr_done[n], 1)
                if (due := upto(b, 1, 1)) is not None:
                    pool.wait_ge(mr_done[n], due)
                pool.tensor_tensor(shift[:, n, :], m_r[:, n, :], minus[:, :], ALU.mult).then_inc(shift_done[n], 1)

            def tile_sum(n, b, x, x_done, used, done):
                if (due := upto(b, TT, TT)) is not None:
                    pool.wait_ge(x_done, due)
                if (due := upto(b - 1, 1, 1)) is not None:
                    pool.wait_ge(used, due)
                pool.tensor_tensor(x_sum[:, n, :], x[:, 0, :], x[:, 1, :], ALU.add).then_inc(done, 1)
                for t in range(2, TT):
                    if (due := upto(b, TT - 1, t - 1)) is not None:
                        pool.wait_ge(done, due)
                    pool.tensor_tensor(x_sum[:, n, :], x_sum[:, n, :], x[:, t, :], ALU.add).then_inc(done, 1)

            def step(i):
                b, c = i - 1, i - 2
                if inside(b):
                    for cc in range(CC):
                        if (due := upto(b, CC, cc + 1)) is not None:
                            pool.wait_ge(yhi_done, due)
                        if (due := upto(b - 1, TT, TT)) is not None:
                            pool.wait_ge(proj_mm, due)
                        pool.tensor_tensor(y_lo[:, cc, :], y[:, cc, :], y_hi[:, cc, :].bitcast(F32), ALU.subtract).then_inc(ylo_done, 1)
                    if (due := upto(b, 16, 16)) is not None:
                        pool.wait_ge(xtok_in, due)
                    pool.tensor_tensor(x_tok[:, :, :], x_tok[:, :, :],
                                       rows[:, BPROJ:BPROJ + 1, :].broadcast_to([P, TT, C]), ALU.add).then_inc(xb_done, 1)
                if inside(c):
                    if (due := upto(c, 1, 1)) is not None:
                        pool.wait_ge(kall2_done, due)
                    if (due := upto(c, 1, 1)) is not None:
                        pool.wait_ge(c_mm, due)
                    pool.tensor_tensor(diag[:, :, :], ident[:, :].unsqueeze(1).broadcast_to([P, XH, P]),
                                       k_all2[:, :].unsqueeze(2).broadcast_to([P, XH, P]), ALU.mult).then_inc(diag2_done, 1)
                    if (due := upto(c, 1, 1)) is not None:
                        pool.wait_ge(kb_done, due)
                    if (due := upto(c, 1, 1)) is not None:
                        pool.wait_ge(g_mm, due)
                    if (due := upto(c, TT - 1, TT - 1)) is not None:
                        pool.wait_ge(xsum_done, due)
                    for t in range(TT):
                        pool.tensor_tensor(x1[:, t, :], x1[:, t, :], const_b[:, :], ALU.add).then_inc(x1c_done, 1)
                if inside(b):
                    if (due := upto(b, XH, XH)) is not None:
                        pool.wait_ge(csum_done, due)
                    if (due := upto(c, 1, 1)) is not None:
                        pool.wait_ge(kb_mm, due)
                    pool.tensor_tensor(diag[:, :, :], ident[:, :].unsqueeze(1).broadcast_to([P, XH, P]),
                                       c_col[:, :].unsqueeze(2).broadcast_to([P, XH, P]), ALU.mult).then_inc(diag_done, 1)
                    rstd_of(0, b)
                if inside(c):
                    rstd_of(1, c)
                if inside(b):
                    tile_sum(0, b, x1, x1_done, sx_mm, xsum_done)
                if inside(c):
                    tile_sum(1, c, x2, x2_done, mean_mm, x2sum_done)

            staged(pool, step)

        @block.scalar
        def _(act):
            def split_weights(n):
                act.wait_ge(w_in[n], 16)
                act.activation(w["hi"][:, n, :, :].rearrange("p t n -> p (t n)"), w_raw[n], ACT.Copy).then_inc(w_hi_done, 1)


            def features(a, cc, kinds=(0, 1)):
                for n, (mm, e, r, done, used, ps) in enumerate((
                        (k_mm, e_k, r_k, ek_done, k_done, K_BANK), (q_mm, e_q, r_q, eq_done, q_done, Q_BANK))):
                    if n not in kinds:
                        continue
                    col = (1 - n) * CC + cc
                    if (due := upto(a, CC, cc + 1)) is not None:
                        act.wait_ge(mm, due)
                    if (due := upto(a, CC, cc)) is not None:
                        act.wait_ge(used, due)
                    act.activation(e[:, :], ps[:, :], ACT.Exp, bias=sb_qkv[:, col:col + 1],
                                   scale=scale[:, 0:1]).then_inc(done, 1)
                    act.activation(r[:, :], ps[:, :], ACT.Relu, bias=sb_qkv[:, col:col + 1],
                                   scale=scale[:, 0:1]).then_inc(done, 1)

            def split_x(b):
                if (due := upto(b, 16, 16)) is not None:
                    act.wait_ge(xT_in, due)
                if (due := upto(b - 1, CC, CC)) is not None:
                    act.wait_ge(q_mm, due)
                for n in range(2):
                    act.activation(xT_hi[:, 2 * n:2 * n + 2, :], xT_raw[:, 2 * n:2 * n + 2, :], ACT.Copy).then_inc(xhi_done, 1)

            def normalise(n, b):
                if (due := upto(b, 1, 1)) is not None:
                    act.wait_ge(shift_done[n], due)
                if n == 0:
                    if (due := upto(b - 1, TT, TT)) is not None:
                        act.wait_ge(res2_done, due)
                src, dst, done = ((x_tok, x1, x1_done), (x2, x2, x2_done))[n]
                for t in range(TT):
                    act.activation(dst[:, t, :], src[:, t, :], ACT.Identity, bias=shift[:, n, t:t + 1],
                                   scale=rstd[:, n, t:t + 1]).then_inc(done, 1)

            split_x(0)
            for n in range(3):
                split_weights(n)
            act.wait_ge(preset, 4)

            def high_parts(b, chunks):
                for cc in chunks:
                    if (due := upto(b, CC, cc + 1)) is not None:
                        act.wait_ge(y_done, due)
                    act.activation(y_hi[:, cc, :], y[:, cc, :], ACT.Copy).then_inc(yhi_done, 1)

            def exps(c, v):
                if (due := upto(c, 2, v + 1)) is not None:
                    act.wait_ge(nmax_done, due)
                if (due := upto(c - 1, 4 * XH, 4 * XH)) is not None:
                    act.wait_ge(av_done, due)
                for h in range(XH):
                    act.activation(s_a[:, v, h, :], s_a[:, v, h, :], ACT.Exp, bias=neg_scaled[:, v, h:h + 1],
                                   scale=XSCALE, accum_out=e_sum[:, v, h:h + 1]).then_inc(exp_done, 1)

            def step(i):
                a, b, c, e = i, i - 1, i - 2, i - 3
                if inside(a):
                    features(a, 0, (0,))
                if inside(b):
                    if isinstance(b, int) and b == 0:
                        act.wait_ge(made, MADE)
                        act.activation(head_all[:, :, :], head_mask, ACT.Copy).then_inc(masks_done, 1)
                        act.activation(rden_all[:, :], zeros, ACT.Copy).then_inc(masks_done, 1)
                        act.wait_ge(masks_done, 2)
                    if (due := upto(b, 3, 3)) is not None:
                        act.wait_ge(rden_done, due)
                    if (due := upto(b - 1, CC, CC)) is not None:
                        act.wait_ge(rb_mm, due)
                    for s in range(TT):
                        rows_s = slice(s * SEG, s * SEG + SEG)
                        act.activation(rden_all[rows_s, s * P:s * P + P], rden[rows_s, :], ACT.Copy).then_inc(rall_done, 1)
                if inside(b):
                    if (due := upto(c, TT, TT)) is not None:
                        act.wait_ge(proj_mm, due)
                    high_parts(b, (0, 1))
                if inside(a):
                    features(a, 0, (1,))
                if inside(e):
                    if (due := upto(e, 1, 1)) is not None:
                        act.wait_ge(mean_mm, due)
                    if inside(c):
                        if (due := upto(c, 1, 1)) is not None:
                            act.wait_ge(sx_mm, due)
                    if (due := upto(e - 1, 1, 1)) is not None:
                        act.wait_ge(route_mm, due)
                    act.activation(m_col[:, :], mean_ps[:, :, 0], ACT.Copy, scale=1.0 / T).then_inc(mcol_done, 1)
                if inside(c):
                    if (due := upto(c, 1, 1)) is not None:
                        act.wait_ge(sx_mm, due)
                    if (due := upto(c - 1, 3, 2)) is not None:
                        act.wait_ge(sq_done, due)
                    act.activation(s_x[:, :], sx_ps[:, :, 0], ACT.Copy).then_inc(sx_done, 1)
                if inside(b):
                    high_parts(b, (2, 3))
                if isinstance(a, int) and a == 0:
                    split_weights(WPROJ)
                if inside(a):
                    features(a, 1, (0,))
                if inside(c):
                    exps(c, 0)
                if inside(c):
                    exps(c, 1)
                if inside(a):
                    features(a, 1, (1,))
                    features(a, 2, (0,))
                if inside(c):
                    if (due := upto(c, 1, 1)) is not None:
                        act.wait_ge(aT_mm, due)
                    if (due := upto(c - 1, TT, TT)) is not None:
                        act.wait_ge(out_mm, due)
                    act.activation(aT[:, :, :], g_ps, ACT.Copy).then_inc(aT_done, 1)
                    if (due := upto(c, 1, 1)) is not None:
                        act.wait_ge(kb_mm, due)
                    if (due := upto(b - 1, XH, XH)) is not None:
                        act.wait_ge(csum_done, due)
                    act.activation(const_b[:, :], C_BANK[:, :], ACT.Copy).then_inc(kb_done, 1)
                if inside(a):
                    features(a, 2, (1,))
                if inside(b):
                    if (due := upto(b, 16, 16)) is not None:
                        act.wait_ge(ctxT_in, due)
                    if (due := upto(c, 1, 1)) is not None:
                        act.wait_ge(diag_done, due)
                    if (due := upto(c, TT, TT)) is not None:
                        act.wait_ge(x1c_done, due)
                    for h in range(XH):
                        if (due := upto(b, XH, h)) is not None:
                            act.wait_ge(csum_done, due)
                        act.activation(const_b[:, :], ctx_T[:, h, :], ACT.Copy,
                                       accum_out=c_col[:, h:h + 1]).then_inc(csum_done, 1)
                if inside(a):
                    features(a, 3, (0,))
                if inside(b):
                    normalise(0, b)
                if inside(i + 1):
                    split_x(i + 1)
                if inside(a):
                    features(a, 3, (1,))
                if inside(c):
                    normalise(1, c)

            staged(act, step)

        @block.vector
        def _(dve):
            def presets():
                dve.wait_ge(small_in, 16 * 3)
                dve.tensor_scalar(sb_qkv[:, :], b_qkv[:, :], scale[:, 0:1], None, ALU.mult).then_inc(preset, 1)
                dve.tensor_scalar(nbq[:, 0, :], cols[:, BQG, :], float(T), None, ALU.mult).then_inc(preset, 1)
                dve.tensor_scalar(nbq[:, 1, :], cols[:, BQL, :], float(T), None, ALU.mult).then_inc(preset, 1)
                dve.tensor_scalar(wp2[:, :], cols[:, WP, :], 2.0, None, ALU.mult).then_inc(preset, 1)
                dve.wait_ge(preset, 4)

            def split_weights(n):
                dve.wait_ge(w_hi_done, n + 1)
                dve.tensor_tensor(w["lo"][:, n, :, :].rearrange("p t n -> p (t n)"), w_raw[n],
                                  w["hi"][:, n, :, :].rearrange("p t n -> p (t n)").bitcast(F32),
                                  ALU.subtract).then_inc(w_lo_done, 1)

            def keys(a, cc):
                if (due := upto(a, 2 * CC, 2 * cc + 2)) is not None:
                    dve.wait_ge(ek_done, due)
                if (due := upto(a, CC, cc)) is not None:
                    dve.wait_ge(qk_done, due)
                dve.scalar_tensor_tensor(k_sum[:, :], e_k[:, :], 1.0, r_k[:, :], ALU.min, ALU.add).then_inc(k_done, 1)

            def values(a, cc):
                if (due := upto(a, CC, cc + 1)) is not None:
                    dve.wait_ge(v_mm, due)
                if (due := upto(a, CC, cc + 1)) is not None:
                    dve.wait_ge(k_done, due)
                if (due := upto(a, CC, cc)) is not None:
                    dve.wait_ge(num_done, due)
                dve.scalar_tensor_tensor(kv_sum[:, :], V_BANK[:, :], b_qkv[:, 2 * CC + cc:2 * CC + cc + 1],
                                         k_sum[:, :], ALU.add, ALU.mult).then_inc(kv_done, 1)
                if (due := upto(a, CC, cc + 1)) is not None:
                    dve.wait_ge(kv_done, due)
                dve.tensor_tensor_scan(k_sum[:, :], k_sum[:, :], k_sum[:, :], 0.0, ALU.add, ALU.bypass).then_inc(kc_done, 1)
                dve.tensor_tensor_scan(kv_sum[:, :], kv_sum[:, :], kv_sum[:, :], 0.0, ALU.add, ALU.bypass).then_inc(kvc_done, 1)

            def queries(a, cc):
                if (due := upto(a, 2 * CC, 2 * cc + 2)) is not None:
                    dve.wait_ge(eq_done, due)
                dve.scalar_tensor_tensor(q[:, :], e_q[:, :], 1.0, r_q[:, :], ALU.min, ALU.add).then_inc(q_done, 1)
                if (due := upto(a, CC, cc + 1)) is not None:
                    dve.wait_ge(q_done, due)
                if (due := upto(a, CC, cc + 1)) is not None:
                    dve.wait_ge(kc_done, due)
                if (due := upto(a - 1, 1, 1)) is not None:
                    dve.wait_ge(den_mm, due)
                dve.tensor_tensor(qk[:, cc, :], q[:, :], k_sum[:, :], ALU.mult).then_inc(qk_done, 1)

            def numerator(a, cc):
                if (due := upto(a, CC, cc + 1)) is not None:
                    dve.wait_ge(q_done, due)
                if (due := upto(a, CC, cc + 1)) is not None:
                    dve.wait_ge(kvc_done, due)
                if (due := upto(a - 1, CC, cc + 1)) is not None:
                    dve.wait_ge(ylo_done, due)
                dve.tensor_tensor(y[:, cc, :], q[:, :], kv_sum[:, :], ALU.mult).then_inc(num_done, 1)

            def residual(n, b, t):
                mm, res, done, src, dst = ((proj_mm, x_tok, res1_done, x_tok, x_tok),
                                           (out_mm, x1, res2_done, x1, x2))[n]
                if (due := upto(b, TT, t + 1)) is not None:
                    dve.wait_ge(mm, due)
                if n == 0:
                    if (due := upto(b, 1, 1)) is not None:
                        dve.wait_ge(xb_done, due)
                else:
                    if (due := upto(b, TT, t + 1)) is not None:
                        dve.wait_ge(x1c_done, due)
                    if (due := upto(b - 1, TT - 1, TT - 1)) is not None:
                        dve.wait_ge(x2sum_done, due)
                    if (due := upto(b - 1, 16, 16)) is not None:
                        dve.wait_ge(x2_stored, due)
                ps = WIDE[t % 2]
                dve.tensor_tensor(dst[:, t, :], ps[:, :], src[:, t, :], ALU.add).then_inc(done, 1)

            def statistics(n, b, tiles):
                done = (res1_done, res2_done)[n]
                x = (x_tok, x2)[n]
                for t in tiles:
                    if (due := upto(b, TT, t + 1)) is not None:
                        dve.wait_ge(done, due)
                    if (due := upto(b - 1, TT, TT)) is not None:
                        dve.wait_ge(mv_done[n], due)
                    dve.bn_stats(stats[:, n, t, :], x[:, t, :]).then_inc(st_done[n], 1)

            def moments(n, b):
                for t in range(TT):
                    dve.wait_ge(preset, 4)
                    if (due := upto(b, TT, t + 1)) is not None:
                        dve.wait_ge(st_done[n], due)
                    if t == 0:
                        if (due := upto(b - 1, 1, 1)) is not None:
                            dve.wait_ge(shift_done[n], due)
                    dve.bn_aggr(mv[:, n, t, :], stats[:, n, t, :]).then_inc(mv_done[n], 1)

            def token_sums(c):
                if (due := upto(c, 1, 1)) is not None:
                    dve.wait_ge(sx_done, due)
                dve.tensor_tensor(s_q[:, 0, :], s_x[:, :], cols[:, WQG, :], ALU.mult).then_inc(sq_done, 1)
                dve.tensor_tensor(s_q[:, 1, :], s_x[:, :], cols[:, WQL, :], ALU.mult).then_inc(sq_done, 1)
                if (due := upto(c, 3, 2)) is not None:
                    dve.wait_ge(sq_done, due)
                dve.tensor_tensor(s_q[:, :, :], s_q[:, :, :], nbq[:, :, :], ALU.add).then_inc(sq_done, 1)

            def row(n):
                return rows[:, n, :].rearrange("p (h e) -> p h e", h=XH)

            def per_channel(col):
                return col.unsqueeze(2).broadcast_to([P, XH, P])

            def scores_inner(c):
                if (due := upto(c, 1, 1)) is not None:
                    dve.wait_ge(g_mm, due)
                if (due := upto(c, 1, 1)) is not None:
                    dve.wait_ge(c_mm, due)
                if (due := upto(c - 1, 4 * XH, 4 * XH)) is not None:
                    dve.wait_ge(av_done, due)
                for v, (wq, bq) in enumerate(((WQG, BQG), (WQL, BQL))):
                    dve.tensor_tensor(s_a[:, v, :, :], g_ps, per_channel(cols[:, wq, :]), ALU.mult).then_inc(sc_done, 1)
                    dve.tensor_tensor(a_v[:, v, :, :], c_ps, per_channel(cols[:, bq, :]), ALU.mult).then_inc(sc_done, 1)

            def scores_outer(c):
                if (due := upto(c, 12, 4)) is not None:
                    dve.wait_ge(sc_done, due)
                for v in range(2):
                    dve.tensor_tensor(s_a[:, v, :, :], s_a[:, v, :, :], a_v[:, v, :, :], ALU.add).then_inc(sc_done, 1)
                for v, wk in enumerate((WKG, WKL)):
                    if (due := upto(c, 12, 5 + v)) is not None:
                        dve.wait_ge(sc_done, due)
                    dve.tensor_tensor(s_a[:, v, :, :], s_a[:, v, :, :], row(wk), ALU.mult).then_inc(sc_done, 1)

            def scores_bias(c):
                if (due := upto(c, 3, 3)) is not None:
                    dve.wait_ge(sq_done, due)
                if (due := upto(c, 12, 6)) is not None:
                    dve.wait_ge(sc_done, due)
                for v, bk in enumerate((BKG, BKL)):
                    dve.tensor_tensor(a_v[:, v, :, :], row(bk), per_channel(s_q[:, v, :]), ALU.mult).then_inc(sc_done, 1)

            def scores_max(c):
                for v in range(2):
                    if (due := upto(c, 12, 9 + v)) is not None:
                        dve.wait_ge(sc_done, due)
                    dve.tensor_tensor(s_a[:, v, :, :], s_a[:, v, :, :], a_v[:, v, :, :], ALU.add).then_inc(sc_done, 1)
                for v in range(2):
                    if (due := upto(c, 12, 11 + v)) is not None:
                        dve.wait_ge(sc_done, due)
                    dve.reduce_max(neg_max[:, v, :], s_a[:, v, :, :], AX.X).then_inc(max_done, 1)
                for v in range(2):
                    if (due := upto(c, 2, v + 1)) is not None:
                        dve.wait_ge(max_done, due)
                    dve.tensor_scalar(neg_scaled[:, v, :], neg_max[:, v, :], -XSCALE, None, ALU.mult).then_inc(nmax_done, 1)

            def weigh(c, v):
                pairs = ((WVG, BVG), (WVL, BVL))
                if (due := upto(c, 2 * XH, (v + 1) * XH)) is not None:
                    dve.wait_ge(exp_done, due)
                dve.reciprocal(e_rec[:, v, :], e_sum[:, v, :]).then_inc(rec_done, 1)
                if (due := upto(c, 2, v + 1)) is not None:
                    dve.wait_ge(rec_done, due)
                dve.tensor_tensor(e_rec2[:, v, :], e_rec[:, v, :], wp2[:, :], ALU.mult).then_inc(rec2_done, 1)
                if (due := upto(c, 2, v + 1)) is not None:
                    dve.wait_ge(rec2_done, due)
                if (due := upto(c - 1, 1, 1)) is not None:
                    dve.wait_ge(kall_done, due)
                wv, bv = pairs[v]
                for h in range(XH):
                    if (due := upto(c, 4 * XH, 2 * XH * v + max(h - 1, 0))) is not None:
                        dve.wait_ge(av_done, due)
                    dve.scalar_tensor_tensor(junk_v[:, h % 2, :], s_a[:, v, h, :], e_rec2[:, v, h:h + 1],
                                             rows[:, bv, h * P:h * P + P],
                                             ALU.mult, ALU.mult, accum_out=k_const[:, v, h:h + 1]).then_inc(av_done, 1)
                for h in range(XH):
                    dve.scalar_tensor_tensor(a_v[:, v, h, :], s_a[:, v, h, :], e_rec2[:, v, h:h + 1],
                                             rows[:, wv, h * P:h * P + P], ALU.mult, ALU.mult).then_inc(av_done, 1)
                    if v == 1 and h == 0:
                        if (due := upto(c, 4 * XH, 3 * XH)) is not None:
                            dve.wait_ge(av_done, due)
                        dve.tensor_tensor(k_all[:, :], k_const[:, 0, :], k_const[:, 1, :], ALU.add).then_inc(kall_done, 1)
                    if v == 1 and h == 1:
                        if (due := upto(c, 1, 1)) is not None:
                            dve.wait_ge(kall_done, due)
                        if (due := upto(c - 1, 1, 1)) is not None:
                            dve.wait_ge(diag2_done, due)
                        dve.tensor_tensor(k_all2[:, :], k_all[:, :], cols[:, BP, :], ALU.add).then_inc(kall2_done, 1)
                if v == 1:
                    if (due := upto(c, 4 * XH, 4 * XH)) is not None:
                        dve.wait_ge(av_done, due)
                    dve.tensor_tensor(a_v[:, 0, :, :], a_v[:, 0, :, :], a_v[:, 1, :, :], ALU.add).then_inc(asum_done, 1)

            def choose(c):
                if (due := upto(c, 1, 1)) is not None:
                    dve.wait_ge(route_mm, due)
                dve.tensor_tensor(logits[:, :], route_ps, br[:, :], ALU.add).then_inc(logit_done, 1)
                dve.wait_ge(preset, 4)
                if (due := upto(c, 1, 1)) is not None:
                    dve.wait_ge(logit_done, due)
                dve.max(top[:, :], logits[:, :]).then_inc(top_done, 1)
                dve.wait_ge(preset, 4)
                if (due := upto(c, 1, 1)) is not None:
                    dve.wait_ge(top_done, due)
                dve.max_index(found[:, :], top[:, :], logits[:, :]).then_inc(found_done, 1)
                if (due := upto(c, 1, 1)) is not None:
                    dve.wait_ge(found_done, due)
                dve.tensor_copy(idx[0:1, c:c + 1] if isinstance(c, int) else idx[0:1, bass.ds(c, 1)],
                                found[:, 0:1]).then_inc(idx_done, 1)

            def split_x(b):
                for n in range(2):
                    ns = slice(2 * n, 2 * n + 2)
                    if (due := upto(b, 2, n + 1)) is not None:
                        dve.wait_ge(xhi_done, due)
                    if (due := upto(b - 1, CC, CC)) is not None:
                        dve.wait_ge(q_mm, due)
                    dve.tensor_tensor(xT_lo[:, ns, :], xT_raw[:, ns, :], xT_hi[:, ns, :].bitcast(F32), ALU.subtract).then_inc(xlo_done, 1)

            split_x(0)
            split_weights(WK)
            split_weights(WV)
            presets()
            split_weights(WQ)
            dve.wait_ge(w_lo_done, 3)

            def times_reciprocal(b, cc):
                if (due := upto(b, CC, cc + 1)) is not None:
                    dve.wait_ge(rb_mm, due)
                if (due := upto(b, CC, cc + 1)) is not None:
                    dve.wait_ge(num_done, due)
                dve.tensor_tensor(y[:, cc, :], y[:, cc, :], WIDE[cc % 2][:, :], ALU.mult).then_inc(y_done, 1)

            def step(i):
                a, b, c, e = i, i - 1, i - 2, i - 3
                if isinstance(c, int) and c == 0:
                    dve.wait_ge(consts_in, 16 * 3)
                    dve.wait_ge(masks_done, 2)
                if inside(c):
                    scores_inner(c)
                if inside(b):
                    if (due := upto(b, 1, 1)) is not None:
                        dve.wait_ge(den_mm, due)
                    if (due := upto(b - 1, TT, TT)) is not None:
                        dve.wait_ge(rall_done, due)
                    dve.tensor_scalar(den[:, :].bitcast(F32), den_ps, EPS_DEN, None, ALU.max).then_inc(den_max, 1)
                    if (due := upto(b, 1, 1)) is not None:
                        dve.wait_ge(den_max, due)
                    dve.reciprocal(rden[:, :], den[:, :].bitcast(F32)).then_inc(rden_done, 1)
                    if (due := upto(b, 3, 1)) is not None:
                        dve.wait_ge(rden_done, due)
                    dve.tensor_copy(den[:, :], rden[:, :]).then_inc(rden_done, 1)
                    if (due := upto(b, 3, 2)) is not None:
                        dve.wait_ge(rden_done, due)
                    dve.scalar_tensor_tensor(rden[:, :], den[:, :].bitcast(F32), low_rows[:, 0:1], rden[:, :],
                                             ALU.mult, ALU.add).then_inc(rden_done, 1)
                if inside(a):
                    keys(a, 0)
                    values(a, 0)
                if inside(b):
                    times_reciprocal(b, 0)
                    times_reciprocal(b, 1)
                if inside(c):
                    scores_outer(c)
                if inside(b):
                    times_reciprocal(b, 2)
                    times_reciprocal(b, 3)
                if inside(a):
                    queries(a, 0)
                    numerator(a, 0)
                if inside(c):
                    token_sums(c)
                    scores_bias(c)
                    scores_max(c)
                if isinstance(a, int) and a == 0:
                    split_weights(WPROJ)
                if inside(a):
                    keys(a, 1)
                    values(a, 1)
                if inside(c):
                    weigh(c, 0)
                if inside(a):
                    queries(a, 1)
                    numerator(a, 1)
                if inside(c):
                    weigh(c, 1)
                if inside(a):
                    keys(a, 2)
                    values(a, 2)
                if inside(b):
                    residual(0, b, 0)
                    residual(0, b, 1)
                if inside(e):
                    choose(e)
                if inside(c):
                    for t in range(TT):
                        residual(1, c, t)
                if inside(a):
                    queries(a, 2)
                    numerator(a, 2)
                if inside(b):
                    statistics(0, b, (0, 1))
                if inside(c):
                    statistics(1, c, (0, 1))
                if inside(b):
                    residual(0, b, 2)
                if inside(c):
                    statistics(1, c, (2,))
                if inside(b):
                    residual(0, b, 3)
                    statistics(0, b, (2, 3))
                    moments(0, b)
                if inside(c):
                    statistics(1, c, (3,))
                    moments(1, c)
                if inside(a):
                    keys(a, 3)
                    values(a, 3)
                if inside(i + 1):
                    split_x(i + 1)
                if inside(a):
                    queries(a, 3)
                    numerator(a, 3)

            staged(dve, step)

        @block.tensor
        def _(pe):

            def product(out, pairs, done):
                n = 0
                for (ah, al), (bh, bl) in pairs:
                    for lhsT, rhs in ((ah, bh), (ah, bl), (al, bh)):
                        last = pe.matmul(out, lhsT, rhs, start=(n == 0), stop=(n == 3 * len(pairs) - 1))
                        n += 1
                last.then_inc(done, 1)

            PARTS = {"k": (WK, K_BANK, k_mm, ek_done, 2), "v": (WV, V_BANK, v_mm, kv_done, 1), "q": (WQ, Q_BANK, q_mm, eq_done, 2)}

            def qkv(a, cc, which):
                part, ps, done, free, per = PARTS[which]
                if isinstance(a, int) and a == 0 and cc == 0:
                    pe.wait_ge(w_lo_done, part + 1)
                if cc == 0:
                    if (due := upto(a, 2, 2)) is not None:
                        pe.wait_ge(xhi_done, due)
                    if (due := upto(a, 2, 2)) is not None:
                        pe.wait_ge(xlo_done, due)
                if (due := upto(a, per * CC, per * cc)) is not None:
                    pe.wait_ge(free, due)
                es = slice(cc * P, cc * P + P)
                product(ps[:, :], [((w["hi"][:, part, j, es], w["lo"][:, part, j, es]), (xT_hi[:, j, :], xT_lo[:, j, :]))
                                   for j in range(CC)], done)

            def project(b, t):
                ts = slice(t * P, t * P + P)
                product(WIDE[t % 2][:, :], [((y_hi[:, j, ts], y_lo[:, j, ts]), (w["hi"][:, WPROJ, j, :], w["lo"][:, WPROJ, j, :]))
                                            for j in range(CC)], proj_mm)

            def step(i):
                a, b, c, e = i, i - 1, i - 2, i - 3
                if inside(a):
                    qkv(a, 0, "k")
                if inside(b):
                    if (due := upto(b, CC, CC)) is not None:
                        pe.wait_ge(qk_done, due)
                    if isinstance(b, int) and b == 0:
                        pe.wait_ge(made, MADE)
                        pe.wait_ge(consts_in, 16 * 3)
                        pe.wait_ge(w_lo_done, 4)
                        pe.wait_ge(masks_done, 2)
                    if (due := upto(b - 3, 1, 1)) is not None:
                        pe.wait_ge(logit_done, due)
                    if (due := upto(b - 2, 1, 1)) is not None:
                        pe.wait_ge(sx_done, due)
                    if (due := upto(b - 1, 1, 1)) is not None:
                        pe.wait_ge(den_max, due)
                    for s in range(TT):
                        for cc in range(CC):
                            last = pe.matmul(DEN_BANK[s * SEG:s * SEG + SEG, 0:P], head_sum[:, cc, :], qk[:, cc, s * P:s * P + P],
                                             start=(cc == 0), stop=(cc == CC - 1))
                    last.then_inc(den_mm, 1)
                if inside(a):
                    qkv(a, 0, "v")
                if inside(b):
                    if (due := upto(b, TT, TT)) is not None:
                        pe.wait_ge(rall_done, due)
                    if (due := upto(c, TT, TT)) is not None:
                        pe.wait_ge(res1_done, due)
                    if (due := upto(e, TT, TT)) is not None:
                        pe.wait_ge(res2_done, due)
                    for cc in range(2):
                        pe.matmul(WIDE[cc][:, :], head_all[:, cc, :], rden_all[:, :], start=True, stop=True).then_inc(rb_mm, 1)
                if inside(a):
                    qkv(a, 0, "q")
                if inside(b):
                    for cc in range(2, CC):
                        if (due := upto(b, CC, cc - 1)) is not None:
                            pe.wait_ge(y_done, due)
                        pe.matmul(WIDE[cc % 2][:, :], head_all[:, cc, :], rden_all[:, :], start=True, stop=True).then_inc(rb_mm, 1)
                    if (due := upto(b, 1, 1)) is not None:
                        pe.wait_ge(den_max, due)
                if inside(e):
                    if (due := upto(e, TT - 1, TT - 1)) is not None:
                        pe.wait_ge(x2sum_done, due)
                    for j in range(CC):
                        last = pe.matmul(mean_ps[:, j, :], x_sum[:, 1, j * P:j * P + P], ones[:, 0:SUM], start=True, stop=True)
                    last.then_inc(mean_mm, 1)
                if inside(c):
                    if (due := upto(c, TT - 1, TT - 1)) is not None:
                        pe.wait_ge(xsum_done, due)
                    for h in range(XH):
                        last = pe.matmul(sx_ps[:, h, :], x_sum[:, 0, h * P:h * P + P], ones[:, 0:SUM], start=True, stop=True)
                    last.then_inc(sx_mm, 1)
                if inside(a):
                    qkv(a, 1, "k")
                if inside(e):
                    if (due := upto(e, 1, 1)) is not None:
                        pe.wait_ge(mcol_done, due)
                    if (due := upto(c, 1, 1)) is not None:
                        pe.wait_ge(sx_done, due)
                    for j in range(CC):
                        last = pe.matmul(route_ps, m_col[:, j:j + 1], wr[:, j, :], start=(j == 0), stop=(j == CC - 1))
                    last.then_inc(route_mm, 1)
                if inside(a):
                    qkv(a, 1, "v")
                    qkv(a, 1, "q")
                    qkv(a, 2, "k")
                    qkv(a, 2, "v")
                if inside(b):
                    if (due := upto(b, CC, CC)) is not None:
                        pe.wait_ge(yhi_done, due)
                    if (due := upto(b, CC, CC)) is not None:
                        pe.wait_ge(ylo_done, due)
                    if (due := upto(b, CC, CC)) is not None:
                        pe.wait_ge(y_done, due)
                    project(b, 0)
                    project(b, 1)
                if inside(c):
                    if (due := upto(c, 1, 1)) is not None:
                        pe.wait_ge(asum_done, due)
                    for h in range(XH):
                        last = pe.transpose(G_BANK[:, h * P:h * P + P], a_v[:, 0, h, :], ident[:, :])
                    last.then_inc(aT_mm, 1)
                    if (due := upto(c, 1, 1)) is not None:
                        pe.wait_ge(diag2_done, due)
                    pe.matmul(c_ps, ones[:, :], diag[:, :, :], start=True, stop=True).then_inc(kb_mm, 1)
                if inside(a):
                    qkv(a, 2, "q")
                if inside(c):
                    if (due := upto(c, 1, 1)) is not None:
                        pe.wait_ge(aT_done, due)
                    if (due := upto(c, 16, 16)) is not None:
                        pe.wait_ge(ctxT_in, due)
                    for t in range(TT):
                        if t < 2:
                            if (due := upto(b, TT, t + 1)) is not None:
                                pe.wait_ge(res1_done, due)
                        else:
                            if (due := upto(c, TT, t - 1)) is not None:
                                pe.wait_ge(res2_done, due)
                        for h in range(XH):
                            last = pe.matmul(WIDE[t % 2][:, h * P:h * P + P], ctx_T[:, h, t * P:t * P + P], aT[:, h, :],
                                             start=True, stop=True)
                        last.then_inc(out_mm, 1)
                if inside(b):
                    for t in (2, 3):
                        if (due := upto(b, TT, t - 1)) is not None:
                            pe.wait_ge(res1_done, due)
                        if (due := upto(c, TT, t + 1)) is not None:
                            pe.wait_ge(res2_done, due)
                        project(b, t)
                if inside(a):
                    for which in "kvq":
                        qkv(a, 3, which)
                if inside(b):
                    if (due := upto(b, 1, 1)) is not None:
                        pe.wait_ge(diag_done, due)
                    if (due := upto(c, 1, 1)) is not None:
                        pe.wait_ge(kb_done, due)
                    pe.matmul(c_ps, ones[:, :], diag[:, :, :], start=True, stop=True).then_inc(c_mm, 1)
                if inside(b):
                    if (due := upto(b, TT, TT)) is not None:
                        pe.wait_ge(x1_done, due)
                    if (due := upto(b, 16, 16)) is not None:
                        pe.wait_ge(ctx_in, due)
                    if (due := upto(c, 1, 1)) is not None:
                        pe.wait_ge(aT_done, due)
                    for h in range(XH):
                        hs = slice(h * P, h * P + P)
                        for t in range(TT):
                            last = pe.matmul(g_ps[:, h, :], x1[:, t, hs], ctx_tok[:, t, hs], start=(t == 0), stop=(t == TT - 1))
                    last.then_inc(g_mm, 1)

            staged(pe, step)


def dyn(ap, b):
    return ap[b] if isinstance(b, int) else ap[bass.ds(b, 1)].rearrange("a p t n -> p (a t) n")


def experts(nc, d, idx, x2_dram, out):
    with ExitStack() as ctx:
        def sb(name, shape, dt=F32):
            return ctx.enter_context(nc.sbuf_tensor(name, shape, dt))

        def sem(name):
            return ctx.enter_context(nc.semaphore(name))

        NR = 4
        NW = 8
        AHEAD = 4
        LAG = 2
        raw = sb("raw", [P, NR, 2 * C])
        w_hi, w_lo = sb("we_hi", [P, NW, 2 * C], F32R), sb("we_lo", [P, NW, 2 * C], F32R)
        x_res = [sb(f"x_res{i}", [P, TT, C]) for i in range(2)]
        xT_hi = [sb(f"x2T_hi{i}", [P, CC, T], F32R) for i in range(2)]
        xT_lo = [sb(f"x2T_lo{i}", [P, CC, T], F32R) for i in range(2)]
        hid = sb("hid", [P, 2, T])
        h_hi, h_lo = sb("h_hi", [P, NR, T], F32R), sb("h_lo", [P, NR, T], F32R)
        b1 = sb("b1", [P, 2, FC])
        b2 = sb("b2", [P, 2, C])
        ident = sb("ident_e", [P, P])
        half, ln_eps, minus = (sb(n, [P, TT]) for n in ("half_e", "ln_eps_e", "minus_e"))
        stats, mv = sb("stats_e", [P, TT, 6]), sb("mv_e", [P, TT, 2])
        var_e, rstd, m_r, shift = (sb(n, [P, TT]) for n in ("var_f", "rstd_f", "m_r_f", "shift_f"))
        acc = [ctx.enter_context(nc.psum_tensor(f"acc{t}", [P, C], F32)) for t in range(TT)]
        h_ps = [ctx.enter_context(nc.psum_tensor(f"h_ps{i}", [P, T], F32)) for i in range(2)]
        t_ps = [ctx.enter_context(nc.psum_tensor(f"t_ps{i}", [P, T], F32)) for i in range(2)]

        made = sem("made_e")
        w_in = [sem(f"we_in{s}") for s in range(NR)]
        b_in = [sem("b_in0"), sem("b_in1")]
        x_in = [sem("x2_in0"), sem("x2_in1")]
        whi_done, wlo_done = sem("whi_done"), sem("wlo_done")
        up_mm, down_mm = sem("up_mm"), sem("down_mm")
        h_done, hhi_done, hlo_done = sem("h_done"), sem("hhi_done"), sem("hlo_done")
        tr_mm, xhi_done, xlo_done = sem("tr_mm"), sem("x2hi_done"), sem("x2lo_done")
        xb_done, acc_mm = sem("x2b_done"), sem("acc_mm")
        res_done, st_done, mv_done = sem("res_done"), sem("st_done"), sem("mv_done")
        ve_done, rstd_done, mr_done, shift_done = (sem(n) for n in ("ve_done", "rstd_done", "mr_done", "shift_done"))
        norm_done = sem("norm_done")
        stored = sem("stored")
        block = ctx.enter_context(nc.Block())
        TR_AT = (10, 11, 12, 13)

        def paired(eng, body):
            for b in range(2):
                body(b, b % 2)
            with eng.Fori(1, NB // 2 - 1) as pair:
                for parity in range(2):
                    body(pair * 2 + parity, parity)
            for b in range(NB - 2, NB):
                body(b, b % 2)

        def b_wait(eng, b, parity):
            eng.wait_ge(b_in[parity], (b - parity) * 16 + 32)

        def w_wait(eng, b, f):
            if isinstance(b, int) and f >= FC:
                b, f = b + 1, f - FC
            eng.wait_ge(w_in[f % NR], b * (16 * FC // NR) + 16 * (f // NR + 1))

        def after_last(b, f):
            return isinstance(b, int) and b * FC + f >= NB * FC

        @block.sync
        def _(sp):
            sp.dma_start(x_res[0][:, :, :], x2_dram[0]).then_inc(x_in[0], 16)

            def step(b, parity):
                e = sp.value_load(idx[0:1, bass.ds(b, 1)], min_val=0, max_val=NE - 1)
                if (due := upto(b - 2, FC, FC)) is not None:
                    sp.wait_ge(h_done, due)
                sp.dma_start(b1[:, parity, :], d["b1"][bass.ds(e, 1)].rearrange("a p f -> p (a f)")).then_inc(b_in[parity], 16)
                if (due := upto(b - 2, 1, 1)) is not None:
                    sp.wait_ge(xb_done, due)
                sp.dma_start(b2[:, parity, :], d["b2"][bass.ds(e, 1), :].broadcast_to([P, C])).then_inc(b_in[parity], 16)
                for f in range(FC):
                    if (due := upto(b, FC, f - NR + 1)) is not None:
                        sp.wait_ge(wlo_done, due)
                    sp.dma_start(raw[:, f % NR, :],
                                 d["w12"][bass.ds(e, 1), f].rearrange("a p n -> p (a n)")).then_inc(w_in[f % NR], 16)
                    if f == 9:
                        if inside(b - 1):
                            if (due := upto(b - 1, TT, TT)) is not None:
                                sp.wait_ge(norm_done, due)
                            sp.dma_start(dyn(out, b - 1), x_res[1 - parity][:, :, :]).then_inc(stored, 16)
                    if f == 10:
                        if inside(b + 1):
                            if (due := upto(b - 1, 16, 16)) is not None:
                                sp.wait_ge(stored, due)
                            sp.dma_start(x_res[1 - parity][:, :, :], dyn(x2_dram, b + 1)).then_inc(x_in[1 - parity], 16)

            paired(sp, step)
            sp.wait_ge(norm_done, NB * TT)
            sp.dma_start(out[NB - 1], x_res[1][:, :, :]).then_inc(stored, 16)
            sp.wait_ge(stored, 16 * NB)

        @block.gpsimd
        def _(pool):
            pool.memset(ident[:, :], 0.0).then_inc(made, 1)
            pool.memset(half[:, :], -0.5).then_inc(made, 1)
            pool.memset(ln_eps[:, :], EPS_LN).then_inc(made, 1)
            pool.memset(minus[:, :], -1.0).then_inc(made, 1)
            pool.wait_ge(made, 4)
            pool.affine_select(out=ident[:, :], in_=ident[:, :], compare_op=ALU.not_equal, fill=1.0, base=0,
                               pattern=[[-1, P]], channel_multiplier=1).then_inc(made, 1)

            def step(b, parity):
                if (due := upto(b, CC, CC)) is not None:
                    pool.wait_ge(tr_mm, due)
                b_wait(pool, b, parity)
                pool.tensor_tensor(x_res[parity][:, :, :], x_res[parity][:, :, :],
                                   b2[:, parity:parity + 1, :].broadcast_to([P, TT, C]), ALU.add).then_inc(xb_done, 1)
                if (due := upto(b, TT, TT)) is not None:
                    pool.wait_ge(mv_done, due)
                if (due := upto(b - 1, TT, TT)) is not None:
                    pool.wait_ge(norm_done, due)
                pool.tensor_tensor(var_e[:, :], mv[:, :, 1], ln_eps[:, :], ALU.add).then_inc(ve_done, 1)
                if (due := upto(b, 1, 1)) is not None:
                    pool.wait_ge(ve_done, due)
                pool.tensor_tensor(rstd[:, :], var_e[:, :], half[:, :], ALU.pow).then_inc(rstd_done, 1)
                if (due := upto(b, 1, 1)) is not None:
                    pool.wait_ge(rstd_done, due)
                pool.tensor_tensor(m_r[:, :], mv[:, :, 0], rstd[:, :], ALU.mult).then_inc(mr_done, 1)
                if (due := upto(b, 1, 1)) is not None:
                    pool.wait_ge(mr_done, due)
                pool.tensor_tensor(shift[:, :], m_r[:, :], minus[:, :], ALU.mult).then_inc(shift_done, 1)

            paired(pool, step)

        @block.scalar
        def _(act):
            def split_w(b, f):
                if after_last(b, f):
                    return
                w_wait(act, b, f)
                if (due := upto(b, FC, f - NW + 1)) is not None:
                    act.wait_ge(down_mm, due)
                act.activation(w_hi[:, f % NW, :], raw[:, f % NR, :], ACT.Copy).then_inc(whi_done, 1)

            def split_x(b, parity, j):
                if (due := upto(b, CC, j + 1)) is not None:
                    act.wait_ge(tr_mm, due)
                if (due := upto(b - 2, FC, FC)) is not None:
                    act.wait_ge(up_mm, due)
                act.activation(xT_hi[parity][:, j, :], t_ps[j % 2][:, :], ACT.Copy).then_inc(xhi_done, 1)

            for j in range(CC):
                split_x(0, 0, j)
            for f in range(AHEAD):
                split_w(0, f)

            def step(b, parity):
                for f in range(FC):
                    if (due := upto(b, FC, f + 1)) is not None:
                        act.wait_ge(up_mm, due)
                    if f == 0:
                        b_wait(act, b, parity)
                    if (due := upto(b, FC, f - 1)) is not None:
                        act.wait_ge(hlo_done, due)
                    act.activation(hid[:, f % 2, :], h_ps[f % 2][:, :], ACT.Relu, bias=b1[:, parity, f:f + 1]).then_inc(h_done, 1)
                    split_w(b, f + AHEAD)
                    if f in TR_AT and inside(b + 1):
                        split_x(b + 1, 1 - parity, TR_AT.index(f))
                    if f == 5:
                        finish(b - 1, 1 - parity)

            def finish(b, parity):
                if not inside(b):
                    return
                if (due := upto(b, 1, 1)) is not None:
                    act.wait_ge(shift_done, due)
                for t in range(TT):
                    act.activation(x_res[parity][:, t, :], x_res[parity][:, t, :], ACT.Identity,
                                   bias=shift[:, t:t + 1], scale=rstd[:, t:t + 1]).then_inc(norm_done, 1)

            paired(act, step)
            finish(NB - 1, 1)

        @block.vector
        def _(dve):
            def split_w(b, f):
                if after_last(b, f):
                    return
                if (due := upto(b, FC, f + 1)) is not None:
                    dve.wait_ge(whi_done, due)
                if (due := upto(b, FC, f - NW + 1)) is not None:
                    dve.wait_ge(down_mm, due)
                dve.tensor_tensor(w_lo[:, f % NW, :], raw[:, f % NR, :], w_hi[:, f % NW, :].bitcast(F32), ALU.subtract).then_inc(wlo_done, 1)

            def split_x(b, parity, j):
                if (due := upto(b, CC, j + 1)) is not None:
                    dve.wait_ge(xhi_done, due)
                if (due := upto(b - 2, FC, FC)) is not None:
                    dve.wait_ge(up_mm, due)
                dve.tensor_tensor(xT_lo[parity][:, j, :], t_ps[j % 2][:, :], xT_hi[parity][:, j, :].bitcast(F32),
                                  ALU.subtract).then_inc(xlo_done, 1)

            for j in range(CC):
                split_x(0, 0, j)
            for f in range(AHEAD):
                split_w(0, f)

            def step(b, parity):
                for f in range(FC):
                    if (due := upto(b, FC, f + 1)) is not None:
                        dve.wait_ge(h_done, due)
                    if (due := upto(b, FC, f - NR + 1)) is not None:
                        dve.wait_ge(down_mm, due)
                    s = f % NR
                    dve.tensor_copy(h_hi[:, s, :], hid[:, f % 2, :]).then_inc(hhi_done, 1)
                    if (due := upto(b, FC, f + 1)) is not None:
                        dve.wait_ge(hhi_done, due)
                    dve.tensor_tensor(h_lo[:, s, :], hid[:, f % 2, :], h_hi[:, s, :].bitcast(F32), ALU.subtract).then_inc(hlo_done, 1)
                    if f in (2, 3):
                        statistics(b - 1, 1 - parity, (0, 1) if f == 2 else (2, 3))
                    split_w(b, f + AHEAD)
                    if f in TR_AT and inside(b + 1):
                        split_x(b + 1, 1 - parity, TR_AT.index(f))
                for t in range(TT):
                    if t < TT - 1:
                        if (due := upto(b, TT - 1, t + 1)) is not None:
                            dve.wait_ge(acc_mm, due)
                    else:
                        if (due := upto(b, FC, FC)) is not None:
                            dve.wait_ge(down_mm, due)
                    if (due := upto(b, 1, 1)) is not None:
                        dve.wait_ge(xb_done, due)
                    x = x_res[parity][:, t, :]
                    dve.tensor_tensor(x, acc[t][:, :], x, ALU.add).then_inc(res_done, 1)

            def statistics(b, parity, tiles):
                if not inside(b):
                    return
                for t in tiles:
                    if (due := upto(b, TT, t + 1)) is not None:
                        dve.wait_ge(res_done, due)
                    if (due := upto(b - 1, TT, TT)) is not None:
                        dve.wait_ge(mv_done, due)
                    dve.bn_stats(stats[:, t, :], x_res[parity][:, t, :]).then_inc(st_done, 1)
                if TT - 1 not in tiles:
                    return
                for t in range(TT):
                    dve.wait_ge(made, 5)
                    if (due := upto(b, TT, t + 1)) is not None:
                        dve.wait_ge(st_done, due)
                    if t == 0:
                        if (due := upto(b - 1, 1, 1)) is not None:
                            dve.wait_ge(shift_done, due)
                    dve.bn_aggr(mv[:, t, :], stats[:, t, :]).then_inc(mv_done, 1)

            paired(dve, step)
            statistics(NB - 1, 1, range(TT))

        @block.tensor
        def _(pe):
            pe.wait_ge(made, 5)

            def transpose_x(b, parity, j):
                pe.wait_ge(x_in[parity], (b - parity) * 8 + 16)
                if (due := upto(b, CC, j - 1)) is not None:
                    pe.wait_ge(xlo_done, due)
                for t in range(TT):
                    last = pe.transpose(t_ps[j % 2][:, t * P:t * P + P], x_res[parity][:, t, j * P:j * P + P], ident[:, :])
                last.then_inc(tr_mm, 1)

            for j in range(CC):
                transpose_x(0, 0, j)

            def up(b, parity, f):
                if f == 0:
                    if (due := upto(b, CC, CC)) is not None:
                        pe.wait_ge(xlo_done, due)
                if (due := upto(b, FC, f + 1)) is not None:
                    pe.wait_ge(whi_done, due)
                if (due := upto(b, FC, f + 1)) is not None:
                    pe.wait_ge(wlo_done, due)
                if (due := upto(b, FC, f - 1)) is not None:
                    pe.wait_ge(h_done, due)
                s, n = f % NW, 0
                for j in range(CC):
                    js = slice(j * P, j * P + P)
                    for wx, xx in ((w_hi, xT_hi), (w_hi, xT_lo), (w_lo, xT_hi)):
                        last = pe.matmul(h_ps[f % 2][:, :], wx[:, s, js], xx[parity][:, j, :], start=(n == 0), stop=(n == 3 * CC - 1))
                        n += 1
                last.then_inc(up_mm, 1)

            def down(b, f):
                if (due := upto(b, FC, f + 1)) is not None:
                    pe.wait_ge(hhi_done, due)
                if (due := upto(b, FC, f + 1)) is not None:
                    pe.wait_ge(hlo_done, due)
                s, sw = f % NR, f % NW
                for t in range(TT):
                    ts = slice(t * P, t * P + P)
                    if f == 0:
                        if (due := upto(b - 1, TT, t + 1)) is not None:
                            pe.wait_ge(res_done, due)
                    for n, (hx, wx) in enumerate(((h_hi, w_hi), (h_hi, w_lo), (h_lo, w_hi))):
                        last = pe.matmul(acc[t][:, :], hx[:, s, ts], wx[:, sw, C:], start=(f == 0 and n == 0),
                                         stop=(f == FC - 1 and n == 2))
                    if f == FC - 1 and t < TT - 1:
                        last.then_inc(acc_mm, 1)
                last.then_inc(down_mm, 1)

            def step(b, parity):
                for f in range(FC):
                    up(b, parity, f)
                    if f >= LAG:
                        down(b, f - LAG)
                    if f in TR_AT and inside(b + 1):
                        transpose_x(b + 1, 1 - parity, TR_AT.index(f))
                for f in range(FC - LAG, FC):
                    down(b, f)

            paired(pe, step)


def build(nc, d, out):
    x2_dram = nc.dram_tensor("x2_scratch", [NB, P, TT, C], F32, kind="Internal").ap()
    with ExitStack() as ctx:
        idx = ctx.enter_context(nc.sbuf_tensor("idx", [1, NB], U32))
        x2_stored = ctx.enter_context(nc.semaphore("x2_stored"))
        mixers(nc, d, idx, x2_dram, x2_stored)
        experts(nc, d, idx, x2_dram, out)


def kernel(**inputs):
    import numpy as np
    import concourse.bacc as bacc
    from concourse.bass_utils import run_bass_kernel_spmd

    g = {k: np.asarray(v) for k, v in inputs.items()}

    def tokens(x):
        return x.reshape(NB, TT, P, C).transpose(0, 2, 1, 3)

    def channels(x):
        return x.transpose(0, 2, 1).reshape(NB, CC, P, T).transpose(0, 2, 1, 3)

    def column(v):
        return v.reshape(-1, P).T

    def weights(w):
        return w.T.reshape(CC, P, -1).transpose(1, 0, 2)

    x_names = {n: g[f"L0_xattn_{n}"] for n in
               ("wqg", "bqg", "wkg", "bkg", "wvg", "bvg", "wql", "bql", "wkl", "bkl", "wvl", "bvl", "wp", "bp")}
    wq, wk, wv = np.split(g["L0_attn_Wqkv"], 3, axis=0)
    w1 = g["L0_ffn_W1"].reshape(NE, CC, P, FC, P).transpose(0, 3, 2, 1, 4).reshape(NE, FC, P, C)
    w2 = g["L0_ffn_W2"].reshape(NE, FC, P, C)
    laid = {
        "xT": channels(g["x"]),
        "x_tok": tokens(g["x"]),
        "ctx_tok": tokens(g["ctx_1024"]),
        "ctxT": channels(g["ctx_1024"]),
        "w_attn": np.stack([weights(wk), weights(wv), weights(wq), weights(g["L0_attn_Wproj"])]),
        "b_qkv": column(g["L0_attn_bqkv"]),
        "scale": g["L0_attn_scale"].reshape(1, 1),
        "rows": np.stack([x_names[n] for n in ("wkg", "bkg", "wkl", "bkl", "wvg", "bvg", "wvl", "bvl")]
                         + [g["L0_attn_bproj"]])[None],
        "cols": np.stack([column(x_names[n]) for n in ("wqg", "bqg", "wql", "bql", "wp", "bp")], axis=1),
        "wr": g["L0_ffn_Wr"].reshape(CC, P, NE).transpose(1, 0, 2),
        "br": g["L0_ffn_br"].reshape(1, NE),
        "w12": np.concatenate([w1, w2], axis=3),
        "b1": g["L0_ffn_b1"].reshape(NE, FC, P).transpose(0, 2, 1),
        "b2": g["L0_ffn_b2"],
    }
    nc = bacc.Bacc("TRN2", target_bir_lowering=False, num_devices=1, dynamic_dma_scratch_size=2048)
    arrays, d = {}, {}
    for name, a in laid.items():
        a = np.ascontiguousarray(a)
        arrays[f"in_{name}"] = a
        d[name] = nc.dram_tensor(f"in_{name}", a.shape, mybir.dt.from_np(a.dtype), kind="ExternalInput").ap()
    out = nc.dram_tensor("out_dram", (NB, P, TT, C), F32, kind="ExternalOutput").ap()
    build(nc, d, out)
    r = run_bass_kernel_spmd(nc, [arrays], core_ids=[0])
    got = r.results[0]["out_dram"]
    return got.transpose(0, 2, 1, 3).reshape(NB, T, C)
```
